# Optimizing a Trainium2 kernel written in Bass

```python
import numpy as np
import jax
import jax.numpy as jnp

def _softmax(x, axis=-1):
    return jax.nn.softmax(x, axis=axis)

def _gelu(x):
    return jax.nn.gelu(x, approximate=True)

def _silu(x):
    return jax.nn.silu(x)

def _sigmoid(x):
    return jax.nn.sigmoid(x)

def _layernorm(x, axis=-1, eps=1e-05):
    m = jnp.mean(x, axis=axis, keepdims=True)
    v = jnp.var(x, axis=axis, keepdims=True)
    return (x - m) / jnp.sqrt(v + eps)

def _scatter_add(tgt, idx, src, axis=0):
    return tgt.at[idx].add(src)

def _segment_sum(src, seg, n):
    return jax.ops.segment_sum(src, seg, n)
kernel_name = 'mk_conv_attn_hybrid_d2_conv_nchw384_r4_2e5aeb'

def setup_inputs(seed: int=0):
    np.random.seed(seed)
    _w = jnp.asarray

    def _rec_inputs():
        import jax
        import jax.numpy as jnp
        _gk = jax.random.key(seed)
        x = -0.0004039 + 1 * jax.random.normal(jax.random.fold_in(_gk, 1), (32, 96, 32, 32), jnp.float32)
        return x
    x = _rec_inputs()

    def _L0_conv_setup():
        import math
        import jax, jax.numpy as jnp
        import numpy as np
        C = 96
        NH = 8
        HD = C // NH
        HIDDEN = int(C * 4.0)
        EPS = 1e-05
        key = jax.random.key(seed)
        ks = jax.random.split(key, 8)
        s = 0.02
        return {'x': jax.random.normal(ks[0], (32, C, 32, 32), dtype=jnp.float32), 'qkv_w': jax.random.normal(ks[1], (C, 3 * C), dtype=jnp.float32) * s, 'proj_w': jax.random.normal(ks[2], (C, C), dtype=jnp.float32) * s, 'proj_b': jnp.zeros((C,), dtype=jnp.float32), 'ln_g': jnp.ones((C,), dtype=jnp.float32), 'ln_b': jnp.zeros((C,), dtype=jnp.float32), 'fc1_w': jax.random.normal(ks[3], (C, HIDDEN), dtype=jnp.float32) * s, 'fc1_b': jnp.zeros((HIDDEN,), dtype=jnp.float32), 'fc2_w': jax.random.normal(ks[4], (HIDDEN, C), dtype=jnp.float32) * s, 'fc2_b': jnp.zeros((C,), dtype=jnp.float32)}
    _L0_conv_all = _L0_conv_setup()
    _L0_conv_in = {k: v for k, v in _L0_conv_all.items() if k in ('qkv_w', 'proj_w', 'proj_b', 'ln_g', 'ln_b', 'fc1_w', 'fc1_b', 'fc2_w', 'fc2_b')}
    del _L0_conv_all

    def _L1_attn_setup():
        import jax, jax.numpy as jnp
        import numpy as np
        N_HEADS = 6
        key = jax.random.key(seed)
        ks = jax.random.split(key, 5)
        B, T, C = (32, 64, 96)
        s = 0.02
        return {'x': jax.random.normal(ks[0], (B, T, C), jnp.float32), 'Wk': jax.random.normal(ks[1], (C, C), jnp.float32) * s, 'Wq': jax.random.normal(ks[2], (C, C), jnp.float32) * s, 'Wv': jax.random.normal(ks[3], (C, C), jnp.float32) * s, 'Wp': jax.random.normal(ks[4], (C, C), jnp.float32) * s, 'bp': jnp.zeros((C,), jnp.float32)}
    _L1_attn_all = _L1_attn_setup()
    _L1_attn_in = {k: v for k, v in _L1_attn_all.items() if k in ('Wk', 'Wq', 'Wv', 'Wp', 'bp')}
    del _L1_attn_all

    def _L1_ffn_setup():
        import jax, jax.numpy as jnp
        import numpy as np
        NUM_GROUPS = 5
        EPS = 1e-05
        QB = 128.0

        def _binarize_weights_groupwise(W):
            n_out = W.shape[0]
            gs = n_out // NUM_GROUPS
            Wb = jnp.zeros_like(W)
            for g in range(NUM_GROUPS):
                wg = W[g * gs:(g + 1) * gs]
                z = wg - wg.mean()
                ste = z + jax.lax.stop_gradient(jnp.sign(z) - z)
                Wb = Wb.at[g * gs:(g + 1) * gs].set(ste)
            return Wb

        def _quantize_activations_groupwise(x):
            n = x.shape[0]
            gs = n // NUM_GROUPS
            xq = jnp.zeros_like(x)
            for g in range(NUM_GROUPS):
                ag = x[g * gs:(g + 1) * gs]
                gamma = jnp.max(jnp.abs(ag))
                xq = xq.at[g * gs:(g + 1) * gs].set(jnp.clip(ag * QB / (gamma + EPS), -QB + EPS, QB - EPS))
            return xq

        def _bitlinear(x, W, b):
            Wb = _binarize_weights_groupwise(W)
            y = jnp.einsum('btc,oc->bto', x, Wb) + b
            return _quantize_activations_groupwise(y)
        key = jax.random.key(seed)
        k1, k2, k3, k4, k5 = jax.random.split(key, 5)
        B, T, C = (10, 512, 96)
        H = 4 * C
        lim1 = 1.0 / np.sqrt(C)
        lim2 = 1.0 / np.sqrt(H)
        x = jax.random.normal(k1, (B, T, C), dtype=jnp.float32)
        W1 = jax.random.uniform(k2, (H, C), minval=-lim1, maxval=lim1, dtype=jnp.float32)
        b1 = jax.random.uniform(k3, (H,), minval=-lim1, maxval=lim1, dtype=jnp.float32)
        W2 = jax.random.uniform(k4, (C, H), minval=-lim2, maxval=lim2, dtype=jnp.float32)
        b2 = jax.random.uniform(k5, (C,), minval=-lim2, maxval=lim2, dtype=jnp.float32)
        return {'x': x, 'W1': W1, 'b1': b1, 'W2': W2, 'b2': b2}
    _L1_ffn_all = _L1_ffn_setup()
    _L1_ffn_in = {k: v for k, v in _L1_ffn_all.items() if k in ('W1', 'b1', 'W2', 'b2')}
    del _L1_ffn_all
    return {'x': x, 'L0_conv_qkv_w': _L0_conv_in['qkv_w'], 'L0_conv_proj_w': _L0_conv_in['proj_w'], 'L0_conv_proj_b': _L0_conv_in['proj_b'], 'L0_conv_ln_g': _L0_conv_in['ln_g'], 'L0_conv_ln_b': _L0_conv_in['ln_b'], 'L0_conv_fc1_w': _L0_conv_in['fc1_w'], 'L0_conv_fc1_b': _L0_conv_in['fc1_b'], 'L0_conv_fc2_w': _L0_conv_in['fc2_w'], 'L0_conv_fc2_b': _L0_conv_in['fc2_b'], 'L1_attn_Wk': _L1_attn_in['Wk'], 'L1_attn_Wq': _L1_attn_in['Wq'], 'L1_attn_Wv': _L1_attn_in['Wv'], 'L1_attn_Wp': _L1_attn_in['Wp'], 'L1_attn_bp': _L1_attn_in['bp'], 'L1_ffn_W1': _L1_ffn_in['W1'], 'L1_ffn_b1': _L1_ffn_in['b1'], 'L1_ffn_W2': _L1_ffn_in['W2'], 'L1_ffn_b2': _L1_ffn_in['b2']}

def reference(x, L0_conv_qkv_w, L0_conv_proj_w, L0_conv_proj_b, L0_conv_ln_g, L0_conv_ln_b, L0_conv_fc1_w, L0_conv_fc1_b, L0_conv_fc2_w, L0_conv_fc2_b, L1_attn_Wk, L1_attn_Wq, L1_attn_Wv, L1_attn_Wp, L1_attn_bp, L1_ffn_W1, L1_ffn_b1, L1_ffn_W2, L1_ffn_b2):
    import jax
    import jax.numpy as jnp

    def _L0_conv_ref(x, qkv_w, proj_w, proj_b, ln_g, ln_b, fc1_w, fc1_b, fc2_w, fc2_b):
        import math
        import jax, jax.numpy as jnp
        import numpy as np
        C = 96
        NH = 8
        HD = C // NH
        HIDDEN = int(C * 4.0)
        EPS = 1e-05
        B, Cc, H, W = x.shape
        L = H * W
        xs = jnp.transpose(x, (0, 2, 3, 1)).reshape(B, L, Cc)
        mu = jnp.mean(xs, axis=-1, keepdims=True)
        var = jnp.mean((xs - mu) ** 2, axis=-1, keepdims=True)
        xn = (xs - mu) / jnp.sqrt(var + EPS) * ln_g + ln_b
        mid = jax.nn.silu(xn @ fc1_w + fc1_b) @ fc2_w + fc2_b
        mid = mid.reshape(B, L, NH, HD).transpose(0, 2, 1, 3)
        qkv = (xs @ qkv_w).reshape(B, L, 3, NH, HD).transpose(2, 0, 3, 1, 4)
        q, k, v = (qkv[0], qkv[1], qkv[2])
        q = q / jnp.linalg.norm(q, axis=-1, keepdims=True)
        k = k / jnp.linalg.norm(k, axis=-1, keepdims=True)
        attn = jnp.einsum('bhld,bhle->bhde', k, v)
        o = 0.5 * v + 1.0 / math.pi * jnp.einsum('bhld,bhde->bhle', q, attn)
        o = o / jnp.linalg.norm(o, axis=-1, keepdims=True)
        o = o + mid
        o = o.transpose(0, 2, 1, 3).reshape(B, L, Cc)
        o = o @ proj_w + proj_b
        return jnp.transpose(o, (0, 2, 1)).reshape(B, Cc, H, W)

    def _L1_attn_ref(x, Wk, Wq, Wv, Wp, bp):
        import jax, jax.numpy as jnp
        import numpy as np
        N_HEADS = 6
        B, T, C = x.shape
        H = N_HEADS
        hs = C // H
        k = (x @ Wk).reshape(B, H, T, hs)
        q = (x @ Wq).reshape(B, H, T, hs)
        v = (x @ Wv).reshape(B, H, T, hs)
        scale = C ** (-0.5)
        wei = jnp.einsum('bhtd,bhsd->bhts', q, k) * scale
        mask = jnp.tril(jnp.ones((T, T), dtype=bool))
        wei = jnp.where(mask, wei, -jnp.inf)
        wei = jax.nn.softmax(wei, axis=-1)
        out = jnp.einsum('bhts,bhsd->bhtd', wei, v).reshape(B, T, C)
        return out @ Wp + bp

    def _L1_ffn_ref(x, W1, b1, W2, b2):
        import jax, jax.numpy as jnp
        import numpy as np
        NUM_GROUPS = 5
        EPS = 1e-05
        QB = 128.0

        def _binarize_weights_groupwise(W):
            n_out = W.shape[0]
            gs = n_out // NUM_GROUPS
            Wb = jnp.zeros_like(W)
            for g in range(NUM_GROUPS):
                wg = W[g * gs:(g + 1) * gs]
                z = wg - wg.mean()
                ste = z + jax.lax.stop_gradient(jnp.sign(z) - z)
                Wb = Wb.at[g * gs:(g + 1) * gs].set(ste)
            return Wb

        def _quantize_activations_groupwise(x):
            n = x.shape[0]
            gs = n // NUM_GROUPS
            xq = jnp.zeros_like(x)
            for g in range(NUM_GROUPS):
                ag = x[g * gs:(g + 1) * gs]
                gamma = jnp.max(jnp.abs(ag))
                xq = xq.at[g * gs:(g + 1) * gs].set(jnp.clip(ag * QB / (gamma + EPS), -QB + EPS, QB - EPS))
            return xq

        def _bitlinear(x, W, b):
            Wb = _binarize_weights_groupwise(W)
            y = jnp.einsum('btc,oc->bto', x, Wb) + b
            return _quantize_activations_groupwise(y)
        h = _bitlinear(x, W1, b1)
        h = jax.nn.gelu(h, approximate=False)
        out = _bitlinear(h, W2, b2)
        return out

    def _gn(v, G=32, eps=1e-05):
        B_, C_, H_, W_ = v.shape
        g = v.reshape(B_, G, C_ // G, H_, W_)
        m = jnp.mean(g, axis=(2, 3, 4), keepdims=True)
        s = jnp.var(g, axis=(2, 3, 4), keepdims=True)
        return ((g - m) / jnp.sqrt(s + eps)).reshape(v.shape)

    def _ln_c(v, eps=1e-06):
        m = jnp.mean(v, axis=1, keepdims=True)
        s = jnp.var(v, axis=1, keepdims=True)
        return (v - m) / jnp.sqrt(s + eps)

    def _ln_t(v, eps=1e-05):
        m = jnp.mean(v, axis=-1, keepdims=True)
        s = jnp.var(v, axis=-1, keepdims=True)
        return (v - m) / jnp.sqrt(s + eps)

    def _to_tokens(v):
        B_, C_, H_, W_ = v.shape
        return v.reshape(B_, C_, H_ * W_).transpose(0, 2, 1)

    def _from_tokens(t, like):
        B_, C_, H_, W_ = like.shape
        return t.transpose(0, 2, 1).reshape(B_, C_, H_, W_)
    x = x + _L0_conv_ref(_gn(x), L0_conv_qkv_w, L0_conv_proj_w, L0_conv_proj_b, L0_conv_ln_g, L0_conv_ln_b, L0_conv_fc1_w, L0_conv_fc1_b, L0_conv_fc2_w, L0_conv_fc2_b)
    t = _to_tokens(x)
    t = t + _L1_attn_ref(_ln_t(t), L1_attn_Wk, L1_attn_Wq, L1_attn_Wv, L1_attn_Wp, L1_attn_bp)
    t = t + _L1_ffn_ref(_ln_t(t), L1_ffn_W1, L1_ffn_b1, L1_ffn_W2, L1_ffn_b2)
    x = _from_tokens(t, x)
    return x

_drawn_inputs = setup_inputs


def setup_inputs(seed=0):
    import zlib

    import numpy as np

    out = dict(_drawn_inputs(seed))
    spreads = {'L0_conv_proj_b': (0.0, 0.1),
     'L0_conv_ln_g': (1.0, 0.6),
     'L0_conv_ln_b': (0.0, 0.8),
     'L0_conv_fc1_b': (0.0, 0.8),
     'L0_conv_fc2_b': (0.0, 0.395),
     'L1_attn_bp': (0.0, 0.1)}
    factors = {'L0_conv_fc1_w': 6.614,
     'L0_conv_fc2_w': 5.674,
     'L1_attn_Wk': 8.0,
     'L1_attn_Wq': 8.0,
     'L1_attn_Wv': 8.0,
     'L1_attn_Wp': 8.0,
     'L1_ffn_b1': 8.0,
     'L1_ffn_b2': 8.0}
    for name, (base, spread) in spreads.items():
        noise = np.random.default_rng([zlib.crc32(name.encode()), seed]).standard_normal(out[name].shape)
        drawn = base * np.exp(spread * noise) if base else spread * noise
        out[name] = jnp.asarray(drawn.astype(out[name].dtype))
    for name, factor in factors.items():
        out[name] = (out[name] * factor).astype(out[name].dtype)
    return out
```

```python
import concourse.bass as bass
from concourse import mybir
from contextlib import ExitStack
import math

FP32 = mybir.dt.float32
BF16 = mybir.dt.bfloat16
U32 = mybir.dt.uint32
ALU = mybir.AluOpType
ACT = mybir.ActivationFunctionType
AX = mybir.AxisListType

BATCH, C, SIDE = 32, 96, 32
L = SIDE * SIDE
P = 128
TILES = L // P
BANK = 512
HIDDEN = 4 * C
CHUNKS = HIDDEN // P
GN_CH = C // 32
LIN_HEADS, LIN_DIM = 8, C // 8
HEADS, HD = 6, C // 6
ROWS = L * C // HD
NHEADS = BATCH * HEADS
PARTS = 2 * 3 * HD
PACK = PARTS // 2 + HD
STACK = 6 * HD
GROUPS = 5
GB = BATCH // GROUPS
QB, QEPS = 128.0, 1e-5
NEG = -1.0e30


def _bcast(ap, axis, n):
    ap = ap.unsqueeze(axis)
    shape = list(ap.shape)
    shape[axis] = n
    return ap.broadcast_to(shape)


def _above(sem_wait, sem, value):
    if not isinstance(value, int) or value > 0:
        sem_wait(sem, value)


def _constants(nc, ctx):
    def sb(name, shape, dt=FP32):
        return ctx.enter_context(nc.sbuf_tensor(name, shape, dt))
    w = {}
    w["ident"] = sb("ident", [P, P])
    w["ident_bf"] = sb("ident_bf", [P, P], BF16)
    w["mask_keys"] = sb("mask_keys", [P, P], BF16)
    w["mask_queries"] = sb("mask_queries", [P, P], BF16)
    w["centre"] = sb("centre", [C, C])
    w["group_mean"] = sb("group_mean", [C, C])
    w["head_blocks"] = sb("head_blocks", [C, C])
    w["w_lin"] = sb("w_lin", [C, 4 * C])
    w["wq_t"] = sb("wq_t", [C, C])
    w["fc1"] = sb("fc1", [C, HIDDEN])
    w["fc1_bias"] = sb("fc1_bias", [P, CHUNKS])
    w["fc2"] = sb("fc2", [P, CHUNKS, C])
    w["proj"] = sb("proj", [C, C])
    w["out_bias"] = sb("out_bias", [C, 1])
    w["w_attn"] = sb("w_attn", [C, 4 * C])
    w["wp"] = sb("wp", [C, C])
    w["bp"] = sb("bp", [C, 1])
    w["w1"] = sb("w1", [C + 1, HIDDEN])
    w["w2"] = sb("w2", [P, CHUNKS, C])
    w["b2"] = sb("b2", [C, 1])
    w["eps"] = sb("eps", [P, 1])
    return w


def prepare(nc, w, A):
    ctx = ExitStack()
    with ctx:
        def sb(name, shape, dt=FP32):
            return ctx.enter_context(nc.sbuf_tensor(name, shape, dt))

        def sem(name):
            return ctx.enter_context(nc.semaphore(name))
        g_fc1 = sb("g_fc1", [C, HIDDEN])
        fc1_raw = sb("fc1_raw", [C, HIDDEN])
        fc2_raw = sb("fc2_raw", [P, CHUNKS, C])
        fc2_t = sb("fc2_t", [C, HIDDEN])
        attn_raw = sb("attn_raw", [C, 4 * C])
        qkv3 = sb("qkv3", [C, 3, C])
        w1_raw = sb("w1_raw", [P, CHUNKS, C])
        w1_t = sb("w1_t", [C, HIDDEN])
        w2_raw = sb("w2_raw", [C, HIDDEN])
        w2_t = sb("w2_t", [P, CHUNKS, C])
        lng = sb("lng", [C, 1])
        lnb = sb("lnb", [C, 1])
        fc1b = sb("fc1b", [P, CHUNKS])
        fc2b = sb("fc2b", [C, 1])
        projb = sb("projb", [C, 1])
        ones1 = sb("ones1", [C, P])
        ones2 = sb("ones2", [P, P])
        s1 = sb("s1", [C, GROUPS])
        s2 = sb("s2", [P, CHUNKS, GROUPS])
        sp2 = sb("sp2", [P, GROUPS])
        m1 = sb("m1", [C, GROUPS])
        m2 = sb("m2", [P, GROUPS])
        z1 = sb("z1", [C, HIDDEN])
        z2 = sb("z2", [P, CHUNKS, C])
        n1 = sb("n1", [C, HIDDEN])
        n2 = sb("n2", [P, CHUNKS, C])
        bank = [ctx.enter_context(nc.psum_tensor(f"prep{i}", [P, BANK], FP32)) for i in range(8)]
        loaded, made = sem("prep_loaded"), sem("prep_made")
        products, step = sem("prep_products"), sem("prep_step")
        gs1, gs2 = HIDDEN // GROUPS, C // GROUPS
        loads = [
            (w["w_lin"][:, 0:3 * C], A["L0_conv_qkv_w"]),
            (w["proj"][:, :], A["L0_conv_proj_w"]),
            (fc1_raw[:, :], A["L0_conv_fc1_w"]),
            (fc2_raw[:, :, :], A["L0_conv_fc2_w"].rearrange("(k p) c -> p k c", p=P)),
            (qkv3[:, 0, :], A["L1_attn_Wq"]),
            (qkv3[:, 1, :], A["L1_attn_Wk"]),
            (qkv3[:, 2, :], A["L1_attn_Wv"]),
            (w["wp"][:, :], A["L1_attn_Wp"]),
            (w1_raw[:, :, :], A["L1_ffn_W1"].rearrange("(k p) c -> p k c", p=P)),
            (w2_raw[:, :], A["L1_ffn_W2"]),
            (w["w1"][C:C + 1, :], A["L1_ffn_b1"].rearrange("(a n) -> a n", a=1)),
            (lng[:, :], A["L0_conv_ln_g"].rearrange("(n a) -> n a", a=1)),
            (lnb[:, :], A["L0_conv_ln_b"].rearrange("(n a) -> n a", a=1)),
            (fc1b[:, :], A["L0_conv_fc1_b"].rearrange("(k p) -> p k", p=P)),
            (fc2b[:, :], A["L0_conv_fc2_b"].rearrange("(n a) -> n a", a=1)),
            (projb[:, :], A["L0_conv_proj_b"].rearrange("(n a) -> n a", a=1)),
            (w["bp"][:, :], A["L1_attn_bp"].rearrange("(n a) -> n a", a=1)),
            (w["b2"][:, :], A["L1_ffn_b2"].rearrange("(n a) -> n a", a=1)),
        ]
        NLOADS = len(loads)
        MADE = 16
        with nc.Block() as block:
            @block.sync
            def _(sp):
                with nc.allow_non_contiguous_dma(reason="bias columns, once"):
                    for dst, src in loads:
                        sp.dma_start(dst, src).then_inc(loaded, 16)
                sp.wait_ge(loaded, 16 * NLOADS)

            @block.gpsimd
            def _(pool):
                def link(ins, n):
                    ins.then_inc(made, 1)
                    pool.wait_ge(made, n)
                link(pool.memset(w["ident"][:, :], 0.0), 1)
                link(pool.affine_select(out=w["ident"][:, :], in_=w["ident"][:, :], compare_op=ALU.not_equal,
                                        fill=1.0, base=0, pattern=[[-1, P]], channel_multiplier=1), 2)
                link(pool.memset(w["ident_bf"][:, :], 0.0), 3)
                link(pool.affine_select(out=w["ident_bf"][:, :], in_=w["ident_bf"][:, :], compare_op=ALU.not_equal,
                                        fill=1.0, base=0, pattern=[[-1, P]], channel_multiplier=1), 4)
                link(pool.memset(w["mask_keys"][:, :], 0.0), 5)
                link(pool.affine_select(out=w["mask_keys"][:, :], in_=w["mask_keys"][:, :], compare_op=ALU.is_ge,
                                        fill=NEG, base=0, pattern=[[1, P]], channel_multiplier=-1), 6)
                link(pool.memset(w["mask_queries"][:, :], 0.0), 7)
                link(pool.affine_select(out=w["mask_queries"][:, :], in_=w["mask_queries"][:, :],
                                        compare_op=ALU.is_ge, fill=NEG, base=0, pattern=[[-1, P]],
                                        channel_multiplier=1), 8)
                n = 8
                for name, size, value in (("group_mean", GN_CH, 1.0 / GN_CH),
                                          ("head_blocks", LIN_DIM, 1.0 / math.pi)):
                    v = w[name][:, :].rearrange("p (g d) -> p g d", d=size)
                    link(pool.memset(w[name][:, :], value), n + 1)
                    link(pool.affine_select(out=v, in_=v, compare_op=ALU.is_ge, fill=0.0, base=0,
                                            pattern=[[-size, C // size], [0, size]], channel_multiplier=1), n + 2)
                    link(pool.affine_select(out=v, in_=v, compare_op=ALU.is_ge, fill=0.0, base=size - 1,
                                            pattern=[[size, C // size], [0, size]], channel_multiplier=-1), n + 3)
                    n += 3
                link(pool.memset(w["centre"][:, :], -1.0 / C), n + 1)
                link(pool.affine_select(out=w["centre"][:, :], in_=w["centre"][:, :], compare_op=ALU.not_equal,
                                        fill=1.0 - 1.0 / C, base=0, pattern=[[-1, C]], channel_multiplier=1), n + 2)
                assert n + 2 == MADE



            @block.vector
            def _(dve):
                cnt = [0]

                def link(ins):
                    cnt[0] += 1
                    ins.then_inc(step, 1)
                    dve.wait_ge(step, cnt[0])
                link(dve.memset(ones1[:, :], 1.0 / (gs1 * C)))
                link(dve.memset(ones2[:, :], 1.0 / (gs2 * HIDDEN)))
                link(dve.memset(w["eps"][:, :], 1e-5))
                dve.wait_ge(loaded, 16 * NLOADS)
                dve.wait_ge(made, MADE)
                link(dve.tensor_copy(w["w_lin"][:, 3 * C:4 * C], w["centre"][:, :]))
                link(dve.tensor_scalar(g_fc1[:, :], fc1_raw[:, :], lng[:, 0:1], None, ALU.mult))
                pairs = attn_raw[:, 0:2 * C].rearrange("p (j s d) -> p j s d", s=2, d=HD)
                link(dve.tensor_copy(pairs[:, :, 0, :], qkv3[:, 0, :].rearrange("p (j d) -> p j d", d=HD)))
                link(dve.tensor_copy(pairs[:, :, 1, :], qkv3[:, 1, :].rearrange("p (j d) -> p j d", d=HD)))
                link(dve.tensor_copy(attn_raw[:, 2 * C:3 * C], qkv3[:, 2, :]))
                link(dve.tensor_copy(attn_raw[:, 3 * C:4 * C], w["ident"][0:C, 0:C]))
                dve.wait_ge(products, 1)
                link(dve.tensor_copy(w["fc1"][:, :], bank[0][0:C, 0:HIDDEN]))
                link(dve.tensor_tensor(w["fc1_bias"][:, :], bank[1][:, 0:CHUNKS], fc1b[:, :], ALU.add))
                link(dve.tensor_copy(w["wq_t"][:, :], bank[2][0:C, 0:C]))
                link(dve.tensor_copy(fc2_t[:, :], bank[3][0:C, 0:HIDDEN]))
                link(dve.tensor_tensor(w["out_bias"][:, :], bank[4][0:C, 0:1], projb[:, :], ALU.add))
                link(dve.tensor_copy(w["w_attn"][:, :], bank[5][0:C, 0:4 * C]))
                link(dve.tensor_copy(w1_t[:, :], bank[6][0:C, 0:HIDDEN]))
                link(dve.tensor_copy(w2_t[:, :, :], bank[7][:, 0:CHUNKS * C].rearrange("p (k c) -> p k c", c=C)))
                link(dve.tensor_reduce(s1[:, :], w1_t[:, 0:GROUPS * gs1].rearrange("p (g n) -> p g n", n=gs1),
                                       AX.X, ALU.add))
                link(dve.tensor_reduce(s2[:, :, :], w2_t[:, :, 0:GROUPS * gs2].rearrange("p k (g n) -> p k g n", n=gs2),
                                       AX.X, ALU.add))
                link(dve.tensor_reduce(sp2[:, :], s2[:, :, :].rearrange("p k g -> p g k"), AX.X, ALU.add))
                dve.wait_ge(products, 2)
                link(dve.tensor_copy(w["fc2"][:, :, :], bank[0][:, 0:CHUNKS * C].rearrange("p (k c) -> p k c", c=C)))
                link(dve.tensor_copy(m1[:, :], bank[1][0:C, 0:GROUPS]))
                link(dve.tensor_copy(m2[:, :], bank[2][:, 0:GROUPS]))
                link(dve.memset(w["w1"][0:C, :], 0.0))
                link(dve.memset(w["w2"][:, :, :], 0.0))
                for g in range(GROUPS):
                    c1, c2 = slice(g * gs1, (g + 1) * gs1), slice(g * gs2, (g + 1) * gs2)
                    link(dve.tensor_scalar(z1[:, c1], w1_t[:, c1], m1[:, g:g + 1], None, ALU.is_gt))
                    link(dve.tensor_scalar(n1[:, c1], w1_t[:, c1], m1[:, g:g + 1], None, ALU.is_lt))
                    link(dve.tensor_tensor(w["w1"][0:C, c1], z1[:, c1], n1[:, c1], ALU.subtract))
                    link(dve.tensor_scalar(z2[:, :, c2], w2_t[:, :, c2], m2[:, g:g + 1], None, ALU.is_gt))
                    link(dve.tensor_scalar(n2[:, :, c2], w2_t[:, :, c2], m2[:, g:g + 1], None, ALU.is_lt))
                    link(dve.tensor_tensor(w["w2"][:, :, c2], z2[:, :, c2], n2[:, :, c2], ALU.subtract))

            @block.tensor
            def _(pe):
                pe.wait_ge(step, 9)
                idn = w["ident"]
                pe.matmul(bank[0][0:C, 0:HIDDEN], w["centre"][:, :], g_fc1[:, :], start=True, stop=True)
                for k in range(CHUNKS):
                    pe.matmul(bank[1][:, k:k + 1], fc1_raw[:, k * P:(k + 1) * P], lnb[:, :], start=True, stop=True)
                pe.transpose(bank[2][0:C, 0:C], w["w_lin"][:, 0:C], idn[0:C, 0:C])
                for k in range(CHUNKS):
                    pe.transpose(bank[3][0:C, k * P:(k + 1) * P], fc2_raw[:, k, :], idn[:, :])
                pe.matmul(bank[4][0:C, 0:1], w["proj"][:, :], fc2b[:, :], start=True, stop=True)
                pe.matmul(bank[5][0:C, 0:4 * C], w["centre"][:, :], attn_raw[:, :], start=True, stop=True)
                for k in range(CHUNKS):
                    pe.transpose(bank[6][0:C, k * P:(k + 1) * P], w1_raw[:, k, :], idn[:, :])
                for k in range(CHUNKS):
                    mm = pe.transpose(bank[7][:, k * C:(k + 1) * C], w2_raw[:, k * P:(k + 1) * P], idn[0:C, 0:C])
                mm.then_inc(products, 1)
                pe.wait_ge(step, 20)
                for k in range(CHUNKS):
                    pe.matmul(bank[0][:, k * C:(k + 1) * C], fc2_t[:, k * P:(k + 1) * P], w["proj"][:, :],
                              start=True, stop=True)
                pe.matmul(bank[1][0:C, 0:GROUPS], ones1[:, 0:C], s1[:, :], start=True, stop=True)
                pe.matmul(bank[2][:, 0:GROUPS], ones2[:, :], sp2[:, :], start=True, stop=True).then_inc(products, 1)


def _pipeline(eng, body, items, stages, unroll):
    first = -(-(stages + 2) // unroll) * unroll
    count = (items - first) // unroll
    last = first + count * unroll

    def peeled(i):
        body(i, i % unroll, i // unroll, lambda s: 0 <= i - s < items)

    for i in range(first):
        peeled(i)
    with eng.Fori(0, count) as k:
        for r in range(unroll):
            body(k * unroll + (first + r), r, k + first // unroll, lambda s: True)
    for i in range(last, items + stages - 1):
        peeled(i)


def _dmas(lap, slot, back, slots):
    return (lap + ((slot - back) // slots + 1)) * 16


def conv_block(nc, w, x_in, x1):
    with ExitStack() as ctx:
        def sb(name, shape, dt=FP32):
            return ctx.enter_context(nc.sbuf_tensor("cb_" + name, shape, dt))

        def sem(name):
            return ctx.enter_context(nc.semaphore("cb_" + name))
        X = sb("x", [C, 2, L])
        XR = sb("x_again", [C, 2, L])
        X1 = sb("x1", [C, 2, L])
        XS = sb("xs", [C, 2, L])
        STATS = sb("stats", [C, 2, 6])
        MV = sb("mean_var", [C, 4])
        GS = sb("group_stats", [C, 4])
        GV = sb("group_var", [C, 3])
        QKV = sb("qkv", [P, 2, TILES, 4 * C])
        SQ = sb("squares", [P, TILES, 3 * C])
        NS = sb("norm_sums", [P, TILES, 16])
        NR = sb("norm_roots", [P, 2, TILES, 16])
        VS = sb("var_sums", [P, TILES])
        VR = sb("var_roots", [P, TILES])
        KR = sb("k_scale", [P, TILES, 8])
        XRS = sb("x_scale", [P, TILES])
        KH = sb("k_hat", [P, 2, TILES, C])
        XN = sb("xn", [P, 2, TILES, C])
        QV = sb("q_norm_v", [P, 2, TILES, C])
        O = sb("o", [P, TILES, C])
        OSQ = sb("o_squares", [P, TILES, C])
        OS = sb("o_sums", [P, TILES * 8])
        OR = sb("o_roots", [P, TILES * 8])
        OI = sb("o_scale", [P, TILES * 8])
        OH = sb("o_hat", [P, TILES, C])
        AM = sb("attn_matrix", [C, C])
        MM = sb("query_matrix", [C, C])
        XNT = sb("xn_t", [C, L])
        OHT = sb("o_hat_t", [C, L])
        HT = sb("hidden_t", [P, 2, CHUNKS, L])
        pq, pt, pf, po = (ctx.enter_context(nc.psum_tensor("cb_ps_" + n, [P, 2 * BANK], FP32))
                          for n in ("qkv", "turn", "hidden", "out"))
        KV, M_, G_ = po[0:C, 0:C], po[0:C, C:2 * C], po[0:C, 2 * C:2 * C + 3]
        x_loaded = [sem(f"x_loaded{i}") for i in range(2)]
        xr_loaded = [sem(f"xr_loaded{i}") for i in range(2)]
        x1_stored = [sem(f"x1_stored{i}") for i in range(2)]
        names = ("bn_parts bn_done mv_ready g_done g_copied gn_var gn_std gn_scale xs_ready qkv_psum qkv_copied "
                 "squares norm_sums norm_roots norm_scales khat_ready xn_ready qv_ready kv_done a_ready m_done "
                 "m_ready xnt_psum xnt_ready fc1_psum hid_ready u_done o_ready o_squares o_sums o_roots o_scale "
                 "ohat_ready oht_psum oht_ready out_done x1_ready").split()
        S = {n: sem(n) for n in names}

        def halves(ps):
            return ps[:, :].rearrange("p (a n) -> p a n", a=2)[:, :, 0:4 * C]

        with nc.Block() as block:
            @block.sync
            def _(sp):
                def body(i, r, lap, on):
                    if on(0):
                        _above(sp.wait_ge, S["xs_ready"], i - 1)
                        sp.dma_start(X[:, r, :], x_in[i]).then_inc(x_loaded[r], 16)
                    if on(3):
                        _above(sp.wait_ge, S["x1_ready"], i - 4)
                        sp.dma_start(XR[:, (r + 1) % 2, :], x_in[i - 3]).then_inc(xr_loaded[(r + 1) % 2], 16)
                    if on(4):
                        sp.wait_ge(S["x1_ready"], i - 3)
                        sp.dma_start(x1[i - 4], X1[:, r, :]).then_inc(x1_stored[r], 16)
                _pipeline(sp, body, BATCH, 5, 2)
                for r in range(2):
                    sp.wait_ge(x1_stored[r], 16 * (BATCH // 2))

            @block.vector
            def _(dve):
                def body(i, r, lap, on):
                    q = (r + 1) % 2
                    if on(0):
                        dve.wait_ge(x_loaded[r], _dmas(lap, r, 0, 2))
                        for a in range(2):
                            dve.bn_stats(STATS[:, a, :], X[:, r, a * BANK:(a + 1) * BANK]).then_inc(S["bn_parts"], 1)
                        dve.wait_ge(S["bn_parts"], 2 * i + 2)
                        _above(dve.wait_ge, S["g_done"], i)
                    if on(2):
                        dve.wait_ge(S["kv_done"], i - 1)
                        dve.tensor_tensor(AM[:, :], KV, w["head_blocks"][:, :], ALU.mult).then_inc(S["a_ready"], 1)
                    if on(0):
                        dve.bn_aggr(MV[:, 0:2], STATS[:, :, :]).then_inc(S["bn_done"], 1)
                        dve.wait_ge(S["bn_done"], i + 1)
                        dve.scalar_tensor_tensor(out=MV[:, 2:3], in0=MV[:, 0:1], scalar=MV[:, 0:1], in1=MV[:, 1:2],
                                                 op0=ALU.mult, op1=ALU.add).then_inc(S["mv_ready"], 1)
                    if on(3):
                        dve.wait_ge(S["o_squares"], i - 2)
                        dve.tensor_reduce(OS[:, :], OSQ[:, :, :].rearrange("p t (h d) -> p (t h) d", d=LIN_DIM),
                                          AX.X, ALU.add).then_inc(S["o_sums"], 1)
                        dve.wait_ge(S["o_roots"], i - 2)
                        _above(dve.wait_ge, S["ohat_ready"], i - 3)
                        dve.reciprocal(OI[:, :], OR[:, :]).then_inc(S["o_scale"], 1)
                    if on(0):
                        dve.wait_ge(S["g_done"], i + 1)
                        dve.tensor_copy(GS[:, 0:3], G_).then_inc(S["g_copied"], 1)
                        dve.wait_ge(S["g_copied"], i + 1)
                        dve.scalar_tensor_tensor(out=GV[:, 0:1], in0=GS[:, 0:1], scalar=GS[:, 0:1], in1=GS[:, 2:3],
                                                 op0=ALU.mult, op1=ALU.subtract).then_inc(S["gn_var"], 1)
                    if on(2):
                        dve.wait_ge(S["m_done"], i - 1)
                        dve.tensor_copy(MM[:, :], M_).then_inc(S["m_ready"], 1)
                    if on(1):
                        dve.wait_ge(S["squares"], 2 * i)
                        dve.tensor_reduce(VS[:, :], SQ[:, :, 2 * C:3 * C], AX.X, ALU.add)
                        dve.tensor_reduce(NS[:, :, :],
                                          SQ[:, :, 0:2 * C].rearrange("p t (h d) -> p t h d", d=LIN_DIM),
                                          AX.X, ALU.add).then_inc(S["norm_sums"], 1)
                        dve.wait_ge(S["norm_roots"], 2 * i)
                        dve.reciprocal(XRS[:, :], VR[:, :]).then_inc(S["norm_scales"], 1)
                        dve.reciprocal(KR[:, :, :], NR[:, q, :, 8:16]).then_inc(S["norm_scales"], 1)
                        dve.wait_ge(S["norm_scales"], 2 * i)
                        dve.tensor_tensor(XN[:, q, :, :], QKV[:, q, :, 3 * C:4 * C], _bcast(XRS[:, :], 2, C),
                                          ALU.mult).then_inc(S["xn_ready"], 1)
                        dve.tensor_tensor(KH[:, q, :, :].rearrange("p t (h d) -> p t h d", d=LIN_DIM),
                                          QKV[:, q, :, C:2 * C].rearrange("p t (h d) -> p t h d", d=LIN_DIM),
                                          _bcast(KR[:, :, :], 3, LIN_DIM), ALU.mult).then_inc(S["khat_ready"], 1)
                    if on(2):
                        dve.wait_ge(S["u_done"], i - 1)
                        dve.wait_ge(S["qv_ready"], i - 1)
                        _above(dve.wait_ge, S["ohat_ready"], i - 2)
                        dve.scalar_tensor_tensor(out=O[:, :, :].rearrange("p (a t) c -> p a (t c)", a=2),
                                                 in0=QV[:, r, :, :].rearrange("p (a t) c -> p a (t c)", a=2),
                                                 scalar=0.5, in1=halves(pf), op0=ALU.mult,
                                                 op1=ALU.add).then_inc(S["o_ready"], 1)
                    if on(0):
                        dve.wait_ge(S["gn_std"], i + 1)
                        dve.reciprocal(GV[:, 2:3], GV[:, 1:2]).then_inc(S["gn_scale"], 1)
                        dve.wait_ge(S["gn_scale"], i + 1)
                        _above(dve.wait_ge, S["u_done"], i - 1)
                        dve.tensor_scalar(XS[:, r, :], X[:, r, :], GS[:, 0:1], GV[:, 2:3], ALU.subtract,
                                          ALU.mult).then_inc(S["xs_ready"], 1)
                    if on(3):
                        dve.wait_ge(S["out_done"], i - 2)
                        dve.wait_ge(xr_loaded[q], _dmas(lap, r, 3, 2))
                        _above(dve.wait_ge, x1_stored[q], _dmas(lap, r, 5, 2))
                        dve.scalar_tensor_tensor(out=X1[:, q, :], in0=po[0:C, :], scalar=w["out_bias"][:, 0:1],
                                                 in1=XR[:, q, :], op0=ALU.add, op1=ALU.add).then_inc(S["x1_ready"], 1)
                _pipeline(dve, body, BATCH, 4, 2)

            @block.gpsimd
            def _(pool):
                def body(i, r, lap, on):
                    q = (r + 1) % 2
                    if on(3):
                        pool.wait_ge(S["o_scale"], i - 2)
                        _above(pool.wait_ge, S["oht_psum"], i - 3)
                        pool.tensor_tensor(OH[:, :, :].rearrange("p t (h d) -> p (t h) d", d=LIN_DIM),
                                           O[:, :, :].rearrange("p t (h d) -> p (t h) d", d=LIN_DIM),
                                           _bcast(OI[:, :], 2, LIN_DIM), ALU.mult).then_inc(S["ohat_ready"], 1)
                    if on(1):
                        pool.wait_ge(S["norm_roots"], 2 * i)
                        pool.tensor_tensor(QV[:, q, :, :].rearrange("p t (h d) -> p t h d", d=LIN_DIM),
                                           QKV[:, q, :, 2 * C:3 * C].rearrange("p t (h d) -> p t h d", d=LIN_DIM),
                                           _bcast(NR[:, q, :, 0:8], 3, LIN_DIM), ALU.mult).then_inc(S["qv_ready"], 1)
                _pipeline(pool, body, BATCH, 4, 2)

            @block.scalar
            def _(act):
                def body(i, r, lap, on):
                    q = (r + 1) % 2
                    if on(3):
                        act.wait_ge(S["o_ready"], i - 2)
                        act.activation(OSQ[:, :, :], O[:, :, :], ACT.Square).then_inc(S["o_squares"], 1)
                    if on(2):
                        act.wait_ge(S["xnt_psum"], i - 1)
                        act.activation(XNT[:, :], pt[0:C, :], ACT.Copy).then_inc(S["xnt_ready"], 1)
                    if on(3):
                        act.wait_ge(S["o_sums"], i - 2)
                        act.activation(OR[:, :], OS[:, :], ACT.Sqrt).then_inc(S["o_roots"], 1)
                    if on(1):
                        for t in range(TILES):
                            act.wait_ge(S["qkv_psum"], 8 * (i - 1) + t + 1)
                            act.activation(QKV[:, q, t, :], pq[:, (t % 2) * BANK:(t % 2) * BANK + 4 * C],
                                           ACT.Copy).then_inc(S["qkv_copied"], 1)
                        act.wait_ge(S["qkv_copied"], 8 * i)
                        act.activation(SQ[:, :, 2 * C:3 * C], QKV[:, q, :, 3 * C:4 * C],
                                       ACT.Square).then_inc(S["squares"], 1)
                        act.activation(SQ[:, :, 0:2 * C], QKV[:, q, :, 0:2 * C], ACT.Square).then_inc(S["squares"], 1)
                    if on(3):
                        act.wait_ge(S["oht_psum"], i - 2)
                        act.activation(OHT[:, :], pt[0:C, :], ACT.Copy).then_inc(S["oht_ready"], 1)
                    if on(0):
                        act.wait_ge(S["gn_var"], i + 1)
                        act.activation(GV[:, 1:2], GV[:, 0:1], ACT.Sqrt, bias=w["eps"][0:C, 0:1],
                                       scale=-1.0).then_inc(S["gn_std"], 1)
                    if on(1):
                        act.wait_ge(S["norm_sums"], i)
                        act.activation(VR[:, :], VS[:, :], ACT.Sqrt, bias=w["eps"][:, 0:1],
                                       scale=1.0 / C).then_inc(S["norm_roots"], 1)
                        act.activation(NR[:, q, :, :], NS[:, :, :], ACT.Sqrt).then_inc(S["norm_roots"], 1)
                    if on(2):
                        for k in range(CHUNKS):
                            for a in range(2):
                                act.wait_ge(S["fc1_psum"], 6 * (i - 2) + 2 * k + a + 1)
                                act.activation(HT[:, r, k, a * BANK:(a + 1) * BANK], pf[:, a * BANK:(a + 1) * BANK],
                                               ACT.Silu, bias=w["fc1_bias"][:, k:k + 1]).then_inc(S["hid_ready"], 1)
                _pipeline(act, body, BATCH, 4, 2)

            @block.tensor
            def _(pe):
                def body(i, r, lap, on):
                    q = (r + 1) % 2
                    if on(2):
                        pe.wait_ge(S["xn_ready"], i - 1)
                        _above(pe.wait_ge, S["oht_ready"], i - 3)
                        for t in range(TILES):
                            mm = pe.transpose(pt[0:C, t * P:(t + 1) * P], XN[:, r, t, :], w["ident"][:, :])
                        mm.then_inc(S["xnt_psum"], 1)
                        pe.wait_ge(S["khat_ready"], i - 1)
                    _above(pe.wait_ge, S["x1_ready"], (i - 3) if not isinstance(i, int) else min(i - 3, BATCH))
                    if on(2):
                        for t in range(TILES):
                            mm = pe.matmul(KV, KH[:, r, t, :], QKV[:, r, t, 2 * C:3 * C], start=(t == 0),
                                           stop=(t == TILES - 1))
                        mm.then_inc(S["kv_done"], 1)
                        pe.wait_ge(S["a_ready"], i - 1)
                    if on(0):
                        pe.wait_ge(S["mv_ready"], i + 1)
                        pe.matmul(G_, w["group_mean"][:, :], MV[:, 0:3], start=True, stop=True).then_inc(S["g_done"], 1)
                    if on(1):
                        pe.wait_ge(S["xs_ready"], i)
                        for t in range(TILES):
                            _above(pe.wait_ge, S["qkv_copied"], 8 * (i - 1) + t - 1)
                            pe.matmul(pq[:, (t % 2) * BANK:(t % 2) * BANK + 4 * C], XS[:, q, t * P:(t + 1) * P],
                                      w["w_lin"][:, :], start=True, stop=True).then_inc(S["qkv_psum"], 1)
                    if on(0):
                        pe.wait_ge(S["g_copied"], i + 1)
                    if on(2):
                        pe.matmul(M_, w["wq_t"][:, :], AM[:, :], start=True, stop=True).then_inc(S["m_done"], 1)
                    if on(3):
                        pe.wait_ge(S["ohat_ready"], i - 2)
                        if on(2):
                            pe.wait_ge(S["xnt_ready"], i - 1)
                        for t in range(TILES):
                            mm = pe.transpose(pt[0:C, t * P:(t + 1) * P], OH[:, t, :], w["ident"][:, :])
                        mm.then_inc(S["oht_psum"], 1)
                    if on(2):
                        pe.wait_ge(S["xnt_ready"], i - 1)
                        _above(pe.wait_ge, S["o_ready"], i - 2)
                        for k in range(CHUNKS):
                            for a in range(2):
                                if k:
                                    pe.wait_ge(S["hid_ready"], 6 * (i - 2) + 2 * k + a - 1)
                                pe.matmul(pf[:, a * BANK:(a + 1) * BANK], w["fc1"][:, k * P:(k + 1) * P],
                                          XNT[:, a * BANK:(a + 1) * BANK], start=True,
                                          stop=True).then_inc(S["fc1_psum"], 1)
                        pe.wait_ge(S["m_ready"], i - 1)
                        pe.wait_ge(S["hid_ready"], 6 * (i - 1))
                        for t in range(TILES):
                            c0 = (t // 4) * BANK + (t % 4) * C
                            mm = pe.matmul(pf[:, c0:c0 + C], XS[:, r, t * P:(t + 1) * P], MM[:, :], start=True,
                                           stop=True)
                        mm.then_inc(S["u_done"], 1)
                    if on(3):
                        pe.wait_ge(S["oht_ready"], i - 2)
                        for a in range(2):
                            half = slice(a * BANK, (a + 1) * BANK)
                            for k in range(CHUNKS):
                                pe.matmul(po[0:C, half], w["fc2"][:, k, :], HT[:, q, k, half], start=(k == 0),
                                          stop=False)
                            mm = pe.matmul(po[0:C, half], w["proj"][:, :], OHT[:, half], start=False, stop=True)
                        mm.then_inc(S["out_done"], 1)
                _pipeline(pe, body, BATCH, 4, 2)


def attention_rows(nc, w, x1, rows):
    with ExitStack() as ctx:
        def sb(name, shape, dt=FP32):
            return ctx.enter_context(nc.sbuf_tensor("ar_" + name, shape, dt))

        def sem(name):
            return ctx.enter_context(nc.semaphore("ar_" + name))
        X = sb("x", [C, 2, L])
        QKV = sb("qkv", [P, 2, TILES, 3 * C])
        SQ = sb("squares", [P, 2, TILES, C])
        VS = sb("var_sums", [P, TILES])
        VR = sb("var_roots", [P, TILES])
        SCALE = sb("scale", [P, 2, TILES])
        QK = sb("qk", [P, 2, TILES * HEADS, 2, HD])
        R1 = sb("rest1", [P, 2, TILES * HEADS, 2, HD])
        PK = sb("packed", [P, 2, TILES * HEADS, PACK], U32)
        pq = ctx.enter_context(nc.psum_tensor("ar_ps_qkv", [P, 8, BANK], FP32))
        x_loaded = [sem(f"x_loaded{i}") for i in range(2)]
        stored = [sem(f"stored{i}") for i in range(2)]
        names = ("qkv_psum qkv_copied squares var_sums var_roots scale qk_ready v_ready high_ready rest_ready "
                 "mid_ready low_ready").split()
        S = {n: sem(n) for n in names}

        def part(slot, n):
            return PK[:, slot, :, 0:PARTS // 2].bitcast(BF16).rearrange("p r (s m d) -> p r s m d", s=2, m=3)[:, :, :, n, :]

        with nc.Block() as block:
            @block.sync
            def _(sp):
                def body(i, r, lap, on):
                    if on(0):
                        _above(sp.wait_ge, S["qkv_psum"], TILES * (i - 1))
                        sp.dma_start(X[:, r, :], x1[i]).then_inc(x_loaded[r], 16)
                    if on(1):
                        q = (r + 1) % 2
                        sp.wait_ge(S["low_ready"], i)
                        sp.wait_ge(S["mid_ready"], i)
                        sp.wait_ge(S["v_ready"], i)
                        sp.dma_start(rows[i - 1].rearrange("(t p) n -> p t n", p=P),
                                     PK[:, q, :, :].rearrange("p (t j) n -> p t (j n)", j=HEADS)
                                     ).then_inc(stored[q], 16)
                _pipeline(sp, body, BATCH, 2, 2)
                for r in range(2):
                    sp.wait_ge(stored[r], 16 * (BATCH // 2))

            @block.tensor
            def _(pe):
                def body(i, r, lap, on):
                    if on(0):
                        pe.wait_ge(x_loaded[r], _dmas(lap, r, 0, 2))
                        for t in range(TILES):
                            _above(pe.wait_ge, S["qkv_copied"], TILES * (i - 1) + t + 1)
                            pe.matmul(pq[:, t, 0:4 * C], X[:, r, t * P:(t + 1) * P], w["w_attn"][:, :], start=True,
                                      stop=True).then_inc(S["qkv_psum"], 1)
                _pipeline(pe, body, BATCH, 2, 2)

            @block.scalar
            def _(act):
                def body(i, r, lap, on):
                    q = (r + 1) % 2
                    if on(1):
                        act.wait_ge(S["qk_ready"], i)
                        _above(act.wait_ge, stored[q], _dmas(lap, r, 3, 2))
                        act.activation(part(q, 0), QK[:, q, :, :, :], ACT.Copy).then_inc(S["high_ready"], 1)
                    if on(0):
                        for t in range(TILES):
                            act.wait_ge(S["qkv_psum"], TILES * i + t + 1)
                            if t == 0:
                                _above(act.wait_ge, S["v_ready"], i - 1)
                            act.activation(QKV[:, r, t, :], pq[:, t, 0:3 * C], ACT.Copy)
                            act.activation(SQ[:, r, t, :], pq[:, t, 3 * C:4 * C],
                                           ACT.Square).then_inc(S["qkv_copied"], 1)
                    if on(1):
                        act.wait_ge(S["rest_ready"], i)
                        act.activation(part(q, 1), R1[:, q, :, :, :], ACT.Copy).then_inc(S["mid_ready"], 1)
                    if on(0):
                        act.wait_ge(S["var_sums"], i + 1)
                        act.activation(VR[:, :], VS[:, :], ACT.Sqrt, bias=w["eps"][:, 0:1],
                                       scale=1.0 / C).then_inc(S["var_roots"], 1)
                _pipeline(act, body, BATCH, 2, 2)

            @block.vector
            def _(dve):
                def body(i, r, lap, on):
                    q = (r + 1) % 2
                    if on(1):
                        dve.wait_ge(S["mid_ready"], i)
                        dve.tensor_tensor(part(q, 2), R1[:, q, :, :, :], part(q, 1),
                                          ALU.subtract).then_inc(S["low_ready"], 1)
                    if on(0):
                        dve.wait_ge(S["qkv_copied"], TILES * (i + 1))
                        dve.tensor_reduce(VS[:, :], SQ[:, r, :, :], AX.X, ALU.add).then_inc(S["var_sums"], 1)
                        dve.wait_ge(S["var_roots"], i + 1)
                        _above(dve.wait_ge, S["v_ready"], i - 1)
                        dve.reciprocal(SCALE[:, r, :], VR[:, :]).then_inc(S["scale"], 1)
                        dve.wait_ge(S["scale"], i + 1)
                        _above(dve.wait_ge, S["rest_ready"], i - 1)
                        dve.tensor_tensor(QK[:, r, :, :, :].rearrange("p (t j) s d -> p t (j s d)", j=HEADS),
                                          QKV[:, r, :, 0:2 * C], _bcast(SCALE[:, r, :], 2, 2 * C),
                                          ALU.mult).then_inc(S["qk_ready"], 1)
                _pipeline(dve, body, BATCH, 2, 2)

            @block.gpsimd
            def _(pool):
                def body(i, r, lap, on):
                    q = (r + 1) % 2
                    if on(1):
                        pool.wait_ge(S["high_ready"], i)
                        _above(pool.wait_ge, S["low_ready"], i - 2)
                        pool.tensor_tensor(R1[:, q, :, :, :], QK[:, q, :, :, :], part(q, 0),
                                           ALU.subtract).then_inc(S["rest_ready"], 1)
                    if on(0):
                        pool.wait_ge(S["scale"], i + 1)
                        _above(pool.wait_ge, stored[r], _dmas(lap, r, 2, 2))
                        v = PK[:, r, :, PARTS // 2:PACK].bitcast(FP32).rearrange("p (t j) d -> p t j d", j=HEADS)
                        pool.tensor_tensor(v, QKV[:, r, :, 2 * C:3 * C].rearrange("p t (j d) -> p t j d", d=HD),
                                           _bcast(_bcast(SCALE[:, r, :], 2, HEADS), 3, HD),
                                           ALU.mult).then_inc(S["v_ready"], 1)
                _pipeline(pool, body, BATCH, 2, 2)


def _score_units():
    units = [[(0, 0, BANK, 0)], [(0, BANK, BANK, 0)]]
    for kb in range(1, TILES // 2 + 1):
        q0 = kb * P
        units.append([(kb, q0, BANK, 0)])
        rest = L - q0 - BANK
        if rest:
            other = TILES - kb
            units.append([(kb, q0 + BANK, rest, 0), (other, other * P, kb * P, rest)])
    return units


def causal_attention(nc, w, rows, att):
    scale = C ** -0.5
    UNITS = _score_units()
    NU = len(UNITS)
    QUNITS = [(qb, k0, min(BANK, (qb + 1) * P - k0)) for qb in range(TILES)
              for k0 in range(0, (qb + 1) * P, BANK)]
    NQ = len(QUNITS)
    SLOTS = 3
    VW = 32
    QG = P // VW
    with ExitStack() as ctx:
        def sb(name, shape, dt=FP32):
            return ctx.enter_context(nc.sbuf_tensor("at_" + name, shape, dt))

        def pb(name, shape, dt=FP32):
            return ctx.enter_context(nc.psum_tensor("at_ps_" + name, shape, dt))

        def sem(name):
            return ctx.enter_context(nc.semaphore("at_" + name))
        RW = sb("rows", [P, SLOTS, TILES, PACK], U32)
        QS = sb("q_stack", [P, SLOTS, TILES, STACK], BF16)
        KS = sb("k_stack", [P, SLOTS, TILES, STACK], BF16)
        V = sb("v", [P, SLOTS, TILES, VW])
        QT = sb("q_t", [P, SLOTS, L], BF16)
        KT = sb("k_t", [P, SLOTS, L], BF16)
        MX = sb("unit_max", [P, TILES, 2])
        NM = sb("neg_max", [P, TILES])
        MP = sb("max_parts", [P, TILES, 32], BF16)
        PR = sb("probs", [P, SLOTS, BANK])
        RC = sb("recip", [P, TILES])
        ONE = sb("one", [P, 1, 1])
        OT = sb("out_t", [P, 2 * P])
        AT = sb("att", [P, SLOTS, TILES, HD])
        pq = pb("queries", [P, 2, BANK])
        pk = pb("keys", [P, SLOTS, BANK])
        pv = pb("values", [P, BANK])
        turned = pb("turn", [P, L], BF16)
        po = pb("out", [P, BANK])
        out_t = pv[:, 0:2 * P]
        out_ps = po[:, 0:2 * P].rearrange("p (t d) -> p t d", d=VW)
        loaded = [sem(f"loaded{i}") for i in range(SLOTS)]
        stored = [sem(f"stored{i}") for i in range(SLOTS)]
        names = ("set_up zeros_set one_set max_set parts_set spread q_turned k_turned q_ready k_ready q_scores unit_max head_max "
                 "max_high max_parts max_turned max_ready k_scores probs values out_copied out_turned recip out_ready").split()
        S = {n: sem(n) for n in names}
        src = rows.rearrange("b l (j n) -> (b l j) n", n=PACK).rearrange("(h t p) n -> h p t n", t=TILES, p=P)
        dst = att.rearrange("b l (j d) -> (b l j) d", d=HD).rearrange("(h t p) d -> h p t d", t=TILES, p=P)

        with nc.Block() as block:
            @block.sync
            def _(sp):
                def body(i, r, lap, on):
                    if on(0):
                        _above(sp.wait_ge, S["spread"], i - SLOTS + 1)
                        sp.dma_start(RW[:, r, :, :], src[i]).then_inc(loaded[r], 16)
                    if on(4):
                        q = (r - 4) % SLOTS
                        sp.wait_ge(S["out_ready"], i - 3)
                        sp.dma_start(dst[i - 4], AT[:, q, :, :]).then_inc(stored[q], 16)
                _pipeline(sp, body, NHEADS, 5, SLOTS)
                for r in range(SLOTS):
                    sp.wait_ge(stored[r], 16 * (NHEADS // SLOTS))

            @block.gpsimd
            def _(pool):
                pool.memset(V[:, :, :, HD:VW], 0.0).then_inc(S["zeros_set"], 1)
                pool.wait_ge(S["zeros_set"], 1)
                pool.memset(V[:, :, :, HD:HD + 1], 1.0)
                pool.memset(ONE[:, :, :], 1.0).then_inc(S["one_set"], 1)
                pool.wait_ge(S["one_set"], 1)

                def body(i, r, lap, on):
                    if on(0):
                        pool.wait_ge(loaded[r], _dmas(lap, r, 0, SLOTS))
                        _above(pool.wait_ge, S["k_turned"], i - 2)
                        _above(pool.wait_ge, S["values"], NU * (i - 2))
                        v = RW[:, r, :, PARTS // 2:PACK].bitcast(FP32)
                        pool.tensor_tensor(V[:, r, :, 0:HD], v, ONE[:, :, :].broadcast_to([P, TILES, HD]), ALU.mult)
                        parts = RW[:, r, :, 0:PARTS // 2].bitcast(BF16)
                        qp = parts[:, :, 0:3 * HD].rearrange("p t (m d) -> p t m d", d=HD)
                        qs = QS[:, r, :, :].rearrange("p t (m d) -> p t m d", d=HD)
                        pool.tensor_copy(qs[:, :, 0:3, :], qp[:, :, 0:1, :].broadcast_to([P, TILES, 3, HD]))
                        pool.tensor_copy(qs[:, :, 3:5, :], qp[:, :, 1:2, :].broadcast_to([P, TILES, 2, HD]))
                        pool.tensor_copy(qs[:, :, 5, :], qp[:, :, 2, :])
                        kp = parts[:, :, 3 * HD:6 * HD]
                        pool.tensor_copy(KS[:, r, :, 0:3 * HD], kp)
                        pool.tensor_copy(KS[:, r, :, 3 * HD:5 * HD], kp[:, :, 0:2 * HD])
                        pool.tensor_copy(KS[:, r, :, 5 * HD:6 * HD], kp[:, :, 0:HD]).then_inc(S["spread"], 1)
                _pipeline(pool, body, NHEADS, 3, SLOTS)

            @block.tensor
            def _(pe):
                pe.wait_ge(S["set_up"], 2)

                def turn_q(i, r):
                    pe.wait_ge(S["spread"], i + 1)
                    _above(pe.wait_ge, S["max_ready"], i - 1)
                    for t in range(TILES):
                        mm = pe.transpose(turned[0:STACK, t * P:(t + 1) * P], QS[:, r, t, :], w["ident_bf"][:, :])
                    mm.then_inc(S["q_turned"], 1)

                def turn_k(i, r):
                    pe.wait_ge(S["q_ready"], i + 1)
                    for t in range(TILES):
                        mm = pe.transpose(turned[0:STACK, t * P:(t + 1) * P], KS[:, r, t, :], w["ident_bf"][:, :])
                    mm.then_inc(S["k_turned"], 1)

                def turn_max(h, last):
                    pe.wait_ge(S["max_parts"], h + 1)
                    if not last:
                        pe.wait_ge(S["k_ready"], h + 2)
                    for t in range(TILES):
                        mm = pe.transpose(turned[96:128, t * P:(t + 1) * P], MP[:, t, :], w["ident_bf"][:, :])
                    mm.then_inc(S["max_turned"], 1)

                def turn_out(h):
                    pe.wait_ge(S["out_copied"], h + 1)
                    _above(pe.wait_ge, S["out_ready"], h)
                    for a in range(2):
                        mm = pe.transpose(po[:, a * P:(a + 1) * P], OT[:, a * P:(a + 1) * P], w["ident"][:, :])
                    mm.then_inc(S["out_turned"], 1)

                def query_scores(h, slot, u):
                    qb, k0, n = QUNITS[u]
                    if u == 0:
                        pe.wait_ge(S["q_ready"], h + 1)
                        pe.wait_ge(S["k_ready"], h + 1)
                    _above(pe.wait_ge, S["unit_max"], NQ * h + u - 1)
                    diag = k0 + n == (qb + 1) * P
                    mm = pe.matmul(pq[:, u % 2, 0:n], QT[0:STACK, slot, qb * P:(qb + 1) * P],
                                   KT[0:STACK, slot, k0:k0 + n], start=True, stop=True)
                    if diag:
                        mm = pe.matmul(pq[:, u % 2, n - P:n], w["ident_bf"][:, :], w["mask_queries"][:, :],
                                       start=False, stop=True, skip_group_check=True)
                    mm.then_inc(S["q_scores"], 1)

                def key_scores(h, slot, u):
                    if u == 0:
                        pe.wait_ge(S["max_ready"], h + 1)
                    _above(pe.wait_ge, S["probs"], NU * h + u - 2)
                    for kb, q0, n, c0 in UNITS[u]:
                        diag = q0 == kb * P
                        mm = pe.matmul(pk[:, u % SLOTS, c0:c0 + n], KT[:, slot, kb * P:(kb + 1) * P],
                                       QT[:, slot, q0:q0 + n], start=True, stop=True)
                        if diag:
                            mm = pe.matmul(pk[:, u % SLOTS, c0:c0 + P], w["ident_bf"][:, :], w["mask_keys"][:, :],
                                           start=False, stop=True, skip_group_check=True)
                    mm.then_inc(S["k_scores"], 1)

                def values(h, slot, u):
                    pe.wait_ge(S["probs"], NU * h + u + 1)
                    if u == 0:
                        _above(pe.wait_ge, S["out_copied"], h)
                    for kb, q0, n, c0 in UNITS[u]:
                        for b in range(n // P):
                            qb = q0 // P + b
                            row, col = VW * (qb % QG), P * (qb // QG)
                            mm = pe.matmul(out_t[row:row + VW, col:col + P], V[:, slot, kb, :],
                                           PR[:, u % SLOTS, c0 + b * P:c0 + (b + 1) * P],
                                           start=(u == 0 and b < QG), stop=True, skip_group_check=True)
                    mm.then_inc(S["values"], 1)

                def body(i, r, lap, on):
                    s1, s2 = (r - 1) % SLOTS, (r - 2) % SLOTS
                    if on(2):
                        turn_max(i - 2, not on(1))
                    nq = 0
                    for u in range(NU):
                        if on(1):
                            want = -(-NQ * (u + 1) // NU)
                            while nq < want:
                                query_scores(i - 1, s1, nq)
                                nq += 1
                        if on(2):
                            key_scores(i - 2, s2, u)
                            if u >= 2:
                                values(i - 2, s2, u - 2)
                        if u == 3 and on(0):
                            turn_q(i, r)
                        if u == 6 and on(0):
                            turn_k(i, r)
                        if u == 1 and on(3):
                            turn_out(i - 3)
                    if on(2):
                        values(i - 2, s2, NU - 2)
                        values(i - 2, s2, NU - 1)
                _pipeline(pe, body, NHEADS, 4, SLOTS)

            @block.scalar
            def _(act):
                def body(i, r, lap, on):
                    for u in range(NU):
                        if on(2):
                            act.wait_ge(S["k_scores"], NU * (i - 2) + u + 1)
                            _above(act.wait_ge, S["values"], NU * (i - 2) + u - 2)
                            act.activation(PR[:, u % SLOTS, :], pk[:, u % SLOTS, :], ACT.Exp,
                                           scale=scale).then_inc(S["probs"], 1)
                        if u == 3 and on(0):
                            act.wait_ge(S["q_turned"], i + 1)
                            act.activation(QT[0:STACK, r, :], turned[0:STACK, :], ACT.Copy).then_inc(S["q_ready"], 1)
                        if u == 6 and on(0):
                            act.wait_ge(S["k_turned"], i + 1)
                            act.activation(KT[0:STACK, r, :], turned[0:STACK, :], ACT.Copy).then_inc(S["k_ready"], 1)
                _pipeline(act, body, NHEADS, 3, SLOTS)

            @block.vector
            def _(dve):
                dve.memset(MX[:, :, :], -3.0e38).then_inc(S["max_set"], 1)
                dve.memset(MP[:, :, :], 0.0).then_inc(S["parts_set"], 1)
                dve.memset(KT[96:128, :, :], 0.0).then_inc(S["set_up"], 1)
                dve.wait_ge(S["set_up"], 1)
                dve.memset(KT[96:98, :, :], 1.0).then_inc(S["set_up"], 1)
                dve.wait_ge(S["max_set"], 1)
                dve.wait_ge(S["parts_set"], 1)

                def body(i, r, lap, on):
                    s1, s2 = (r - 1) % SLOTS, (r - 2) % SLOTS
                    if on(2):
                        dve.wait_ge(S["max_turned"], i - 1)
                        dve.tensor_copy(QT[96:128, s2, :], turned[96:128, :]).then_inc(S["max_ready"], 1)
                    for u, (qb, k0, n) in enumerate(QUNITS):
                        if on(1):
                            dve.wait_ge(S["q_scores"], NQ * (i - 1) + u + 1)
                            dve.tensor_reduce(MX[:, qb, k0 // BANK:k0 // BANK + 1], pq[:, u % 2, 0:n], AX.X,
                                              ALU.max).then_inc(S["unit_max"], 1)
                        if u == 3 and on(3):
                            dve.wait_ge(S["out_turned"], i - 2)
                            dve.reciprocal(RC[:, :], out_ps[:, :, HD]).then_inc(S["recip"], 1)
                            dve.wait_ge(S["recip"], i - 2)
                            _above(dve.wait_ge, stored[r], _dmas(lap, r, 6, SLOTS))
                            dve.tensor_tensor(AT[:, r, :, :], out_ps[:, :, 0:HD], _bcast(RC[:, :], 2, HD),
                                              ALU.mult).then_inc(S["out_ready"], 1)
                    if on(1):
                        dve.wait_ge(S["unit_max"], NQ * i)
                        dve.tensor_reduce(NM[:, :], MX[:, :, :], AX.X, ALU.max, negate=True).then_inc(S["head_max"], 1)
                        dve.wait_ge(S["head_max"], i)
                        dve.tensor_copy(MP[:, :, 0], NM[:, :]).then_inc(S["max_high"], 1)
                        dve.wait_ge(S["max_high"], i)
                        dve.tensor_tensor(MP[:, :, 1], NM[:, :], MP[:, :, 0],
                                          ALU.subtract).then_inc(S["max_parts"], 1)
                    if on(2):
                        dve.wait_ge(S["values"], NU * (i - 1))
                        dve.tensor_copy(OT[:, :], out_t).then_inc(S["out_copied"], 1)
                _pipeline(dve, body, NHEADS, 4, SLOTS)


def project_and_ffn(nc, w, att, x1, y_out):
    LIMIT = QB - QEPS
    REST = BATCH - GROUPS * GB
    with ExitStack() as ctx:
        def sb(name, shape, dt=FP32):
            return ctx.enter_context(nc.sbuf_tensor("ff_" + name, shape, dt))

        def sem(name):
            return ctx.enter_context(nc.semaphore("ff_" + name))
        AR = sb("att_rows", [P, 2, TILES, C])
        X1 = sb("x1", [C, 2, L])
        AT = sb("att_t", [C, L])
        X2 = sb("x2", [C, GB, L])
        SQ = sb("squares", [P, TILES, C])
        VS = sb("var_sums", [P, TILES])
        VR = sb("var_roots", [P, TILES])
        SCALE = sb("scale", [P, TILES])
        XN = sb("xn", [P, 2, TILES, C])
        XNT = sb("xn_t", [C + 1, L])
        Y1 = sb("hidden", [P, GB, CHUNKS, L])
        Y2 = sb("ffn", [C, GB, L])
        OUT = sb("out", [C, 2, L])
        G1, G2 = sb("max1", [P, GB]), sb("max2", [C, GB])
        ROW = sb("row_of_ones", [1, P])
        M1, M2 = sb("group_max1", [P, 4]), sb("group_max2", [C, 4])
        pt, py, pc, pf = (ctx.enter_context(nc.psum_tensor("ff_ps_" + n, [P, 2 * BANK], FP32))
                          for n in ("turn", "out", "centred", "hidden"))
        xc = pc[:, :].rearrange("p (a n) -> p a n", a=2)[:, :, 0:4 * C]
        a_loaded = [sem(f"att_loaded{i}") for i in range(2)]
        x_loaded = [sem(f"x1_loaded{i}") for i in range(2)]
        stored = [sem(f"stored{i}") for i in range(2)]
        names = ("ones_set att_turned att_copied y_done x2_ready xc_done squares var_sums var_roots scale xn_ready "
                 "xn_turned xnt_ready y1_psum y1_copied y1_max max1 all_max1 scale1 gelu h_ready y2_psum y2_ready "
                 "y2_max max2 all_max2 scale2 limited out_ready").split()
        S = {n: sem(n) for n in names}

        def groups(eng, body):
            with eng.Fori(0, GROUPS) as g:
                body(g, lambda j: g * GB + j, GB)
            body(GROUPS, lambda j: GROUPS * GB + j, REST)

        with nc.Block() as block:
            @block.sync
            def _(sp):
                def load(j, entry):
                    sp.dma_start(AR[:, j % 2, :, :], att[entry].rearrange("(t p) c -> p t c", p=P)
                                 ).then_inc(a_loaded[j % 2], 16)
                    sp.dma_start(X1[:, j % 2, :], x1[entry]).then_inc(x_loaded[j % 2], 16)

                load(0, 0)
                load(1, 1)
                with sp.Fori(0, GROUPS) as g:
                    n = g * GB
                    for j in range(2, GB):
                        sp.wait_ge(S["att_turned"], n + (j - 1))
                        sp.wait_ge(S["x2_ready"], n + (j - 1))
                        load(j, n + j)
                    for j in range(GB):
                        sp.wait_ge(S["out_ready"], n + (j + 1))
                        sp.dma_start(y_out[n + j], OUT[:, j % 2, :]).then_inc(stored[j % 2], 16)
                    for j in range(2):
                        sp.wait_ge(stored[j], (g + 1) * (16 * GB // 2))
                        load(j, n + (GB + j))
                for j in range(REST):
                    sp.wait_ge(S["x2_ready"], GROUPS * GB + j + 1)
                    sp.dma_start(y_out[GROUPS * GB + j], X2[:, j, :]).then_inc(stored[j % 2], 16)
                for r in range(2):
                    sp.wait_ge(stored[r], 16 * (BATCH // 2))

            @block.tensor
            def _(pe):
                pe.wait_ge(S["ones_set"], 2)

                def body(g, n, size):
                    full = size == GB

                    def hidden(j, k):
                        for a in range(2):
                            if k or j:
                                pe.wait_ge(S["y1_copied"], 6 * n(j) + 2 * k + a - 1)
                            pe.matmul(pf[:, a * BANK:(a + 1) * BANK], w["w1"][:, k * P:(k + 1) * P],
                                      XNT[:, a * BANK:(a + 1) * BANK], start=True, stop=True
                                      ).then_inc(S["y1_psum"], 1)
                    def spread_max(M, name, all_name):
                        parts = M.shape[0]
                        pe.wait_ge(S[name], 2 * g + 1)
                        pe.transpose(pc[0:1, 0:parts], M[:, 0:1], w["ident"][0:parts, 0:parts]
                                     ).then_inc(S[all_name], 1)
                        pe.wait_ge(S[name], 2 * g + 2)
                        pe.matmul(pc[0:parts, BANK:BANK + 1], ROW[:, 0:parts], M[0:1, 1:2], start=True, stop=True
                                  ).then_inc(S[all_name], 1)

                    for j in range(size + 2):
                        if full and j >= 2:
                            pe.wait_ge(S["xn_ready"], n(j - 1))
                            for t in range(TILES):
                                mm = pe.transpose(pt[0:C, t * P:(t + 1) * P], XN[:, j % 2, t, :], w["ident"][:, :])
                            mm.then_inc(S["xn_turned"], 1)
                        if full and 1 <= j <= size:
                            pe.wait_ge(S["x2_ready"], n(j))
                            for t in range(TILES):
                                c0 = (t // 4) * BANK + (t % 4) * C
                                mm = pe.matmul(pc[:, c0:c0 + C], X2[:, j - 1, t * P:(t + 1) * P], w["centre"][:, :],
                                               start=True, stop=True)
                            mm.then_inc(S["xc_done"], 1)
                        if j < size:
                            pe.wait_ge(a_loaded[j % 2], (g * (GB // 2) + (j // 2 + 1)) * 16)
                            if full and j >= 2:
                                pe.wait_ge(S["xnt_ready"], n(j - 1))
                            for t in range(TILES):
                                mm = pe.transpose(pt[0:C, t * P:(t + 1) * P], AR[:, j % 2, t, :], w["ident"][:, :])
                            mm.then_inc(S["att_turned"], 1)
                        if full and j >= 2:
                            pe.wait_ge(S["xnt_ready"], n(j - 1))
                            hidden(j - 2, 0)
                        if j < size:
                            pe.wait_ge(S["att_copied"], n(j + 1))
                            if not full or j:
                                pe.wait_ge(S["x2_ready"], n(j))
                            for a in range(2):
                                half = slice(a * BANK, (a + 1) * BANK)
                                mm = pe.matmul(py[0:C, half], w["wp"][:, :], AT[:, half], start=True, stop=True)
                            mm.then_inc(S["y_done"], 1)
                        if full and j >= 2:
                            hidden(j - 2, 1)
                            hidden(j - 2, 2)
                    if not full:
                        return
                    spread_max(M1, "max1", "all_max1")
                    for j in range(size):
                        pe.wait_ge(S["h_ready"], 3 * n(j + 1))
                        if j:
                            pe.wait_ge(S["y2_ready"], n(j))
                        for a in range(2):
                            half = slice(a * BANK, (a + 1) * BANK)
                            for k in range(CHUNKS):
                                mm = pe.matmul(py[0:C, half], w["w2"][:, k, :], Y1[:, j, k, half], start=(k == 0),
                                               stop=(k == CHUNKS - 1))
                        mm.then_inc(S["y2_psum"], 1)
                    spread_max(M2, "max2", "all_max2")
                groups(pe, body)

            @block.scalar
            def _(act):
                def body(g, n, size):
                    full = size == GB
                    for j in range(size + 2):
                        if full and j >= 2:
                            act.wait_ge(S["xn_turned"], n(j - 1))
                            act.activation(XNT[0:C, :], pt[0:C, :], ACT.Copy).then_inc(S["xnt_ready"], 1)
                        if j < size:
                            act.wait_ge(S["att_turned"], n(j + 1))
                            act.activation(AT[:, :], pt[0:C, :], ACT.Copy).then_inc(S["att_copied"], 1)
                        if full and 1 <= j <= size:
                            act.wait_ge(S["xc_done"], n(j))
                            act.activation(SQ[:, :, :].rearrange("p (a t) c -> p a (t c)", a=2), xc,
                                           ACT.Square).then_inc(S["squares"], 1)
                            act.wait_ge(S["var_sums"], n(j))
                            act.activation(VR[:, :], VS[:, :], ACT.Sqrt, bias=w["eps"][:, 0:1],
                                           scale=1.0 / C).then_inc(S["var_roots"], 1)
                        if full and j >= 2:
                            for k in range(CHUNKS):
                                for a in range(2):
                                    act.wait_ge(S["y1_psum"], 6 * n(j - 2) + 2 * k + a + 1)
                                    act.activation(Y1[:, j - 2, k, a * BANK:(a + 1) * BANK],
                                                   pf[:, a * BANK:(a + 1) * BANK], ACT.Copy
                                                   ).then_inc(S["y1_copied"], 1)
                    if full:
                        act.wait_ge(S["scale1"], 2 * g + 2)
                        for j in range(size + 1):
                            if j < size:
                                for k in range(CHUNKS):
                                    act.activation(Y1[:, j, k, :], Y1[:, j, k, :], ACT.Gelu,
                                                   scale=M1[:, 3:4]).then_inc(S["gelu"], 1)
                            if j:
                                act.wait_ge(S["y2_psum"], n(j))
                                act.activation(Y2[:, j - 1, :], py[0:C, :], ACT.Identity, bias=w["b2"][:, 0:1]
                                               ).then_inc(S["y2_ready"], 1)
                groups(act, body)

            @block.vector
            def _(dve):
                dve.memset(ROW[:, :], 1.0).then_inc(S["ones_set"], 1)
                dve.memset(XNT[C:C + 1, :], 1.0).then_inc(S["ones_set"], 1)

                def group_scale(g, entry, peak, maxima, M, name, all_name, scale_name):
                    dve.wait_ge(S[peak], entry)
                    dve.tensor_reduce(M[:, 0:1], maxima[:, :], AX.X, ALU.max).then_inc(S[name], 1)
                    dve.wait_ge(S[all_name], 2 * g + 1)
                    dve.tensor_reduce(M[0:1, 1:2], pc[0:1, 0:M.shape[0]], AX.X, ALU.max).then_inc(S[name], 1)
                    dve.wait_ge(S[all_name], 2 * g + 2)
                    dve.tensor_scalar(M[:, 2:3], pc[0:M.shape[0], BANK:BANK + 1], QEPS, 1.0 / QB, ALU.add, ALU.mult
                                      ).then_inc(S[scale_name], 1)
                    dve.wait_ge(S[scale_name], 2 * g + 1)
                    dve.reciprocal(M[:, 3:4], M[:, 2:3]).then_inc(S[scale_name], 1)

                def body(g, n, size):
                    full = size == GB

                    def peak1(j):
                        dve.wait_ge(S["y1_copied"], 6 * n(j + 1))
                        dve.tensor_reduce(G1[:, j:j + 1], Y1[:, j, :, :], AX.XY, ALU.max,
                                          apply_absolute_value=True).then_inc(S["y1_max"], 1)
                    for j in range(size + 2):
                        if full and 1 <= j <= size:
                            q = (j - 1) % 2
                            dve.wait_ge(S["squares"], n(j))
                            dve.tensor_reduce(VS[:, :], SQ[:, :, :], AX.X, ALU.add).then_inc(S["var_sums"], 1)
                            dve.wait_ge(S["var_roots"], n(j))
                            dve.reciprocal(SCALE[:, :], VR[:, :]).then_inc(S["scale"], 1)
                            dve.wait_ge(S["scale"], n(j))
                            for a in range(2):
                                ins = dve.tensor_tensor(XN[:, q, 4 * a:4 * a + 4, :],
                                                        xc[:, a, :].rearrange("p (t c) -> p t c", c=C),
                                                        _bcast(SCALE[:, 4 * a:4 * a + 4], 2, C), ALU.mult)
                            ins.then_inc(S["xn_ready"], 1)
                        if j < size:
                            dve.wait_ge(S["y_done"], n(j + 1))
                            dve.wait_ge(x_loaded[j % 2], (g * (GB // 2) + (j // 2 + 1)) * 16)
                            dve.scalar_tensor_tensor(out=X2[:, j, :], in0=py[0:C, :], scalar=w["bp"][:, 0:1],
                                                     in1=X1[:, j % 2, :], op0=ALU.add, op1=ALU.add
                                                     ).then_inc(S["x2_ready"], 1)
                        if full and j >= 2:
                            peak1(j - 2)
                    if not full:
                        return
                    group_scale(g, n(size), "y1_max", G1, M1, "max1", "all_max1", "scale1")
                    for j in range(size + 1):
                        if j < size:
                            for k in range(CHUNKS):
                                dve.wait_ge(S["gelu"], 3 * n(j) + k + 1)
                                dve.tensor_scalar(Y1[:, j, k, :], Y1[:, j, k, :], LIMIT, None, ALU.min
                                                  ).then_inc(S["h_ready"], 1)
                        if j:
                            dve.wait_ge(S["y2_ready"], n(j))
                            dve.tensor_reduce(G2[:, j - 1:j], Y2[:, j - 1, :], AX.X, ALU.max,
                                              apply_absolute_value=True).then_inc(S["y2_max"], 1)
                    group_scale(g, n(size), "y2_max", G2, M2, "max2", "all_max2", "scale2")
                    dve.wait_ge(S["scale2"], 2 * g + 2)
                    for j in range(size):
                        dve.tensor_scalar(Y2[:, j, :], Y2[:, j, :], M2[:, 3:4], LIMIT, ALU.mult, ALU.min
                                          ).then_inc(S["limited"], 1)
                        dve.wait_ge(S["limited"], n(j + 1))
                        if j >= 2:
                            dve.wait_ge(stored[j % 2], (g * (GB // 2) + j // 2) * 16)
                        dve.scalar_tensor_tensor(out=OUT[:, j % 2, :], in0=Y2[:, j, :], scalar=-LIMIT,
                                                 in1=X2[:, j, :], op0=ALU.max, op1=ALU.add
                                                 ).then_inc(S["out_ready"], 1)
                groups(dve, body)


def build(nc, A, out):
    x1 = nc.dram_tensor("x_after_conv", [BATCH, C, L], FP32, kind="Internal").ap()
    rows = nc.dram_tensor("qkv_rows", [BATCH, L, HEADS * PACK], U32, kind="Internal").ap()
    att = nc.dram_tensor("attention_rows", [BATCH, L, C], FP32, kind="Internal").ap()
    x_in = A["x"].rearrange("b c h w -> b c (h w)")
    y_out = out.rearrange("b c h w -> b c (h w)")
    with ExitStack() as ctx:
        w = _constants(nc, ctx)
        prepare(nc, w, A)
        conv_block(nc, w, x_in, x1)
        attention_rows(nc, w, x1, rows)
        causal_attention(nc, w, rows, att)
        project_and_ffn(nc, w, att, x1, y_out)


_INS = ['x', 'L0_conv_qkv_w', 'L0_conv_proj_w', 'L0_conv_proj_b', 'L0_conv_ln_g', 'L0_conv_ln_b',
        'L0_conv_fc1_w', 'L0_conv_fc1_b', 'L0_conv_fc2_w', 'L0_conv_fc2_b', 'L1_attn_Wk', 'L1_attn_Wq',
        'L1_attn_Wv', 'L1_attn_Wp', 'L1_attn_bp', 'L1_ffn_W1', 'L1_ffn_b1', 'L1_ffn_W2', 'L1_ffn_b2']


def kernel(**inputs):
    import numpy as _np
    import concourse.bacc as _bacc
    from concourse import mybir as _mybir
    from concourse.bass_utils import run_bass_kernel_spmd as _run

    nc = _bacc.Bacc("TRN2", target_bir_lowering=False, num_devices=1)
    arrays, args = {}, {}
    for name in _INS:
        a = _np.ascontiguousarray(inputs[name])
        arrays[f"in_{name}_dram"] = a
        args[name] = nc.dram_tensor(f"in_{name}_dram", a.shape, _mybir.dt.from_np(a.dtype), kind="ExternalInput").ap()
    out = nc.dram_tensor("out_0_dram", (BATCH, C, SIDE, SIDE), _mybir.dt.from_np(_np.dtype("float32")),
                         kind="ExternalOutput").ap()
    build(nc, args, out)
    r = _run(nc, [arrays], core_ids=[0])
    return r.results[0]["out_0_dram"]
```

```python
import concourse.bass as bass
from concourse import mybir
from contextlib import ExitStack
import math

FP32 = mybir.dt.float32
BF16 = mybir.dt.bfloat16
U32 = mybir.dt.uint32
ALU = mybir.AluOpType
ACT = mybir.ActivationFunctionType
AX = mybir.AxisListType

BATCH, C, SIDE = 32, 96, 32
L = SIDE * SIDE
P = 128
TILES = L // P
BANK = 512
HIDDEN = 4 * C
CHUNKS = HIDDEN // P
GN_CH = C // 32
LIN_HEADS, LIN_DIM = 8, C // 8
HEADS, HD = 6, C // 6
ROWS = L * C // HD
NHEADS = BATCH * HEADS
PW = 3 * HD // 2
PACK = PW + HD + PW
STACK = 6 * HD
GROUPS = 5
GB = BATCH // GROUPS
QB, QEPS = 128.0, 1e-5
NEG = -1.0e30


def _bcast(ap, axis, n):
    ap = ap.unsqueeze(axis)
    shape = list(ap.shape)
    shape[axis] = n
    return ap.broadcast_to(shape)


def _above(sem_wait, sem, value):
    if not isinstance(value, int) or value > 0:
        sem_wait(sem, value)


def _constants(nc, ctx):
    def sb(name, shape, dt=FP32):
        return ctx.enter_context(nc.sbuf_tensor(name, shape, dt))
    w = {}
    w["ident"] = sb("ident", [P, P])
    w["ident_bf"] = sb("ident_bf", [P, P], BF16)
    w["mask_keys"] = sb("mask_keys", [P, P], BF16)
    w["mask_queries"] = sb("mask_queries", [P, P], BF16)
    w["centre"] = sb("centre", [C, C])
    w["group_mean"] = sb("group_mean", [C, C])
    w["head_blocks"] = sb("head_blocks", [C, C])
    w["w_lin"] = sb("w_lin", [C, 4 * C])
    w["wq_t"] = sb("wq_t", [C, C])
    w["fc1"] = sb("fc1", [C, HIDDEN])
    w["fc1_bias"] = sb("fc1_bias", [P, CHUNKS])
    w["fc2"] = sb("fc2", [P, CHUNKS, C])
    w["proj"] = sb("proj", [C, C])
    w["out_bias"] = sb("out_bias", [C, 1])
    w["w_attn"] = sb("w_attn", [C, 4 * C])
    w["wp"] = sb("wp", [C, C])
    w["bp"] = sb("bp", [C, 1])
    w["w1"] = sb("w1", [C + 1, HIDDEN])
    w["w2"] = sb("w2", [P, CHUNKS, C])
    w["b2"] = sb("b2", [C, 1])
    w["eps"] = sb("eps", [P, 1])
    return w


def prepare(nc, w, A):
    ctx = ExitStack()
    with ctx:
        def sb(name, shape, dt=FP32):
            return ctx.enter_context(nc.sbuf_tensor(name, shape, dt))

        def sem(name):
            return ctx.enter_context(nc.semaphore(name))
        g_fc1 = sb("g_fc1", [C, HIDDEN])
        fc1_raw = sb("fc1_raw", [C, HIDDEN])
        fc2_raw = sb("fc2_raw", [P, CHUNKS, C])
        fc2_t = sb("fc2_t", [C, HIDDEN])
        attn_raw = sb("attn_raw", [C, 4 * C])
        qkv3 = sb("qkv3", [C, 3, C])
        w1_raw = sb("w1_raw", [P, CHUNKS, C])
        w1_t = sb("w1_t", [C, HIDDEN])
        w2_raw = sb("w2_raw", [C, HIDDEN])
        w2_t = sb("w2_t", [P, CHUNKS, C])
        lng = sb("lng", [C, 1])
        lnb = sb("lnb", [C, 1])
        fc1b = sb("fc1b", [P, CHUNKS])
        fc2b = sb("fc2b", [C, 1])
        projb = sb("projb", [C, 1])
        ones1 = sb("ones1", [C, P])
        ones2 = sb("ones2", [P, P])
        s1 = sb("s1", [C, GROUPS])
        s2 = sb("s2", [P, CHUNKS, GROUPS])
        sp2 = sb("sp2", [P, GROUPS])
        m1 = sb("m1", [C, GROUPS])
        m2 = sb("m2", [P, GROUPS])
        z1 = sb("z1", [C, HIDDEN])
        z2 = sb("z2", [P, CHUNKS, C])
        n1 = sb("n1", [C, HIDDEN])
        n2 = sb("n2", [P, CHUNKS, C])
        bank = [ctx.enter_context(nc.psum_tensor(f"prep{i}", [P, BANK], FP32)) for i in range(8)]
        loaded, made = sem("prep_loaded"), sem("prep_made")
        products, step = sem("prep_products"), sem("prep_step")
        gs1, gs2 = HIDDEN // GROUPS, C // GROUPS
        loads = [
            (w["w_lin"][:, 0:3 * C], A["L0_conv_qkv_w"]),
            (w["proj"][:, :], A["L0_conv_proj_w"]),
            (fc1_raw[:, :], A["L0_conv_fc1_w"]),
            (fc2_raw[:, :, :], A["L0_conv_fc2_w"].rearrange("(k p) c -> p k c", p=P)),
            (qkv3[:, 0, :], A["L1_attn_Wq"]),
            (qkv3[:, 1, :], A["L1_attn_Wk"]),
            (qkv3[:, 2, :], A["L1_attn_Wv"]),
            (w["wp"][:, :], A["L1_attn_Wp"]),
            (w1_raw[:, :, :], A["L1_ffn_W1"].rearrange("(k p) c -> p k c", p=P)),
            (w2_raw[:, :], A["L1_ffn_W2"]),
            (w["w1"][C:C + 1, :], A["L1_ffn_b1"].rearrange("(a n) -> a n", a=1)),
            (lng[:, :], A["L0_conv_ln_g"].rearrange("(n a) -> n a", a=1)),
            (lnb[:, :], A["L0_conv_ln_b"].rearrange("(n a) -> n a", a=1)),
            (fc1b[:, :], A["L0_conv_fc1_b"].rearrange("(k p) -> p k", p=P)),
            (fc2b[:, :], A["L0_conv_fc2_b"].rearrange("(n a) -> n a", a=1)),
            (projb[:, :], A["L0_conv_proj_b"].rearrange("(n a) -> n a", a=1)),
            (w["bp"][:, :], A["L1_attn_bp"].rearrange("(n a) -> n a", a=1)),
            (w["b2"][:, :], A["L1_ffn_b2"].rearrange("(n a) -> n a", a=1)),
        ]
        NLOADS = len(loads)
        MADE = 16
        with nc.Block() as block:
            @block.sync
            def _(sp):
                with nc.allow_non_contiguous_dma(reason="bias columns, once"):
                    for dst, src in loads:
                        sp.dma_start(dst, src).then_inc(loaded, 16)
                sp.wait_ge(loaded, 16 * NLOADS)

            @block.gpsimd
            def _(pool):
                def link(ins, n):
                    ins.then_inc(made, 1)
                    pool.wait_ge(made, n)
                link(pool.memset(w["ident"][:, :], 0.0), 1)
                link(pool.affine_select(out=w["ident"][:, :], in_=w["ident"][:, :], compare_op=ALU.not_equal,
                                        fill=1.0, base=0, pattern=[[-1, P]], channel_multiplier=1), 2)
                link(pool.memset(w["ident_bf"][:, :], 0.0), 3)
                link(pool.affine_select(out=w["ident_bf"][:, :], in_=w["ident_bf"][:, :], compare_op=ALU.not_equal,
                                        fill=1.0, base=0, pattern=[[-1, P]], channel_multiplier=1), 4)
                link(pool.memset(w["mask_keys"][:, :], 0.0), 5)
                link(pool.affine_select(out=w["mask_keys"][:, :], in_=w["mask_keys"][:, :], compare_op=ALU.is_ge,
                                        fill=NEG, base=0, pattern=[[1, P]], channel_multiplier=-1), 6)
                link(pool.memset(w["mask_queries"][:, :], 0.0), 7)
                link(pool.affine_select(out=w["mask_queries"][:, :], in_=w["mask_queries"][:, :],
                                        compare_op=ALU.is_ge, fill=NEG, base=0, pattern=[[-1, P]],
                                        channel_multiplier=1), 8)
                n = 8
                for name, size, value in (("group_mean", GN_CH, 1.0 / GN_CH),
                                          ("head_blocks", LIN_DIM, 1.0 / math.pi)):
                    v = w[name][:, :].rearrange("p (g d) -> p g d", d=size)
                    link(pool.memset(w[name][:, :], value), n + 1)
                    link(pool.affine_select(out=v, in_=v, compare_op=ALU.is_ge, fill=0.0, base=0,
                                            pattern=[[-size, C // size], [0, size]], channel_multiplier=1), n + 2)
                    link(pool.affine_select(out=v, in_=v, compare_op=ALU.is_ge, fill=0.0, base=size - 1,
                                            pattern=[[size, C // size], [0, size]], channel_multiplier=-1), n + 3)
                    n += 3
                link(pool.memset(w["centre"][:, :], -1.0 / C), n + 1)
                link(pool.affine_select(out=w["centre"][:, :], in_=w["centre"][:, :], compare_op=ALU.not_equal,
                                        fill=1.0 - 1.0 / C, base=0, pattern=[[-1, C]], channel_multiplier=1), n + 2)
                assert n + 2 == MADE



            @block.vector
            def _(dve):
                cnt = [0]

                def link(ins):
                    cnt[0] += 1
                    ins.then_inc(step, 1)
                    dve.wait_ge(step, cnt[0])
                link(dve.memset(ones1[:, :], 1.0 / (gs1 * C)))
                link(dve.memset(ones2[:, :], 1.0 / (gs2 * HIDDEN)))
                link(dve.memset(w["eps"][:, :], 1e-5))
                dve.wait_ge(loaded, 16 * NLOADS)
                dve.wait_ge(made, MADE)
                link(dve.tensor_copy(w["w_lin"][:, 3 * C:4 * C], w["centre"][:, :]))
                link(dve.tensor_scalar(g_fc1[:, :], fc1_raw[:, :], lng[:, 0:1], None, ALU.mult))
                pairs = attn_raw[:, 0:2 * C].rearrange("p (j s d) -> p j s d", s=2, d=HD)
                link(dve.tensor_copy(pairs[:, :, 0, :], qkv3[:, 1, :].rearrange("p (j d) -> p j d", d=HD)))
                link(dve.tensor_copy(pairs[:, :, 1, :], qkv3[:, 0, :].rearrange("p (j d) -> p j d", d=HD)))
                link(dve.tensor_copy(attn_raw[:, 2 * C:3 * C], qkv3[:, 2, :]))
                link(dve.tensor_copy(attn_raw[:, 3 * C:4 * C], w["ident"][0:C, 0:C]))
                dve.wait_ge(products, 1)
                link(dve.tensor_copy(w["fc1"][:, :], bank[0][0:C, 0:HIDDEN]))
                link(dve.tensor_tensor(w["fc1_bias"][:, :], bank[1][:, 0:CHUNKS], fc1b[:, :], ALU.add))
                link(dve.tensor_copy(w["wq_t"][:, :], bank[2][0:C, 0:C]))
                link(dve.tensor_copy(fc2_t[:, :], bank[3][0:C, 0:HIDDEN]))
                link(dve.tensor_tensor(w["out_bias"][:, :], bank[4][0:C, 0:1], projb[:, :], ALU.add))
                link(dve.tensor_copy(w["w_attn"][:, :], bank[5][0:C, 0:4 * C]))
                link(dve.tensor_copy(w1_t[:, :], bank[6][0:C, 0:HIDDEN]))
                link(dve.tensor_copy(w2_t[:, :, :], bank[7][:, 0:CHUNKS * C].rearrange("p (k c) -> p k c", c=C)))
                link(dve.tensor_reduce(s1[:, :], w1_t[:, 0:GROUPS * gs1].rearrange("p (g n) -> p g n", n=gs1),
                                       AX.X, ALU.add))
                link(dve.tensor_reduce(s2[:, :, :], w2_t[:, :, 0:GROUPS * gs2].rearrange("p k (g n) -> p k g n", n=gs2),
                                       AX.X, ALU.add))
                link(dve.tensor_reduce(sp2[:, :], s2[:, :, :].rearrange("p k g -> p g k"), AX.X, ALU.add))
                dve.wait_ge(products, 2)
                link(dve.tensor_copy(w["fc2"][:, :, :], bank[0][:, 0:CHUNKS * C].rearrange("p (k c) -> p k c", c=C)))
                link(dve.tensor_copy(m1[:, :], bank[1][0:C, 0:GROUPS]))
                link(dve.tensor_copy(m2[:, :], bank[2][:, 0:GROUPS]))
                link(dve.memset(w["w1"][0:C, :], 0.0))
                link(dve.memset(w["w2"][:, :, :], 0.0))
                for g in range(GROUPS):
                    c1, c2 = slice(g * gs1, (g + 1) * gs1), slice(g * gs2, (g + 1) * gs2)
                    link(dve.tensor_scalar(z1[:, c1], w1_t[:, c1], m1[:, g:g + 1], None, ALU.is_gt))
                    link(dve.tensor_scalar(n1[:, c1], w1_t[:, c1], m1[:, g:g + 1], None, ALU.is_lt))
                    link(dve.tensor_tensor(w["w1"][0:C, c1], z1[:, c1], n1[:, c1], ALU.subtract))
                    link(dve.tensor_scalar(z2[:, :, c2], w2_t[:, :, c2], m2[:, g:g + 1], None, ALU.is_gt))
                    link(dve.tensor_scalar(n2[:, :, c2], w2_t[:, :, c2], m2[:, g:g + 1], None, ALU.is_lt))
                    link(dve.tensor_tensor(w["w2"][:, :, c2], z2[:, :, c2], n2[:, :, c2], ALU.subtract))

            @block.tensor
            def _(pe):
                pe.wait_ge(step, 9)
                idn = w["ident"]
                pe.matmul(bank[0][0:C, 0:HIDDEN], w["centre"][:, :], g_fc1[:, :], start=True, stop=True)
                for k in range(CHUNKS):
                    pe.matmul(bank[1][:, k:k + 1], fc1_raw[:, k * P:(k + 1) * P], lnb[:, :], start=True, stop=True)
                pe.transpose(bank[2][0:C, 0:C], w["w_lin"][:, 0:C], idn[0:C, 0:C])
                for k in range(CHUNKS):
                    pe.transpose(bank[3][0:C, k * P:(k + 1) * P], fc2_raw[:, k, :], idn[:, :])
                pe.matmul(bank[4][0:C, 0:1], w["proj"][:, :], fc2b[:, :], start=True, stop=True)
                pe.matmul(bank[5][0:C, 0:4 * C], w["centre"][:, :], attn_raw[:, :], start=True, stop=True)
                for k in range(CHUNKS):
                    pe.transpose(bank[6][0:C, k * P:(k + 1) * P], w1_raw[:, k, :], idn[:, :])
                for k in range(CHUNKS):
                    mm = pe.transpose(bank[7][:, k * C:(k + 1) * C], w2_raw[:, k * P:(k + 1) * P], idn[0:C, 0:C])
                mm.then_inc(products, 1)
                pe.wait_ge(step, 20)
                for k in range(CHUNKS):
                    pe.matmul(bank[0][:, k * C:(k + 1) * C], fc2_t[:, k * P:(k + 1) * P], w["proj"][:, :],
                              start=True, stop=True)
                pe.matmul(bank[1][0:C, 0:GROUPS], ones1[:, 0:C], s1[:, :], start=True, stop=True)
                pe.matmul(bank[2][:, 0:GROUPS], ones2[:, :], sp2[:, :], start=True, stop=True).then_inc(products, 1)


def _pipeline(eng, body, items, stages, unroll):
    first = -(-(stages + 2) // unroll) * unroll
    count = (items - first) // unroll
    last = first + count * unroll

    def peeled(i):
        body(i, i % unroll, i // unroll, lambda s: 0 <= i - s < items)

    for i in range(first):
        peeled(i)
    with eng.Fori(0, count) as k:
        for r in range(unroll):
            body(k * unroll + (first + r), r, k + first // unroll, lambda s: True)
    for i in range(last, items + stages - 1):
        peeled(i)


def _dmas(lap, slot, back, slots):
    return (lap + ((slot - back) // slots + 1)) * 16


def conv_block(nc, w, x_in, x1, rows):
    with ExitStack() as ctx:
        def sb(name, shape, dt=FP32):
            return ctx.enter_context(nc.sbuf_tensor("cb_" + name, shape, dt))

        def sem(name):
            return ctx.enter_context(nc.semaphore("cb_" + name))
        X = sb("x", [C, 2, L])
        XR = sb("x_again", [C, 2, L])
        X1 = sb("x1", [C, 2, L])
        XS = sb("xs", [C, 2, L])
        STATS = sb("stats", [C, 2, 6])
        MV = sb("mean_var", [C, 4])
        GS = sb("group_stats", [C, 4])
        GV = sb("group_var", [C, 3])
        QKV = sb("qkv", [P, 2, TILES, 4 * C])
        SQ = sb("squares", [P, TILES, 3 * C])
        NS = sb("norm_sums", [P, TILES, 16])
        NR = sb("norm_roots", [P, 2, TILES, 16])
        VS = sb("var_sums", [P, TILES])
        VR = sb("var_roots", [P, TILES])
        KR = sb("k_scale", [P, TILES, 8])
        XRS = sb("x_scale", [P, TILES])
        KH = sb("k_hat", [P, 2, TILES, C])
        XN = sb("xn", [P, 2, TILES, C])
        QV = sb("q_norm_v", [P, 2, TILES, C])
        O = sb("o", [P, TILES, C])
        OSQ = sb("o_squares", [P, TILES, C])
        OS = sb("o_sums", [P, TILES * 8])
        OR = sb("o_roots", [P, TILES * 8])
        OI = sb("o_scale", [P, TILES * 8])
        OH = sb("o_hat", [P, TILES, C])
        AM = sb("attn_matrix", [C, C])
        MM = sb("query_matrix", [C, C])
        XNT = sb("xn_t", [C, L])
        OHT = sb("o_hat_t", [C, L])
        HT = sb("hidden_t", [P, 2, CHUNKS, L])
        AQKV = sb("a_qkv", [P, 2, TILES, 3 * C])
        ASQ = sb("a_squares", [P, TILES, C])
        AVS = sb("a_var_sums", [P, TILES])
        AVR = sb("a_var_roots", [P, TILES])
        ASC = sb("a_scale", [P, 2, TILES])
        AQK = sb("a_qk", [P, TILES * HEADS, 2, HD])
        AR1 = sb("a_rest", [P, TILES * HEADS, 2, HD])
        PK = sb("packed", [P, 2, TILES * HEADS, PACK], U32)

        def part(slot, n):
            return PK[:, slot, :, :].bitcast(BF16).rearrange("p r (m d) -> p r m d", d=HD)[:, :, n:n + 6:5, :]

        pq, pt, pf, po = (ctx.enter_context(nc.psum_tensor("cb_ps_" + n, [P, 2 * BANK], FP32))
                          for n in ("qkv", "turn", "hidden", "out"))
        KV, M_, G_ = po[0:C, 0:C], po[0:C, C:2 * C], po[0:C, 2 * C:2 * C + 3]
        x_loaded = [sem(f"x_loaded{i}") for i in range(2)]
        xr_loaded = [sem(f"xr_loaded{i}") for i in range(2)]
        x1_stored = [sem(f"x1_stored{i}") for i in range(2)]
        rows_stored = [sem(f"rows_stored{i}") for i in range(2)]
        names = ("bn_parts bn_done mv_ready g_done g_copied gn_var gn_std gn_scale xs_ready qkv_psum qkv_copied "
                 "squares norm_sums norm_roots norm_scales khat_ready xn_ready qv_ready kv_done a_ready m_done "
                 "m_ready xnt_psum xnt_ready fc1_psum hid_ready u_done o_ready o_squares o_sums o_roots o_scale "
                 "ohat_ready oht_psum oht_ready out_done x1_ready a_psum a_copied a_sums a_roots a_scale qk_ready "
                 "v_ready high_ready rest_ready mid_ready low_ready").split()
        S = {n: sem(n) for n in names}

        def halves(ps):
            return ps[:, :].rearrange("p (a n) -> p a n", a=2)[:, :, 0:4 * C]

        with nc.Block() as block:
            @block.sync
            def _(sp):
                def body(i, r, lap, on):
                    if on(0):
                        _above(sp.wait_ge, S["xs_ready"], i - 1)
                        sp.dma_start(X[:, r, :], x_in[i]).then_inc(x_loaded[r], 16)
                    if on(3):
                        _above(sp.wait_ge, S["x1_ready"], i - 4)
                        sp.dma_start(XR[:, (r + 1) % 2, :], x_in[i - 3]).then_inc(xr_loaded[(r + 1) % 2], 16)
                    if on(4):
                        sp.wait_ge(S["x1_ready"], i - 3)
                        sp.dma_start(x1[i - 4], X1[:, r, :]).then_inc(x1_stored[r], 16)
                    if on(7):
                        sp.wait_ge(S["low_ready"], i - 6)
                        sp.dma_start(rows[i - 7].rearrange("(t p) n -> p t n", p=P),
                                     PK[:, (r + 1) % 2, :, :].rearrange("p (t j) n -> p t (j n)", j=HEADS)
                                     ).then_inc(rows_stored[(r + 1) % 2], 16)
                _pipeline(sp, body, BATCH, 8, 2)
                for r in range(2):
                    sp.wait_ge(x1_stored[r], 16 * (BATCH // 2))
                    sp.wait_ge(rows_stored[r], 16 * (BATCH // 2))

            @block.vector
            def _(dve):
                def body(i, r, lap, on):
                    q = (r + 1) % 2
                    if on(5):
                        dve.wait_ge(S["a_copied"], TILES * (i - 4))
                        dve.tensor_reduce(AVS[:, :], ASQ[:, :, :], AX.X, ALU.add).then_inc(S["a_sums"], 1)
                    if on(0):
                        dve.wait_ge(x_loaded[r], _dmas(lap, r, 0, 2))
                        for a in range(2):
                            dve.bn_stats(STATS[:, a, :], X[:, r, a * BANK:(a + 1) * BANK]).then_inc(S["bn_parts"], 1)
                        dve.wait_ge(S["bn_parts"], 2 * i + 2)
                        _above(dve.wait_ge, S["g_done"], i)
                    if on(2):
                        dve.wait_ge(S["kv_done"], i - 1)
                        dve.tensor_tensor(AM[:, :], KV, w["head_blocks"][:, :], ALU.mult).then_inc(S["a_ready"], 1)
                    if on(0):
                        dve.bn_aggr(MV[:, 0:2], STATS[:, :, :]).then_inc(S["bn_done"], 1)
                        dve.wait_ge(S["bn_done"], i + 1)
                        dve.scalar_tensor_tensor(out=MV[:, 2:3], in0=MV[:, 0:1], scalar=MV[:, 0:1], in1=MV[:, 1:2],
                                                 op0=ALU.mult, op1=ALU.add).then_inc(S["mv_ready"], 1)
                    if on(3):
                        dve.wait_ge(S["o_squares"], i - 2)
                        dve.tensor_reduce(OS[:, :], OSQ[:, :, :].rearrange("p t (h d) -> p (t h) d", d=LIN_DIM),
                                          AX.X, ALU.add).then_inc(S["o_sums"], 1)
                        dve.wait_ge(S["o_roots"], i - 2)
                        _above(dve.wait_ge, S["ohat_ready"], i - 3)
                        dve.reciprocal(OI[:, :], OR[:, :]).then_inc(S["o_scale"], 1)
                    if on(0):
                        dve.wait_ge(S["g_done"], i + 1)
                        dve.tensor_copy(GS[:, 0:3], G_).then_inc(S["g_copied"], 1)
                        dve.wait_ge(S["g_copied"], i + 1)
                        dve.scalar_tensor_tensor(out=GV[:, 0:1], in0=GS[:, 0:1], scalar=GS[:, 0:1], in1=GS[:, 2:3],
                                                 op0=ALU.mult, op1=ALU.subtract).then_inc(S["gn_var"], 1)
                    if on(2):
                        dve.wait_ge(S["m_done"], i - 1)
                        dve.tensor_copy(MM[:, :], M_).then_inc(S["m_ready"], 1)
                    if on(5):
                        dve.wait_ge(S["a_roots"], i - 4)
                        _above(dve.wait_ge, S["v_ready"], i - 6)
                        dve.reciprocal(ASC[:, q, :], AVR[:, :]).then_inc(S["a_scale"], 1)
                        dve.wait_ge(S["a_scale"], i - 4)
                        _above(dve.wait_ge, S["rest_ready"], i - 5)
                        dve.tensor_tensor(AQK[:, :, :, :].rearrange("p (t j) s d -> p t (j s d)", j=HEADS),
                                          AQKV[:, q, :, 0:2 * C], _bcast(ASC[:, q, :], 2, 2 * C),
                                          ALU.mult).then_inc(S["qk_ready"], 1)
                    if on(6):
                        dve.wait_ge(S["mid_ready"], i - 5)
                        dve.tensor_tensor(part(r, 2), AR1[:, :, :, :], part(r, 1),
                                          ALU.subtract).then_inc(S["low_ready"], 1)
                    if on(1):
                        dve.wait_ge(S["squares"], 2 * i)
                        dve.tensor_reduce(VS[:, :], SQ[:, :, 2 * C:3 * C], AX.X, ALU.add)
                        dve.tensor_reduce(NS[:, :, :],
                                          SQ[:, :, 0:2 * C].rearrange("p t (h d) -> p t h d", d=LIN_DIM),
                                          AX.X, ALU.add).then_inc(S["norm_sums"], 1)
                        dve.wait_ge(S["norm_roots"], 2 * i)
                        dve.reciprocal(XRS[:, :], VR[:, :]).then_inc(S["norm_scales"], 1)
                        dve.reciprocal(KR[:, :, :], NR[:, q, :, 8:16]).then_inc(S["norm_scales"], 1)
                        dve.wait_ge(S["norm_scales"], 2 * i)
                        dve.tensor_tensor(XN[:, q, :, :], QKV[:, q, :, 3 * C:4 * C], _bcast(XRS[:, :], 2, C),
                                          ALU.mult).then_inc(S["xn_ready"], 1)
                        dve.tensor_tensor(KH[:, q, :, :].rearrange("p t (h d) -> p t h d", d=LIN_DIM),
                                          QKV[:, q, :, C:2 * C].rearrange("p t (h d) -> p t h d", d=LIN_DIM),
                                          _bcast(KR[:, :, :], 3, LIN_DIM), ALU.mult).then_inc(S["khat_ready"], 1)
                    if on(3):
                        dve.wait_ge(S["out_done"], i - 2)
                        dve.wait_ge(xr_loaded[q], _dmas(lap, r, 3, 2))
                        _above(dve.wait_ge, x1_stored[q], _dmas(lap, r, 5, 2))
                        _above(dve.wait_ge, S["a_psum"], TILES * (i - 4))
                        dve.scalar_tensor_tensor(out=X1[:, q, :], in0=po[0:C, :], scalar=w["out_bias"][:, 0:1],
                                                 in1=XR[:, q, :], op0=ALU.add, op1=ALU.add).then_inc(S["x1_ready"], 1)
                    if on(2):
                        dve.wait_ge(S["u_done"], i - 1)
                        dve.wait_ge(S["qv_ready"], i - 1)
                        _above(dve.wait_ge, S["ohat_ready"], i - 2)
                        dve.scalar_tensor_tensor(out=O[:, :, :].rearrange("p (a t) c -> p a (t c)", a=2),
                                                 in0=QV[:, r, :, :].rearrange("p (a t) c -> p a (t c)", a=2),
                                                 scalar=0.5, in1=halves(pf), op0=ALU.mult,
                                                 op1=ALU.add).then_inc(S["o_ready"], 1)
                    if on(0):
                        dve.wait_ge(S["gn_std"], i + 1)
                        dve.reciprocal(GV[:, 2:3], GV[:, 1:2]).then_inc(S["gn_scale"], 1)
                        dve.wait_ge(S["gn_scale"], i + 1)
                        _above(dve.wait_ge, S["u_done"], i - 1)
                        dve.tensor_scalar(XS[:, r, :], X[:, r, :], GS[:, 0:1], GV[:, 2:3], ALU.subtract,
                                          ALU.mult).then_inc(S["xs_ready"], 1)
                _pipeline(dve, body, BATCH, 7, 2)

            @block.gpsimd
            def _(pool):
                def body(i, r, lap, on):
                    q = (r + 1) % 2
                    if on(3):
                        pool.wait_ge(S["o_scale"], i - 2)
                        _above(pool.wait_ge, S["oht_psum"], i - 3)
                        pool.tensor_tensor(OH[:, :, :].rearrange("p t (h d) -> p (t h) d", d=LIN_DIM),
                                           O[:, :, :].rearrange("p t (h d) -> p (t h) d", d=LIN_DIM),
                                           _bcast(OI[:, :], 2, LIN_DIM), ALU.mult).then_inc(S["ohat_ready"], 1)
                    if on(5):
                        pool.wait_ge(S["a_scale"], i - 4)
                        _above(pool.wait_ge, rows_stored[q], _dmas(lap, r, 7, 2))
                        v = PK[:, q, :, PW:PW + HD].bitcast(FP32).rearrange("p (t j) d -> p t j d", j=HEADS)
                        pool.tensor_tensor(v, AQKV[:, q, :, 2 * C:3 * C].rearrange("p t (j d) -> p t j d", d=HD),
                                           _bcast(_bcast(ASC[:, q, :], 2, HEADS), 3, HD),
                                           ALU.mult).then_inc(S["v_ready"], 1)
                        pool.wait_ge(S["high_ready"], i - 4)
                        _above(pool.wait_ge, S["low_ready"], i - 5)
                        pool.tensor_tensor(AR1[:, :, :, :], AQK[:, :, :, :], part(q, 0),
                                           ALU.subtract).then_inc(S["rest_ready"], 1)
                    if on(1):
                        pool.wait_ge(S["norm_roots"], 2 * i)
                        pool.tensor_tensor(QV[:, q, :, :].rearrange("p t (h d) -> p t h d", d=LIN_DIM),
                                           QKV[:, q, :, 2 * C:3 * C].rearrange("p t (h d) -> p t h d", d=LIN_DIM),
                                           _bcast(NR[:, q, :, 0:8], 3, LIN_DIM), ALU.mult).then_inc(S["qv_ready"], 1)
                _pipeline(pool, body, BATCH, 7, 2)

            @block.scalar
            def _(act):
                def body(i, r, lap, on):
                    q = (r + 1) % 2
                    if on(3):
                        act.wait_ge(S["o_ready"], i - 2)
                        act.activation(OSQ[:, :, :], O[:, :, :], ACT.Square).then_inc(S["o_squares"], 1)
                    if on(2):
                        act.wait_ge(S["xnt_psum"], i - 1)
                        act.activation(XNT[:, :], pt[0:C, :], ACT.Copy).then_inc(S["xnt_ready"], 1)
                    if on(6):
                        act.wait_ge(S["rest_ready"], i - 5)
                        act.activation(part(r, 1), AR1[:, :, :, :], ACT.Copy).then_inc(S["mid_ready"], 1)
                    if on(5):
                        act.wait_ge(S["a_sums"], i - 4)
                        act.activation(AVR[:, :], AVS[:, :], ACT.Sqrt, bias=w["eps"][:, 0:1],
                                       scale=1.0 / C).then_inc(S["a_roots"], 1)
                    if on(3):
                        act.wait_ge(S["o_sums"], i - 2)
                        act.activation(OR[:, :], OS[:, :], ACT.Sqrt).then_inc(S["o_roots"], 1)
                    if on(1):
                        for t in range(TILES):
                            act.wait_ge(S["qkv_psum"], 8 * (i - 1) + t + 1)
                            act.activation(QKV[:, q, t, :], pq[:, (t % 2) * BANK:(t % 2) * BANK + 4 * C],
                                           ACT.Copy).then_inc(S["qkv_copied"], 1)
                        act.wait_ge(S["qkv_copied"], 8 * i)
                        act.activation(SQ[:, :, 2 * C:3 * C], QKV[:, q, :, 3 * C:4 * C],
                                       ACT.Square).then_inc(S["squares"], 1)
                        act.activation(SQ[:, :, 0:2 * C], QKV[:, q, :, 0:2 * C], ACT.Square).then_inc(S["squares"], 1)
                    if on(3):
                        act.wait_ge(S["oht_psum"], i - 2)
                        act.activation(OHT[:, :], pt[0:C, :], ACT.Copy).then_inc(S["oht_ready"], 1)
                    if on(5):
                        act.wait_ge(S["qk_ready"], i - 4)
                        _above(act.wait_ge, rows_stored[q], _dmas(lap, r, 7, 2))
                        act.activation(part(q, 0), AQK[:, :, :, :], ACT.Copy).then_inc(S["high_ready"], 1)
                    if on(0):
                        act.wait_ge(S["gn_var"], i + 1)
                        act.activation(GV[:, 1:2], GV[:, 0:1], ACT.Sqrt, bias=w["eps"][0:C, 0:1],
                                       scale=-1.0).then_inc(S["gn_std"], 1)
                    if on(1):
                        act.wait_ge(S["norm_sums"], i)
                        act.activation(VR[:, :], VS[:, :], ACT.Sqrt, bias=w["eps"][:, 0:1],
                                       scale=1.0 / C).then_inc(S["norm_roots"], 1)
                        act.activation(NR[:, q, :, :], NS[:, :, :], ACT.Sqrt).then_inc(S["norm_roots"], 1)
                    if on(2):
                        for k in range(CHUNKS):
                            for a in range(2):
                                act.wait_ge(S["fc1_psum"], 6 * (i - 2) + 2 * k + a + 1)
                                act.activation(HT[:, r, k, a * BANK:(a + 1) * BANK], pf[:, a * BANK:(a + 1) * BANK],
                                               ACT.Silu, bias=w["fc1_bias"][:, k:k + 1]).then_inc(S["hid_ready"], 1)
                    if on(4):
                        for t in range(TILES):
                            act.wait_ge(S["a_psum"], TILES * (i - 4) + t + 1)
                            if t == 0:
                                _above(act.wait_ge, S["v_ready"], i - 5)
                                _above(act.wait_ge, S["a_sums"], i - 4)
                            act.activation(AQKV[:, r, t, :], pq[:, (t % 2) * BANK:(t % 2) * BANK + 3 * C], ACT.Copy)
                            act.activation(ASQ[:, t, :], pq[:, (t % 2) * BANK + 3 * C:(t % 2) * BANK + 4 * C],
                                           ACT.Square).then_inc(S["a_copied"], 1)
                _pipeline(act, body, BATCH, 7, 2)

            @block.tensor
            def _(pe):
                def hidden(i, k):
                    for a in range(2):
                        if k:
                            pe.wait_ge(S["hid_ready"], 6 * (i - 2) + 2 * k + a - 1)
                        pe.matmul(pf[:, a * BANK:(a + 1) * BANK], w["fc1"][:, k * P:(k + 1) * P],
                                  XNT[:, a * BANK:(a + 1) * BANK], start=True, stop=True).then_inc(S["fc1_psum"], 1)

                def body(i, r, lap, on):
                    q = (r + 1) % 2
                    if on(2):
                        pe.wait_ge(S["xn_ready"], i - 1)
                        _above(pe.wait_ge, S["oht_ready"], i - 3)
                        for t in range(TILES):
                            mm = pe.transpose(pt[0:C, t * P:(t + 1) * P], XN[:, r, t, :], w["ident"][:, :])
                        mm.then_inc(S["xnt_psum"], 1)
                        pe.wait_ge(S["khat_ready"], i - 1)
                    if on(4):
                        pe.wait_ge(S["x1_ready"], i - 3)
                    if on(2):
                        for t in range(TILES):
                            mm = pe.matmul(KV, KH[:, r, t, :], QKV[:, r, t, 2 * C:3 * C], start=(t == 0),
                                           stop=(t == TILES - 1))
                        mm.then_inc(S["kv_done"], 1)
                        pe.wait_ge(S["a_ready"], i - 1)
                    if on(0):
                        pe.wait_ge(S["mv_ready"], i + 1)
                        pe.matmul(G_, w["group_mean"][:, :], MV[:, 0:3], start=True, stop=True).then_inc(S["g_done"], 1)
                    if on(1):
                        pe.wait_ge(S["xs_ready"], i)
                        for t in range(TILES):
                            if t >= 2:
                                pe.wait_ge(S["qkv_copied"], 8 * (i - 1) + t - 1)
                            elif on(5):
                                pe.wait_ge(S["a_copied"], 8 * (i - 5) + t + 7)
                            elif on(2):
                                pe.wait_ge(S["qkv_copied"], 8 * (i - 1) + t - 1)
                            pe.matmul(pq[:, (t % 2) * BANK:(t % 2) * BANK + 4 * C], XS[:, q, t * P:(t + 1) * P],
                                      w["w_lin"][:, :], start=True, stop=True).then_inc(S["qkv_psum"], 1)
                    if on(0):
                        pe.wait_ge(S["g_copied"], i + 1)
                    if on(2):
                        pe.matmul(M_, w["wq_t"][:, :], AM[:, :], start=True, stop=True).then_inc(S["m_done"], 1)
                    if on(3):
                        pe.wait_ge(S["ohat_ready"], i - 2)
                        if on(2):
                            pe.wait_ge(S["xnt_ready"], i - 1)
                        for t in range(TILES):
                            mm = pe.transpose(pt[0:C, t * P:(t + 1) * P], OH[:, t, :], w["ident"][:, :])
                        mm.then_inc(S["oht_psum"], 1)
                    if on(2):
                        pe.wait_ge(S["xnt_ready"], i - 1)
                        _above(pe.wait_ge, S["o_ready"], i - 2)
                        hidden(i, 0)
                    if on(3):
                        if on(2):
                            pe.wait_ge(S["m_ready"], i - 1)
                        for a in range(2):
                            half = slice(a * BANK, (a + 1) * BANK)
                            for k in range(CHUNKS):
                                pe.matmul(po[0:C, half], w["fc2"][:, k, :], HT[:, q, k, half], start=(k == 0),
                                          stop=False)
                            if a == 0:
                                pe.wait_ge(S["oht_ready"], i - 2)
                            mm = pe.matmul(po[0:C, half], w["proj"][:, :], OHT[:, half], start=False, stop=True)
                        mm.then_inc(S["out_done"], 1)
                    if on(2):
                        hidden(i, 1)
                        hidden(i, 2)
                    if on(4):
                        for t in range(TILES):
                            if t >= 2:
                                pe.wait_ge(S["a_copied"], 8 * (i - 4) + t - 1)
                            elif on(1):
                                pe.wait_ge(S["qkv_copied"], 8 * (i - 1) + t + 7)
                            elif on(5):
                                pe.wait_ge(S["a_copied"], 8 * (i - 5) + t + 7)
                            pe.matmul(pq[:, (t % 2) * BANK:(t % 2) * BANK + 4 * C], X1[:, r, t * P:(t + 1) * P],
                                      w["w_attn"][:, :], start=True, stop=True).then_inc(S["a_psum"], 1)
                    if on(2):
                        pe.wait_ge(S["m_ready"], i - 1)
                        pe.wait_ge(S["hid_ready"], 6 * (i - 1))
                        for t in range(TILES):
                            c0 = (t // 4) * BANK + (t % 4) * C
                            mm = pe.matmul(pf[:, c0:c0 + C], XS[:, r, t * P:(t + 1) * P], MM[:, :], start=True,
                                           stop=True)
                        mm.then_inc(S["u_done"], 1)
                _pipeline(pe, body, BATCH, 7, 2)


def _score_units():
    units = [[(0, 0, BANK, 0)], [(0, BANK, BANK, 0)]]
    for kb in range(1, TILES // 2 + 1):
        q0 = kb * P
        units.append([(kb, q0, BANK, 0)])
        rest = L - q0 - BANK
        if rest:
            other = TILES - kb
            units.append([(kb, q0 + BANK, rest, 0), (other, other * P, kb * P, rest)])
    return units


def causal_attention(nc, w, rows, att):
    scale = C ** -0.5
    UNITS = _score_units()
    NU = len(UNITS)
    QUNITS = [(qb, k0, min(BANK, (qb + 1) * P - k0)) for qb in range(TILES)
              for k0 in range(0, (qb + 1) * P, BANK)]
    NQ = len(QUNITS)
    SLOTS = 4
    RING = 3
    QBANKS, KBANKS = 3, 2
    LAG = 2
    VW = 32
    QG = P // VW
    with ExitStack() as ctx:
        def sb(name, shape, dt=FP32):
            return ctx.enter_context(nc.sbuf_tensor("at_" + name, shape, dt))

        def pb(name, shape, dt=FP32):
            return ctx.enter_context(nc.psum_tensor("at_ps_" + name, shape, dt))

        def sem(name):
            return ctx.enter_context(nc.semaphore("at_" + name))
        ST = sb("stacks", [P, SLOTS, TILES, PW + PACK + PW], U32)
        V = sb("v", [P, SLOTS, TILES, VW])
        QT = sb("q_t", [P, SLOTS, L], BF16)
        KT = sb("k_t", [P, SLOTS, L], BF16)
        MX = sb("unit_max", [P, TILES, 2])
        NM = sb("neg_max", [P, TILES])
        MP = sb("max_parts", [P, TILES, 32], BF16)
        PR = sb("probs", [P, RING, BANK])
        RC = sb("recip", [P, TILES])
        ONE = sb("one", [P, 1, 1])
        OT = sb("out_t", [P, 2 * P])
        AT = sb("att", [P, SLOTS, TILES, HD])
        pq = pb("queries", [P, QBANKS, BANK])
        pk = pb("keys", [P, KBANKS, BANK])
        pv = pb("values", [P, BANK])
        turned = pb("turn", [P, L], BF16)
        po = pb("out", [P, BANK])
        out_t = pv[:, 0:2 * P]
        out_ps = po[:, 0:2 * P].rearrange("p (t d) -> p t d", d=VW)
        loaded = [sem(f"loaded{i}") for i in range(SLOTS)]
        stored = [sem(f"stored{i}") for i in range(SLOTS)]
        names = ("set_up zeros_set one_set max_set parts_set spread q_turned k_turned q_ready k_ready q_scores unit_max head_max "
                 "max_high max_parts max_turned max_ready k_scores probs values out_copied out_turned recip out_ready").split()
        S = {n: sem(n) for n in names}
        src = rows.rearrange("b l (j n) -> (b l j) n", n=PACK).rearrange("(h t p) n -> h p t n", t=TILES, p=P)
        dst = att.rearrange("b l (j d) -> (b l j) d", d=HD).rearrange("(h t p) d -> h p t d", t=TILES, p=P)

        def k_stack(slot):
            return ST[:, slot, :, 0:2 * PW].bitcast(BF16)

        def q_stack(slot):
            return ST[:, slot, :, 2 * PW + HD:4 * PW + HD].bitcast(BF16)

        with nc.Block() as block:
            @block.sync
            def _(sp):
                def body(i, r, lap, on):
                    if on(0):
                        _above(sp.wait_ge, S["k_turned"], i - SLOTS + 1)
                        _above(sp.wait_ge, S["spread"], i - SLOTS + 1)
                        sp.dma_start(ST[:, r, :, PW:PW + PACK], src[i]).then_inc(loaded[r], 16)
                    if on(5):
                        q = (r - 5) % SLOTS
                        sp.wait_ge(S["out_ready"], i - 4)
                        sp.dma_start(dst[i - 5], AT[:, q, :, :]).then_inc(stored[q], 16)
                _pipeline(sp, body, NHEADS, 6, SLOTS)
                for r in range(SLOTS):
                    sp.wait_ge(stored[r], 16 * (NHEADS // SLOTS))

            @block.gpsimd
            def _(pool):
                pool.memset(V[:, :, :, HD:VW], 0.0).then_inc(S["zeros_set"], 1)
                pool.wait_ge(S["zeros_set"], 1)
                pool.memset(V[:, :, :, HD:HD + 1], 1.0)
                pool.memset(ONE[:, :, :], 1.0).then_inc(S["one_set"], 1)
                pool.wait_ge(S["one_set"], 1)

                def body(i, r, lap, on):
                    if on(0):
                        pool.wait_ge(loaded[r], _dmas(lap, r, 0, SLOTS))
                        _above(pool.wait_ge, S["values"], NU * (i - SLOTS + 1))
                        v = ST[:, r, :, 2 * PW:2 * PW + HD].bitcast(FP32)
                        pool.tensor_tensor(V[:, r, :, 0:HD], v, ONE[:, :, :].broadcast_to([P, TILES, HD]), ALU.mult)
                        ks, qs = k_stack(r), q_stack(r)
                        pool.tensor_copy(ks[:, :, 0:2 * HD], ks[:, :, 3 * HD:5 * HD])
                        pool.tensor_copy(ks[:, :, 2 * HD:3 * HD], ks[:, :, 3 * HD:4 * HD])
                        pool.tensor_copy(qs[:, :, 3 * HD:4 * HD], qs[:, :, HD:2 * HD])
                        high = qs[:, :, 0:HD].rearrange("p t (m d) -> p t m d", m=1)
                        pool.tensor_copy(qs[:, :, 4 * HD:6 * HD].rearrange("p t (m d) -> p t m d", m=2),
                                         high.broadcast_to([P, TILES, 2, HD])).then_inc(S["spread"], 1)
                _pipeline(pool, body, NHEADS, 5, SLOTS)

            @block.tensor
            def _(pe):
                pe.wait_ge(S["set_up"], 2)

                def turn_q(i, r):
                    pe.wait_ge(S["spread"], i + 1)
                    _above(pe.wait_ge, S["max_ready"], i - 1)
                    for t in range(TILES):
                        mm = pe.transpose(turned[0:STACK, t * P:(t + 1) * P], q_stack(r)[:, t, :], w["ident_bf"][:, :])
                    mm.then_inc(S["q_turned"], 1)

                def turn_k(i, r):
                    pe.wait_ge(S["q_ready"], i + 1)
                    for t in range(TILES):
                        mm = pe.transpose(turned[0:STACK, t * P:(t + 1) * P], k_stack(r)[:, t, :], w["ident_bf"][:, :])
                    mm.then_inc(S["k_turned"], 1)

                def turn_max(h, last):
                    pe.wait_ge(S["max_parts"], h + 1)
                    if not last:
                        pe.wait_ge(S["k_ready"], h + 2)
                    for t in range(TILES):
                        mm = pe.transpose(turned[96:128, t * P:(t + 1) * P], MP[:, t, :], w["ident_bf"][:, :])
                    mm.then_inc(S["max_turned"], 1)

                def turn_out(h):
                    pe.wait_ge(S["out_copied"], h + 1)
                    _above(pe.wait_ge, S["out_ready"], h)
                    for a in range(2):
                        mm = pe.transpose(po[:, a * P:(a + 1) * P], OT[:, a * P:(a + 1) * P], w["ident"][:, :])
                    mm.then_inc(S["out_turned"], 1)

                def query_scores(h, slot, u):
                    qb, k0, n = QUNITS[u]
                    if u == 0:
                        pe.wait_ge(S["q_ready"], h + 1)
                        pe.wait_ge(S["k_ready"], h + 1)
                    _above(pe.wait_ge, S["unit_max"], NQ * h + u - QBANKS + 1)
                    diag = k0 + n == (qb + 1) * P
                    mm = pe.matmul(pq[:, u % QBANKS, 0:n], QT[0:STACK, slot, qb * P:(qb + 1) * P],
                                   KT[0:STACK, slot, k0:k0 + n], start=True, stop=True)
                    if diag:
                        mm = pe.matmul(pq[:, u % QBANKS, n - P:n], w["ident_bf"][:, :], w["mask_queries"][:, :],
                                       start=False, stop=True, skip_group_check=True)
                    mm.then_inc(S["q_scores"], 1)

                def key_scores(h, slot, u):
                    if u == 0:
                        pe.wait_ge(S["max_ready"], h + 1)
                    _above(pe.wait_ge, S["probs"], NU * h + u - KBANKS + 1)
                    for kb, q0, n, c0 in UNITS[u]:
                        diag = q0 == kb * P
                        mm = pe.matmul(pk[:, (slot * NU + u) % KBANKS, c0:c0 + n], KT[:, slot, kb * P:(kb + 1) * P],
                                       QT[:, slot, q0:q0 + n], start=True, stop=True)
                        if diag:
                            mm = pe.matmul(pk[:, (slot * NU + u) % KBANKS, c0:c0 + P], w["ident_bf"][:, :], w["mask_keys"][:, :],
                                           start=False, stop=True, skip_group_check=True)
                    mm.then_inc(S["k_scores"], 1)

                def values(h, slot, u):
                    pe.wait_ge(S["probs"], NU * h + u + 1)
                    if u == 0:
                        _above(pe.wait_ge, S["out_copied"], h)
                    for kb, q0, n, c0 in UNITS[u]:
                        for b in range(n // P):
                            qb = q0 // P + b
                            row, col = VW * (qb % QG), P * (qb // QG)
                            mm = pe.matmul(out_t[row:row + VW, col:col + P], V[:, slot, kb, :],
                                           PR[:, u % RING, c0 + b * P:c0 + (b + 1) * P],
                                           start=(u == 0 and b < QG), stop=True, skip_group_check=True)
                    mm.then_inc(S["values"], 1)

                def body(i, r, lap, on):
                    nq = 0
                    for u in range(NU):
                        if u == 1 and on(3):
                            turn_max(i - 3, not on(2))
                        if on(2):
                            want = -(-NQ * (u + 1) // NU)
                            while nq < want:
                                query_scores(i - 2, (r - 2) % SLOTS, nq)
                                nq += 1
                        back = 3 if u >= LAG else 4
                        if on(back):
                            key_scores(i - back, (r - back) % SLOTS, (u - LAG) % NU)
                        back = 3 if u >= 2 * LAG else 4
                        if on(back):
                            values(i - back, (r - back) % SLOTS, (u - 2 * LAG) % NU)
                        if u == 3 and on(1):
                            turn_q(i - 1, (r - 1) % SLOTS)
                        if u == 5 and on(4):
                            turn_out(i - 4)
                        if u == 6 and on(1):
                            turn_k(i - 1, (r - 1) % SLOTS)
                _pipeline(pe, body, NHEADS, 5, SLOTS)

            @block.scalar
            def _(act):
                def body(i, r, lap, on):
                    q = (r - 1) % SLOTS
                    for u in range(NU):
                        back = 3 if u >= LAG else 4
                        if on(back):
                            v = (u - LAG) % NU
                            act.wait_ge(S["k_scores"], NU * (i - back) + v + 1)
                            _above(act.wait_ge, S["values"], NU * (i - back) + v - RING + 1)
                            act.activation(PR[:, v % RING, :], pk[:, ((r - back) % SLOTS * NU + v) % KBANKS, :], ACT.Exp,
                                           scale=scale).then_inc(S["probs"], 1)
                        if u == 3 and on(1):
                            act.wait_ge(S["q_turned"], i)
                            act.activation(QT[0:STACK, q, :], turned[0:STACK, :], ACT.Copy).then_inc(S["q_ready"], 1)
                        if u == 6 and on(1):
                            act.wait_ge(S["k_turned"], i)
                            act.activation(KT[0:STACK, q, :], turned[0:STACK, :], ACT.Copy).then_inc(S["k_ready"], 1)
                _pipeline(act, body, NHEADS, 5, SLOTS)

            @block.vector
            def _(dve):
                dve.memset(MX[:, :, :], -3.0e38).then_inc(S["max_set"], 1)
                dve.memset(MP[:, :, :], 0.0).then_inc(S["parts_set"], 1)
                dve.memset(KT[96:128, :, :], 0.0).then_inc(S["set_up"], 1)
                dve.wait_ge(S["set_up"], 1)
                dve.memset(KT[96:98, :, :], 1.0).then_inc(S["set_up"], 1)
                dve.wait_ge(S["max_set"], 1)
                dve.wait_ge(S["parts_set"], 1)

                def body(i, r, lap, on):
                    for u, (qb, k0, n) in enumerate(QUNITS):
                        if on(2):
                            dve.wait_ge(S["q_scores"], NQ * (i - 2) + u + 1)
                            dve.tensor_reduce(MX[:, qb, k0 // BANK:k0 // BANK + 1], pq[:, u % QBANKS, 0:n], AX.X,
                                              ALU.max).then_inc(S["unit_max"], 1)
                        if u == 1 and on(3):
                            dve.wait_ge(S["max_turned"], i - 2)
                            dve.tensor_copy(QT[96:128, (r - 3) % SLOTS, :], turned[96:128, :]
                                            ).then_inc(S["max_ready"], 1)
                        if u == 6 and on(4):
                            dve.wait_ge(S["values"], NU * (i - 3))
                            dve.tensor_copy(OT[:, :], out_t).then_inc(S["out_copied"], 1)
                        if u == 9 and on(4):
                            dve.wait_ge(S["out_turned"], i - 3)
                            dve.reciprocal(RC[:, :], out_ps[:, :, HD]).then_inc(S["recip"], 1)
                            dve.wait_ge(S["recip"], i - 3)
                            _above(dve.wait_ge, stored[r], _dmas(lap, r, 8, SLOTS))
                            dve.tensor_tensor(AT[:, r, :, :], out_ps[:, :, 0:HD], _bcast(RC[:, :], 2, HD),
                                              ALU.mult).then_inc(S["out_ready"], 1)
                    if on(2):
                        dve.wait_ge(S["unit_max"], NQ * (i - 1))
                        dve.tensor_reduce(NM[:, :], MX[:, :, :], AX.X, ALU.max, negate=True).then_inc(S["head_max"], 1)
                        dve.wait_ge(S["head_max"], i - 1)
                        _above(dve.wait_ge, S["max_turned"], i - 2)
                        dve.tensor_copy(MP[:, :, 0], NM[:, :]).then_inc(S["max_high"], 1)
                        dve.wait_ge(S["max_high"], i - 1)
                        dve.tensor_tensor(MP[:, :, 1], NM[:, :], MP[:, :, 0],
                                          ALU.subtract).then_inc(S["max_parts"], 1)
                _pipeline(dve, body, NHEADS, 5, SLOTS)


def project_and_ffn(nc, w, att, x1, y_out):
    LIMIT = QB - QEPS
    REST = BATCH - GROUPS * GB
    with ExitStack() as ctx:
        def sb(name, shape, dt=FP32):
            return ctx.enter_context(nc.sbuf_tensor("ff_" + name, shape, dt))

        def sem(name):
            return ctx.enter_context(nc.semaphore("ff_" + name))
        AR = sb("att_rows", [P, 2, TILES, C])
        X1 = sb("x1", [C, 2, L])
        AT = sb("att_t", [C, L])
        X2 = sb("x2", [C, GB, L])
        SQ = sb("squares", [P, TILES, C])
        VS = sb("var_sums", [P, TILES])
        VR = sb("var_roots", [P, TILES])
        SCALE = sb("scale", [P, TILES])
        XN = sb("xn", [P, 2, TILES, C])
        XNT = sb("xn_t", [C + 1, L])
        Y1 = sb("hidden", [P, GB, CHUNKS, L])
        Y2 = sb("ffn", [C, GB, L])
        OUT = sb("out", [C, 2, L])
        G1, G2 = sb("max1", [P, GB]), sb("max2", [C, GB])
        ROW = sb("row_of_ones", [1, P])
        M1, M2 = sb("group_max1", [P, 4]), sb("group_max2", [C, 4])
        pt, py, pc, pf = (ctx.enter_context(nc.psum_tensor("ff_ps_" + n, [P, 2 * BANK], FP32))
                          for n in ("turn", "out", "centred", "hidden"))
        xc = pc[:, :].rearrange("p (a n) -> p a n", a=2)[:, :, 0:4 * C]
        a_loaded = [sem(f"att_loaded{i}") for i in range(2)]
        x_loaded = [sem(f"x1_loaded{i}") for i in range(2)]
        stored = [sem(f"stored{i}") for i in range(2)]
        names = ("ones_set att_turned att_copied y_done x2_ready xc_done squares var_sums var_roots scale xn_ready "
                 "xn_turned xnt_ready y1_psum y1_copied y1_max max1 all_max1 scale1 gelu h_ready y2_psum y2_ready "
                 "y2_max max2 all_max2 scale2 limited out_ready").split()
        S = {n: sem(n) for n in names}

        def groups(eng, body):
            with eng.Fori(0, GROUPS) as g:
                body(g, lambda j: g * GB + j, GB)
            body(GROUPS, lambda j: GROUPS * GB + j, REST)

        with nc.Block() as block:
            @block.sync
            def _(sp):
                def load(j, entry):
                    sp.dma_start(AR[:, j % 2, :, :], att[entry].rearrange("(t p) c -> p t c", p=P)
                                 ).then_inc(a_loaded[j % 2], 16)
                    sp.dma_start(X1[:, j % 2, :], x1[entry]).then_inc(x_loaded[j % 2], 16)

                load(0, 0)
                load(1, 1)
                with sp.Fori(0, GROUPS) as g:
                    n = g * GB
                    for j in range(2, GB):
                        sp.wait_ge(S["att_turned"], n + (j - 1))
                        sp.wait_ge(S["x2_ready"], n + (j - 1))
                        load(j, n + j)
                    for j in range(GB):
                        sp.wait_ge(S["out_ready"], n + (j + 1))
                        sp.dma_start(y_out[n + j], OUT[:, j % 2, :]).then_inc(stored[j % 2], 16)
                    for j in range(2):
                        sp.wait_ge(stored[j], (g + 1) * (16 * GB // 2))
                        load(j, n + (GB + j))
                for j in range(REST):
                    sp.wait_ge(S["x2_ready"], GROUPS * GB + j + 1)
                    sp.dma_start(y_out[GROUPS * GB + j], X2[:, j, :]).then_inc(stored[j % 2], 16)
                for r in range(2):
                    sp.wait_ge(stored[r], 16 * (BATCH // 2))

            @block.tensor
            def _(pe):
                pe.wait_ge(S["ones_set"], 2)

                def body(g, n, size):
                    full = size == GB

                    def hidden(j, k):
                        for a in range(2):
                            if k or j:
                                pe.wait_ge(S["y1_copied"], 6 * n(j) + 2 * k + a - 1)
                            pe.matmul(pf[:, a * BANK:(a + 1) * BANK], w["w1"][:, k * P:(k + 1) * P],
                                      XNT[:, a * BANK:(a + 1) * BANK], start=True, stop=True
                                      ).then_inc(S["y1_psum"], 1)
                    def spread_max(M, name, all_name):
                        parts = M.shape[0]
                        pe.wait_ge(S[name], 2 * g + 1)
                        pe.transpose(pc[0:1, 0:parts], M[:, 0:1], w["ident"][0:parts, 0:parts]
                                     ).then_inc(S[all_name], 1)
                        pe.wait_ge(S[name], 2 * g + 2)
                        pe.matmul(pc[0:parts, BANK:BANK + 1], ROW[:, 0:parts], M[0:1, 1:2], start=True, stop=True
                                  ).then_inc(S[all_name], 1)

                    for j in range(size + 2):
                        if full and j >= 2:
                            pe.wait_ge(S["xn_ready"], n(j - 1))
                            for t in range(TILES):
                                mm = pe.transpose(pt[0:C, t * P:(t + 1) * P], XN[:, j % 2, t, :], w["ident"][:, :])
                            mm.then_inc(S["xn_turned"], 1)
                        if full and 1 <= j <= size:
                            pe.wait_ge(S["x2_ready"], n(j))
                            for t in range(TILES):
                                c0 = (t // 4) * BANK + (t % 4) * C
                                mm = pe.matmul(pc[:, c0:c0 + C], X2[:, j - 1, t * P:(t + 1) * P], w["centre"][:, :],
                                               start=True, stop=True)
                            mm.then_inc(S["xc_done"], 1)
                        if j < size:
                            pe.wait_ge(a_loaded[j % 2], (g * (GB // 2) + (j // 2 + 1)) * 16)
                            if full and j >= 2:
                                pe.wait_ge(S["xnt_ready"], n(j - 1))
                            for t in range(TILES):
                                mm = pe.transpose(pt[0:C, t * P:(t + 1) * P], AR[:, j % 2, t, :], w["ident"][:, :])
                            mm.then_inc(S["att_turned"], 1)
                        if full and j >= 2:
                            pe.wait_ge(S["xnt_ready"], n(j - 1))
                            hidden(j - 2, 0)
                        if j < size:
                            pe.wait_ge(S["att_copied"], n(j + 1))
                            if not full or j:
                                pe.wait_ge(S["x2_ready"], n(j))
                            for a in range(2):
                                half = slice(a * BANK, (a + 1) * BANK)
                                mm = pe.matmul(py[0:C, half], w["wp"][:, :], AT[:, half], start=True, stop=True)
                            mm.then_inc(S["y_done"], 1)
                        if full and j >= 2:
                            hidden(j - 2, 1)
                            hidden(j - 2, 2)
                    if not full:
                        return
                    spread_max(M1, "max1", "all_max1")
                    for j in range(size):
                        pe.wait_ge(S["h_ready"], 3 * n(j + 1))
                        if j:
                            pe.wait_ge(S["y2_ready"], n(j))
                        for a in range(2):
                            half = slice(a * BANK, (a + 1) * BANK)
                            for k in range(CHUNKS):
                                mm = pe.matmul(py[0:C, half], w["w2"][:, k, :], Y1[:, j, k, half], start=(k == 0),
                                               stop=(k == CHUNKS - 1))
                        mm.then_inc(S["y2_psum"], 1)
                    spread_max(M2, "max2", "all_max2")
                groups(pe, body)

            @block.scalar
            def _(act):
                def body(g, n, size):
                    full = size == GB
                    for j in range(size + 2):
                        if full and j >= 2:
                            act.wait_ge(S["xn_turned"], n(j - 1))
                            act.activation(XNT[0:C, :], pt[0:C, :], ACT.Copy).then_inc(S["xnt_ready"], 1)
                        if j < size:
                            act.wait_ge(S["att_turned"], n(j + 1))
                            act.activation(AT[:, :], pt[0:C, :], ACT.Copy).then_inc(S["att_copied"], 1)
                        if full and 1 <= j <= size:
                            act.wait_ge(S["xc_done"], n(j))
                            act.activation(SQ[:, :, :].rearrange("p (a t) c -> p a (t c)", a=2), xc,
                                           ACT.Square).then_inc(S["squares"], 1)
                            act.wait_ge(S["var_sums"], n(j))
                            act.activation(VR[:, :], VS[:, :], ACT.Sqrt, bias=w["eps"][:, 0:1],
                                           scale=1.0 / C).then_inc(S["var_roots"], 1)
                        if full and j >= 2:
                            for k in range(CHUNKS):
                                for a in range(2):
                                    act.wait_ge(S["y1_psum"], 6 * n(j - 2) + 2 * k + a + 1)
                                    act.activation(Y1[:, j - 2, k, a * BANK:(a + 1) * BANK],
                                                   pf[:, a * BANK:(a + 1) * BANK], ACT.Copy
                                                   ).then_inc(S["y1_copied"], 1)
                    if full:
                        act.wait_ge(S["scale1"], 2 * g + 2)
                        for j in range(size + 1):
                            if j < size:
                                for k in range(CHUNKS):
                                    act.activation(Y1[:, j, k, :], Y1[:, j, k, :], ACT.Gelu,
                                                   scale=M1[:, 3:4]).then_inc(S["gelu"], 1)
                            if j:
                                act.wait_ge(S["y2_psum"], n(j))
                                act.activation(Y2[:, j - 1, :], py[0:C, :], ACT.Identity, bias=w["b2"][:, 0:1]
                                               ).then_inc(S["y2_ready"], 1)
                groups(act, body)

            @block.vector
            def _(dve):
                dve.memset(ROW[:, :], 1.0).then_inc(S["ones_set"], 1)
                dve.memset(XNT[C:C + 1, :], 1.0).then_inc(S["ones_set"], 1)

                def group_scale(g, entry, peak, maxima, M, name, all_name, scale_name):
                    dve.wait_ge(S[peak], entry)
                    dve.tensor_reduce(M[:, 0:1], maxima[:, :], AX.X, ALU.max).then_inc(S[name], 1)
                    dve.wait_ge(S[all_name], 2 * g + 1)
                    dve.tensor_reduce(M[0:1, 1:2], pc[0:1, 0:M.shape[0]], AX.X, ALU.max).then_inc(S[name], 1)
                    dve.wait_ge(S[all_name], 2 * g + 2)
                    dve.tensor_scalar(M[:, 2:3], pc[0:M.shape[0], BANK:BANK + 1], QEPS, 1.0 / QB, ALU.add, ALU.mult
                                      ).then_inc(S[scale_name], 1)
                    dve.wait_ge(S[scale_name], 2 * g + 1)
                    dve.reciprocal(M[:, 3:4], M[:, 2:3]).then_inc(S[scale_name], 1)

                def body(g, n, size):
                    full = size == GB

                    def peak1(j):
                        dve.wait_ge(S["y1_copied"], 6 * n(j + 1))
                        dve.tensor_reduce(G1[:, j:j + 1], Y1[:, j, :, :], AX.XY, ALU.max,
                                          apply_absolute_value=True).then_inc(S["y1_max"], 1)
                    for j in range(size + 2):
                        if full and 1 <= j <= size:
                            q = (j - 1) % 2
                            dve.wait_ge(S["squares"], n(j))
                            dve.tensor_reduce(VS[:, :], SQ[:, :, :], AX.X, ALU.add).then_inc(S["var_sums"], 1)
                            dve.wait_ge(S["var_roots"], n(j))
                            dve.reciprocal(SCALE[:, :], VR[:, :]).then_inc(S["scale"], 1)
                            dve.wait_ge(S["scale"], n(j))
                            for a in range(2):
                                ins = dve.tensor_tensor(XN[:, q, 4 * a:4 * a + 4, :],
                                                        xc[:, a, :].rearrange("p (t c) -> p t c", c=C),
                                                        _bcast(SCALE[:, 4 * a:4 * a + 4], 2, C), ALU.mult)
                            ins.then_inc(S["xn_ready"], 1)
                        if j < size:
                            dve.wait_ge(S["y_done"], n(j + 1))
                            dve.wait_ge(x_loaded[j % 2], (g * (GB // 2) + (j // 2 + 1)) * 16)
                            dve.scalar_tensor_tensor(out=X2[:, j, :], in0=py[0:C, :], scalar=w["bp"][:, 0:1],
                                                     in1=X1[:, j % 2, :], op0=ALU.add, op1=ALU.add
                                                     ).then_inc(S["x2_ready"], 1)
                        if full and j >= 2:
                            peak1(j - 2)
                    if not full:
                        return
                    group_scale(g, n(size), "y1_max", G1, M1, "max1", "all_max1", "scale1")
                    for j in range(size + 1):
                        if j < size:
                            for k in range(CHUNKS):
                                dve.wait_ge(S["gelu"], 3 * n(j) + k + 1)
                                dve.tensor_scalar(Y1[:, j, k, :], Y1[:, j, k, :], LIMIT, None, ALU.min
                                                  ).then_inc(S["h_ready"], 1)
                        if j:
                            dve.wait_ge(S["y2_ready"], n(j))
                            dve.tensor_reduce(G2[:, j - 1:j], Y2[:, j - 1, :], AX.X, ALU.max,
                                              apply_absolute_value=True).then_inc(S["y2_max"], 1)
                    group_scale(g, n(size), "y2_max", G2, M2, "max2", "all_max2", "scale2")
                    dve.wait_ge(S["scale2"], 2 * g + 2)
                    for j in range(size):
                        dve.tensor_scalar(Y2[:, j, :], Y2[:, j, :], M2[:, 3:4], LIMIT, ALU.mult, ALU.min
                                          ).then_inc(S["limited"], 1)
                        dve.wait_ge(S["limited"], n(j + 1))
                        if j >= 2:
                            dve.wait_ge(stored[j % 2], (g * (GB // 2) + j // 2) * 16)
                        dve.scalar_tensor_tensor(out=OUT[:, j % 2, :], in0=Y2[:, j, :], scalar=-LIMIT,
                                                 in1=X2[:, j, :], op0=ALU.max, op1=ALU.add
                                                 ).then_inc(S["out_ready"], 1)
                groups(dve, body)


def build(nc, A, out):
    x1 = nc.dram_tensor("x_after_conv", [BATCH, C, L], FP32, kind="Internal").ap()
    rows = nc.dram_tensor("qkv_rows", [BATCH, L, HEADS * PACK], U32, kind="Internal").ap()
    att = nc.dram_tensor("attention_rows", [BATCH, L, C], FP32, kind="Internal").ap()
    x_in = A["x"].rearrange("b c h w -> b c (h w)")
    y_out = out.rearrange("b c h w -> b c (h w)")
    with ExitStack() as ctx:
        w = _constants(nc, ctx)
        prepare(nc, w, A)
        conv_block(nc, w, x_in, x1, rows)
        causal_attention(nc, w, rows, att)
        project_and_ffn(nc, w, att, x1, y_out)


_INS = ['x', 'L0_conv_qkv_w', 'L0_conv_proj_w', 'L0_conv_proj_b', 'L0_conv_ln_g', 'L0_conv_ln_b',
        'L0_conv_fc1_w', 'L0_conv_fc1_b', 'L0_conv_fc2_w', 'L0_conv_fc2_b', 'L1_attn_Wk', 'L1_attn_Wq',
        'L1_attn_Wv', 'L1_attn_Wp', 'L1_attn_bp', 'L1_ffn_W1', 'L1_ffn_b1', 'L1_ffn_W2', 'L1_ffn_b2']


def kernel(**inputs):
    import numpy as _np
    import concourse.bacc as _bacc
    from concourse import mybir as _mybir
    from concourse.bass_utils import run_bass_kernel_spmd as _run

    nc = _bacc.Bacc("TRN2", target_bir_lowering=False, num_devices=1)
    arrays, args = {}, {}
    for name in _INS:
        a = _np.ascontiguousarray(inputs[name])
        arrays[f"in_{name}_dram"] = a
        args[name] = nc.dram_tensor(f"in_{name}_dram", a.shape, _mybir.dt.from_np(a.dtype), kind="ExternalInput").ap()
    out = nc.dram_tensor("out_0_dram", (BATCH, C, SIDE, SIDE), _mybir.dt.from_np(_np.dtype("float32")),
                         kind="ExternalOutput").ap()
    build(nc, args, out)
    r = _run(nc, [arrays], core_ids=[0])
    return r.results[0]["out_0_dram"]
```

```python
import concourse.bass as bass
from concourse import mybir
from contextlib import ExitStack
import math

FP32 = mybir.dt.float32
BF16 = mybir.dt.bfloat16
U32 = mybir.dt.uint32
ALU = mybir.AluOpType
ACT = mybir.ActivationFunctionType
AX = mybir.AxisListType

BATCH, C, SIDE = 32, 96, 32
L = SIDE * SIDE
P = 128
TILES = L // P
BANK = 512
HIDDEN = 4 * C
CHUNKS = HIDDEN // P
GN_CH = C // 32
LIN_HEADS, LIN_DIM = 8, C // 8
HEADS, HD = 6, C // 6
ROWS = L * C // HD
NHEADS = BATCH * HEADS
PW = 3 * HD // 2
PACK = PW + HD + PW
STACK = 6 * HD
GROUPS = 5
GB = BATCH // GROUPS
QB, QEPS = 128.0, 1e-5
NEG = -1.0e30


def _bcast(ap, axis, n):
    ap = ap.unsqueeze(axis)
    shape = list(ap.shape)
    shape[axis] = n
    return ap.broadcast_to(shape)


def _above(sem_wait, sem, value):
    if not isinstance(value, int) or value > 0:
        sem_wait(sem, value)


def _constants(nc, ctx):
    def sb(name, shape, dt=FP32):
        return ctx.enter_context(nc.sbuf_tensor(name, shape, dt))
    w = {}
    w["ident"] = sb("ident", [P, P])
    w["ident_bf"] = sb("ident_bf", [P, P], BF16)
    w["mask_keys"] = sb("mask_keys", [P, P], BF16)
    w["mask_queries"] = sb("mask_queries", [P, P], BF16)
    w["centre"] = sb("centre", [C, C])
    w["group_mean"] = sb("group_mean", [C, C])
    w["head_blocks"] = sb("head_blocks", [C, C])
    w["w_lin"] = sb("w_lin", [C, 4 * C])
    w["wq_t"] = sb("wq_t", [C, C])
    w["fc1"] = sb("fc1", [C, HIDDEN])
    w["fc1_bias"] = sb("fc1_bias", [P, CHUNKS])
    w["fc2"] = sb("fc2", [P, CHUNKS, C])
    w["proj"] = sb("proj", [C, C])
    w["out_bias"] = sb("out_bias", [C, 1])
    w["w_attn"] = sb("w_attn", [C, 4 * C])
    w["wp"] = sb("wp", [C, C])
    w["bp"] = sb("bp", [C, 1])
    w["w1"] = sb("w1", [C + 1, HIDDEN])
    w["w2"] = sb("w2", [P, CHUNKS, C])
    w["b2"] = sb("b2", [C, 1])
    w["eps"] = sb("eps", [P, 1])
    return w


def prepare(nc, w, A):
    ctx = ExitStack()
    with ctx:
        def sb(name, shape, dt=FP32):
            return ctx.enter_context(nc.sbuf_tensor(name, shape, dt))

        def sem(name):
            return ctx.enter_context(nc.semaphore(name))
        g_fc1 = sb("g_fc1", [C, HIDDEN])
        fc1_raw = sb("fc1_raw", [C, HIDDEN])
        fc2_raw = sb("fc2_raw", [P, CHUNKS, C])
        fc2_t = sb("fc2_t", [C, HIDDEN])
        attn_raw = sb("attn_raw", [C, 4 * C])
        qkv3 = sb("qkv3", [C, 3, C])
        w1_raw = sb("w1_raw", [P, CHUNKS, C])
        w1_t = sb("w1_t", [C, HIDDEN])
        w2_raw = sb("w2_raw", [C, HIDDEN])
        w2_t = sb("w2_t", [P, CHUNKS, C])
        lng = sb("lng", [C, 1])
        lnb = sb("lnb", [C, 1])
        fc1b = sb("fc1b", [P, CHUNKS])
        fc2b = sb("fc2b", [C, 1])
        projb = sb("projb", [C, 1])
        ones1 = sb("ones1", [C, P])
        ones2 = sb("ones2", [P, P])
        s1 = sb("s1", [C, GROUPS])
        s2 = sb("s2", [P, CHUNKS, GROUPS])
        sp2 = sb("sp2", [P, GROUPS])
        m1 = sb("m1", [C, GROUPS])
        m2 = sb("m2", [P, GROUPS])
        z1 = sb("z1", [C, HIDDEN])
        z2 = sb("z2", [P, CHUNKS, C])
        n1 = sb("n1", [C, HIDDEN])
        n2 = sb("n2", [P, CHUNKS, C])
        bank = [ctx.enter_context(nc.psum_tensor(f"prep{i}", [P, BANK], FP32)) for i in range(8)]
        loaded, made = sem("prep_loaded"), sem("prep_made")
        products, step = sem("prep_products"), sem("prep_step")
        gs1, gs2 = HIDDEN // GROUPS, C // GROUPS
        loads = [
            (w["w_lin"][:, 0:3 * C], A["L0_conv_qkv_w"]),
            (w["proj"][:, :], A["L0_conv_proj_w"]),
            (fc1_raw[:, :], A["L0_conv_fc1_w"]),
            (fc2_raw[:, :, :], A["L0_conv_fc2_w"].rearrange("(k p) c -> p k c", p=P)),
            (qkv3[:, 0, :], A["L1_attn_Wq"]),
            (qkv3[:, 1, :], A["L1_attn_Wk"]),
            (qkv3[:, 2, :], A["L1_attn_Wv"]),
            (w["wp"][:, :], A["L1_attn_Wp"]),
            (w1_raw[:, :, :], A["L1_ffn_W1"].rearrange("(k p) c -> p k c", p=P)),
            (w2_raw[:, :], A["L1_ffn_W2"]),
            (w["w1"][C:C + 1, :], A["L1_ffn_b1"].rearrange("(a n) -> a n", a=1)),
            (lng[:, :], A["L0_conv_ln_g"].rearrange("(n a) -> n a", a=1)),
            (lnb[:, :], A["L0_conv_ln_b"].rearrange("(n a) -> n a", a=1)),
            (fc1b[:, :], A["L0_conv_fc1_b"].rearrange("(k p) -> p k", p=P)),
            (fc2b[:, :], A["L0_conv_fc2_b"].rearrange("(n a) -> n a", a=1)),
            (projb[:, :], A["L0_conv_proj_b"].rearrange("(n a) -> n a", a=1)),
            (w["bp"][:, :], A["L1_attn_bp"].rearrange("(n a) -> n a", a=1)),
            (w["b2"][:, :], A["L1_ffn_b2"].rearrange("(n a) -> n a", a=1)),
        ]
        NLOADS = len(loads)
        MADE = 16
        with nc.Block() as block:
            @block.sync
            def _(sp):
                with nc.allow_non_contiguous_dma(reason="bias columns, once"):
                    for dst, src in loads:
                        sp.dma_start(dst, src).then_inc(loaded, 16)
                sp.wait_ge(loaded, 16 * NLOADS)

            @block.gpsimd
            def _(pool):
                def link(ins, n):
                    ins.then_inc(made, 1)
                    pool.wait_ge(made, n)
                link(pool.memset(w["ident"][:, :], 0.0), 1)
                link(pool.affine_select(out=w["ident"][:, :], in_=w["ident"][:, :], compare_op=ALU.not_equal,
                                        fill=1.0, base=0, pattern=[[-1, P]], channel_multiplier=1), 2)
                link(pool.memset(w["ident_bf"][:, :], 0.0), 3)
                link(pool.affine_select(out=w["ident_bf"][:, :], in_=w["ident_bf"][:, :], compare_op=ALU.not_equal,
                                        fill=1.0, base=0, pattern=[[-1, P]], channel_multiplier=1), 4)
                link(pool.memset(w["mask_keys"][:, :], 0.0), 5)
                link(pool.affine_select(out=w["mask_keys"][:, :], in_=w["mask_keys"][:, :], compare_op=ALU.is_ge,
                                        fill=NEG, base=0, pattern=[[1, P]], channel_multiplier=-1), 6)
                link(pool.memset(w["mask_queries"][:, :], 0.0), 7)
                link(pool.affine_select(out=w["mask_queries"][:, :], in_=w["mask_queries"][:, :],
                                        compare_op=ALU.is_ge, fill=NEG, base=0, pattern=[[-1, P]],
                                        channel_multiplier=1), 8)
                n = 8
                for name, size, value in (("group_mean", GN_CH, 1.0 / GN_CH),
                                          ("head_blocks", LIN_DIM, 1.0 / math.pi)):
                    v = w[name][:, :].rearrange("p (g d) -> p g d", d=size)
                    link(pool.memset(w[name][:, :], value), n + 1)
                    link(pool.affine_select(out=v, in_=v, compare_op=ALU.is_ge, fill=0.0, base=0,
                                            pattern=[[-size, C // size], [0, size]], channel_multiplier=1), n + 2)
                    link(pool.affine_select(out=v, in_=v, compare_op=ALU.is_ge, fill=0.0, base=size - 1,
                                            pattern=[[size, C // size], [0, size]], channel_multiplier=-1), n + 3)
                    n += 3
                link(pool.memset(w["centre"][:, :], -1.0 / C), n + 1)
                link(pool.affine_select(out=w["centre"][:, :], in_=w["centre"][:, :], compare_op=ALU.not_equal,
                                        fill=1.0 - 1.0 / C, base=0, pattern=[[-1, C]], channel_multiplier=1), n + 2)
                assert n + 2 == MADE



            @block.vector
            def _(dve):
                cnt = [0]

                def link(ins):
                    cnt[0] += 1
                    ins.then_inc(step, 1)
                    dve.wait_ge(step, cnt[0])
                link(dve.memset(ones1[:, :], 1.0 / (gs1 * C)))
                link(dve.memset(ones2[:, :], 1.0 / (gs2 * HIDDEN)))
                link(dve.memset(w["eps"][:, :], 1e-5))
                dve.wait_ge(loaded, 16 * NLOADS)
                dve.wait_ge(made, MADE)
                link(dve.tensor_copy(w["w_lin"][:, 3 * C:4 * C], w["centre"][:, :]))
                link(dve.tensor_scalar(g_fc1[:, :], fc1_raw[:, :], lng[:, 0:1], None, ALU.mult))
                pairs = attn_raw[:, 0:2 * C].rearrange("p (j s d) -> p j s d", s=2, d=HD)
                link(dve.tensor_copy(pairs[:, :, 0, :], qkv3[:, 1, :].rearrange("p (j d) -> p j d", d=HD)))
                link(dve.tensor_copy(pairs[:, :, 1, :], qkv3[:, 0, :].rearrange("p (j d) -> p j d", d=HD)))
                link(dve.tensor_copy(attn_raw[:, 2 * C:3 * C], qkv3[:, 2, :]))
                link(dve.tensor_copy(attn_raw[:, 3 * C:4 * C], w["ident"][0:C, 0:C]))
                dve.wait_ge(products, 1)
                link(dve.tensor_copy(w["fc1"][:, :], bank[0][0:C, 0:HIDDEN]))
                link(dve.tensor_tensor(w["fc1_bias"][:, :], bank[1][:, 0:CHUNKS], fc1b[:, :], ALU.add))
                link(dve.tensor_copy(w["wq_t"][:, :], bank[2][0:C, 0:C]))
                link(dve.tensor_copy(fc2_t[:, :], bank[3][0:C, 0:HIDDEN]))
                link(dve.tensor_tensor(w["out_bias"][:, :], bank[4][0:C, 0:1], projb[:, :], ALU.add))
                link(dve.tensor_copy(w["w_attn"][:, :], bank[5][0:C, 0:4 * C]))
                link(dve.tensor_copy(w1_t[:, :], bank[6][0:C, 0:HIDDEN]))
                link(dve.tensor_copy(w2_t[:, :, :], bank[7][:, 0:CHUNKS * C].rearrange("p (k c) -> p k c", c=C)))
                link(dve.tensor_reduce(s1[:, :], w1_t[:, 0:GROUPS * gs1].rearrange("p (g n) -> p g n", n=gs1),
                                       AX.X, ALU.add))
                link(dve.tensor_reduce(s2[:, :, :], w2_t[:, :, 0:GROUPS * gs2].rearrange("p k (g n) -> p k g n", n=gs2),
                                       AX.X, ALU.add))
                link(dve.tensor_reduce(sp2[:, :], s2[:, :, :].rearrange("p k g -> p g k"), AX.X, ALU.add))
                dve.wait_ge(products, 2)
                link(dve.tensor_copy(w["fc2"][:, :, :], bank[0][:, 0:CHUNKS * C].rearrange("p (k c) -> p k c", c=C)))
                link(dve.tensor_copy(m1[:, :], bank[1][0:C, 0:GROUPS]))
                link(dve.tensor_copy(m2[:, :], bank[2][:, 0:GROUPS]))
                link(dve.memset(w["w1"][0:C, :], 0.0))
                link(dve.memset(w["w2"][:, :, :], 0.0))
                for g in range(GROUPS):
                    c1, c2 = slice(g * gs1, (g + 1) * gs1), slice(g * gs2, (g + 1) * gs2)
                    link(dve.tensor_scalar(z1[:, c1], w1_t[:, c1], m1[:, g:g + 1], None, ALU.is_gt))
                    link(dve.tensor_scalar(n1[:, c1], w1_t[:, c1], m1[:, g:g + 1], None, ALU.is_lt))
                    link(dve.tensor_tensor(w["w1"][0:C, c1], z1[:, c1], n1[:, c1], ALU.subtract))
                    link(dve.tensor_scalar(z2[:, :, c2], w2_t[:, :, c2], m2[:, g:g + 1], None, ALU.is_gt))
                    link(dve.tensor_scalar(n2[:, :, c2], w2_t[:, :, c2], m2[:, g:g + 1], None, ALU.is_lt))
                    link(dve.tensor_tensor(w["w2"][:, :, c2], z2[:, :, c2], n2[:, :, c2], ALU.subtract))

            @block.tensor
            def _(pe):
                pe.wait_ge(step, 9)
                idn = w["ident"]
                pe.matmul(bank[0][0:C, 0:HIDDEN], w["centre"][:, :], g_fc1[:, :], start=True, stop=True)
                for k in range(CHUNKS):
                    pe.matmul(bank[1][:, k:k + 1], fc1_raw[:, k * P:(k + 1) * P], lnb[:, :], start=True, stop=True)
                pe.transpose(bank[2][0:C, 0:C], w["w_lin"][:, 0:C], idn[0:C, 0:C])
                for k in range(CHUNKS):
                    pe.transpose(bank[3][0:C, k * P:(k + 1) * P], fc2_raw[:, k, :], idn[:, :])
                pe.matmul(bank[4][0:C, 0:1], w["proj"][:, :], fc2b[:, :], start=True, stop=True)
                pe.matmul(bank[5][0:C, 0:4 * C], w["centre"][:, :], attn_raw[:, :], start=True, stop=True)
                for k in range(CHUNKS):
                    pe.transpose(bank[6][0:C, k * P:(k + 1) * P], w1_raw[:, k, :], idn[:, :])
                for k in range(CHUNKS):
                    mm = pe.transpose(bank[7][:, k * C:(k + 1) * C], w2_raw[:, k * P:(k + 1) * P], idn[0:C, 0:C])
                mm.then_inc(products, 1)
                pe.wait_ge(step, 20)
                for k in range(CHUNKS):
                    pe.matmul(bank[0][:, k * C:(k + 1) * C], fc2_t[:, k * P:(k + 1) * P], w["proj"][:, :],
                              start=True, stop=True)
                pe.matmul(bank[1][0:C, 0:GROUPS], ones1[:, 0:C], s1[:, :], start=True, stop=True)
                pe.matmul(bank[2][:, 0:GROUPS], ones2[:, :], sp2[:, :], start=True, stop=True).then_inc(products, 1)


def _pipeline(eng, body, items, stages, unroll, ahead=0):
    first = -(-(stages + 2) // unroll) * unroll
    count = (items - ahead - first) // unroll
    last = first + count * unroll

    def peeled(i):
        body(i, i % unroll, i // unroll, lambda s: 0 <= i - s < items)

    for i in range(-ahead, first):
        peeled(i)
    with eng.Fori(0, count) as k:
        for r in range(unroll):
            body(k * unroll + (first + r), r, k + first // unroll, lambda s: True)
    for i in range(last, items + stages - 1):
        peeled(i)


def _dmas(lap, slot, back, slots):
    return (lap + ((slot - back) // slots + 1)) * 16


def conv_block(nc, w, x_in, x1, rows):
    with ExitStack() as ctx:
        def sb(name, shape, dt=FP32):
            return ctx.enter_context(nc.sbuf_tensor("cb_" + name, shape, dt))

        def sem(name):
            return ctx.enter_context(nc.semaphore("cb_" + name))
        X = sb("x", [C, 2, L])
        XR = sb("x_again", [C, 2, L])
        X1 = sb("x1", [C, 2, L])
        XS = sb("xs", [C, 2, L])
        STATS = sb("stats", [C, 2, 6])
        MV = sb("mean_var", [C, 4])
        GS = sb("group_stats", [C, 4])
        GV = sb("group_var", [C, 3])
        QKV = sb("qkv", [P, 2, TILES, 4 * C])
        SQ = sb("squares", [P, TILES, 3 * C])
        NS = sb("norm_sums", [P, TILES, 16])
        NR = sb("norm_roots", [P, 2, TILES, 16])
        VS = sb("var_sums", [P, TILES])
        VR = sb("var_roots", [P, TILES])
        KR = sb("k_scale", [P, TILES, 8])
        XRS = sb("x_scale", [P, TILES])
        KH = sb("k_hat", [P, 2, TILES, C])
        XN = sb("xn", [P, 2, TILES, C])
        QV = sb("q_norm_v", [P, 2, TILES, C])
        O = sb("o", [P, TILES, C])
        OSQ = sb("o_squares", [P, TILES, C])
        OS = sb("o_sums", [P, TILES * 8])
        OR = sb("o_roots", [P, TILES * 8])
        OI = sb("o_scale", [P, TILES * 8])
        OH = sb("o_hat", [P, TILES, C])
        AM = sb("attn_matrix", [C, C])
        MM = sb("query_matrix", [C, C])
        XNT = sb("xn_t", [C, L])
        OHT = sb("o_hat_t", [C, L])
        HT = sb("hidden_t", [P, 2, CHUNKS, L])
        AQKV = sb("a_qkv", [P, 2, TILES, 3 * C])
        ASQ = sb("a_squares", [P, TILES, C])
        AVS = sb("a_var_sums", [P, TILES])
        AVR = sb("a_var_roots", [P, TILES])
        ASC = sb("a_scale", [P, 2, TILES])
        AQK = sb("a_qk", [P, TILES * HEADS, 2, HD])
        AR1 = sb("a_rest", [P, TILES * HEADS, 2, HD])
        PK = sb("packed", [P, 2, TILES * HEADS, PACK], U32)

        def part(slot, n):
            return PK[:, slot, :, :].bitcast(BF16).rearrange("p r (m d) -> p r m d", d=HD)[:, :, n:n + 6:5, :]

        pq, pt, pf, po = (ctx.enter_context(nc.psum_tensor("cb_ps_" + n, [P, 2 * BANK], FP32))
                          for n in ("qkv", "turn", "hidden", "out"))
        KV, M_, G_ = po[0:C, 0:C], po[0:C, C:2 * C], po[0:C, 2 * C:2 * C + 3]
        x_loaded = [sem(f"x_loaded{i}") for i in range(2)]
        xr_loaded = [sem(f"xr_loaded{i}") for i in range(2)]
        x1_stored = [sem(f"x1_stored{i}") for i in range(2)]
        rows_stored = [sem(f"rows_stored{i}") for i in range(2)]
        names = ("bn_parts bn_done mv_ready g_done g_copied gn_var gn_std gn_scale xs_ready qkv_psum qkv_copied "
                 "squares norm_sums norm_roots norm_scales khat_ready xn_ready qv_ready kv_done a_ready m_done "
                 "m_ready xnt_psum xnt_ready fc1_psum hid_ready u_done o_ready o_squares o_sums o_roots o_scale "
                 "ohat_ready oht_psum oht_ready out_done x1_ready a_psum a_copied a_sums a_roots a_scale qk_ready "
                 "v_ready high_ready rest_ready mid_ready low_ready").split()
        S = {n: sem(n) for n in names}

        def halves(ps):
            return ps[:, :].rearrange("p (a n) -> p a n", a=2)[:, :, 0:4 * C]

        with nc.Block() as block:
            @block.sync
            def _(sp):
                def body(i, r, lap, on):
                    if on(-1):
                        _above(sp.wait_ge, S["xs_ready"], i)
                        sp.dma_start(X[:, (r + 1) % 2, :], x_in[i + 1]).then_inc(x_loaded[(r + 1) % 2], 16)
                    if on(3):
                        _above(sp.wait_ge, S["x1_ready"], i - 4)
                        sp.dma_start(XR[:, (r + 1) % 2, :], x_in[i - 3]).then_inc(xr_loaded[(r + 1) % 2], 16)
                    if on(4):
                        sp.wait_ge(S["x1_ready"], i - 3)
                        sp.dma_start(x1[i - 4], X1[:, r, :]).then_inc(x1_stored[r], 16)
                    if on(7):
                        sp.wait_ge(S["low_ready"], i - 6)
                        sp.dma_start(rows[i - 7].rearrange("(t p) n -> p t n", p=P),
                                     PK[:, (r + 1) % 2, :, :].rearrange("p (t j) n -> p t (j n)", j=HEADS)
                                     ).then_inc(rows_stored[(r + 1) % 2], 16)
                _pipeline(sp, body, BATCH, 8, 2, ahead=1)
                for r in range(2):
                    sp.wait_ge(x1_stored[r], 16 * (BATCH // 2))
                    sp.wait_ge(rows_stored[r], 16 * (BATCH // 2))

            @block.vector
            def _(dve):
                def body(i, r, lap, on):
                    q = (r + 1) % 2
                    if on(5):
                        dve.wait_ge(S["a_copied"], TILES * (i - 4))
                        dve.tensor_reduce(AVS[:, :], ASQ[:, :, :], AX.X, ALU.add).then_inc(S["a_sums"], 1)
                    if on(2):
                        dve.wait_ge(S["kv_done"], i - 1)
                        dve.tensor_tensor(AM[:, :], KV, w["head_blocks"][:, :], ALU.mult).then_inc(S["a_ready"], 1)
                    if on(3):
                        dve.wait_ge(S["o_squares"], i - 2)
                        dve.tensor_reduce(OS[:, :], OSQ[:, :, :].rearrange("p t (h d) -> p (t h) d", d=LIN_DIM),
                                          AX.X, ALU.add).then_inc(S["o_sums"], 1)
                        dve.wait_ge(S["o_roots"], i - 2)
                        _above(dve.wait_ge, S["ohat_ready"], i - 3)
                        dve.reciprocal(OI[:, :], OR[:, :]).then_inc(S["o_scale"], 1)
                    if on(0):
                        _above(dve.wait_ge, S["xs_ready"], i)
                        dve.wait_ge(S["g_done"], i + 1)
                        dve.tensor_copy(GS[:, 0:3], G_).then_inc(S["g_copied"], 1)
                        dve.wait_ge(S["g_copied"], i + 1)
                        dve.scalar_tensor_tensor(out=GV[:, 0:1], in0=GS[:, 0:1], scalar=GS[:, 0:1], in1=GS[:, 2:3],
                                                 op0=ALU.mult, op1=ALU.subtract).then_inc(S["gn_var"], 1)
                    if on(2):
                        dve.wait_ge(S["m_done"], i - 1)
                        dve.tensor_copy(MM[:, :], M_).then_inc(S["m_ready"], 1)
                    if on(5):
                        dve.wait_ge(S["a_roots"], i - 4)
                        _above(dve.wait_ge, S["v_ready"], i - 6)
                        dve.reciprocal(ASC[:, q, :], AVR[:, :]).then_inc(S["a_scale"], 1)
                        dve.wait_ge(S["a_scale"], i - 4)
                        _above(dve.wait_ge, S["mid_ready"], i - 5)
                        dve.tensor_tensor(AQK[:, :, :, :].rearrange("p (t j) s d -> p t (j s d)", j=HEADS),
                                          AQKV[:, q, :, 0:2 * C], _bcast(ASC[:, q, :], 2, 2 * C),
                                          ALU.mult).then_inc(S["qk_ready"], 1)
                    if on(6):
                        dve.wait_ge(S["mid_ready"], i - 5)
                        dve.tensor_tensor(part(r, 2), AR1[:, :, :, :], part(r, 1),
                                          ALU.subtract).then_inc(S["low_ready"], 1)
                    if on(1):
                        dve.wait_ge(S["squares"], 2 * i)
                        dve.tensor_reduce(VS[:, :], SQ[:, :, 2 * C:3 * C], AX.X, ALU.add)
                        dve.tensor_reduce(NS[:, :, :],
                                          SQ[:, :, 0:2 * C].rearrange("p t (h d) -> p t h d", d=LIN_DIM),
                                          AX.X, ALU.add).then_inc(S["norm_sums"], 1)
                        dve.wait_ge(S["norm_roots"], 2 * i)
                        dve.reciprocal(XRS[:, :], VR[:, :]).then_inc(S["norm_scales"], 1)
                        dve.reciprocal(KR[:, :, :], NR[:, q, :, 8:16]).then_inc(S["norm_scales"], 1)
                        dve.wait_ge(S["norm_scales"], 2 * i)
                        dve.tensor_tensor(XN[:, q, :, :], QKV[:, q, :, 3 * C:4 * C], _bcast(XRS[:, :], 2, C),
                                          ALU.mult).then_inc(S["xn_ready"], 1)
                        dve.tensor_tensor(KH[:, q, :, :].rearrange("p t (h d) -> p t h d", d=LIN_DIM),
                                          QKV[:, q, :, C:2 * C].rearrange("p t (h d) -> p t h d", d=LIN_DIM),
                                          _bcast(KR[:, :, :], 3, LIN_DIM), ALU.mult).then_inc(S["khat_ready"], 1)
                    if on(-1):
                        dve.wait_ge(x_loaded[q], _dmas(lap, r, -1, 2))
                        for a in range(2):
                            dve.bn_stats(STATS[:, a, :], X[:, q, a * BANK:(a + 1) * BANK]).then_inc(S["bn_parts"], 1)
                        dve.wait_ge(S["bn_parts"], 2 * i + 4)
                        _above(dve.wait_ge, S["g_done"], i + 1)
                    if on(3):
                        dve.wait_ge(S["out_done"], i - 2)
                        dve.wait_ge(xr_loaded[q], _dmas(lap, r, 3, 2))
                        _above(dve.wait_ge, x1_stored[q], _dmas(lap, r, 5, 2))
                        _above(dve.wait_ge, S["a_psum"], TILES * (i - 4))
                        dve.scalar_tensor_tensor(out=X1[:, q, :], in0=po[0:C, :], scalar=w["out_bias"][:, 0:1],
                                                 in1=XR[:, q, :], op0=ALU.add, op1=ALU.add).then_inc(S["x1_ready"], 1)
                    if on(-1):
                        dve.bn_aggr(MV[:, 0:2], STATS[:, :, :]).then_inc(S["bn_done"], 1)
                        dve.wait_ge(S["bn_done"], i + 2)
                        dve.scalar_tensor_tensor(out=MV[:, 2:3], in0=MV[:, 0:1], scalar=MV[:, 0:1], in1=MV[:, 1:2],
                                                 op0=ALU.mult, op1=ALU.add).then_inc(S["mv_ready"], 1)
                    if on(2):
                        dve.wait_ge(S["u_done"], i - 1)
                        dve.wait_ge(S["qv_ready"], i - 1)
                        _above(dve.wait_ge, S["ohat_ready"], i - 2)
                        dve.scalar_tensor_tensor(out=O[:, :, :].rearrange("p (a t) c -> p a (t c)", a=2),
                                                 in0=QV[:, r, :, :].rearrange("p (a t) c -> p a (t c)", a=2),
                                                 scalar=0.5, in1=halves(pf), op0=ALU.mult,
                                                 op1=ALU.add).then_inc(S["o_ready"], 1)
                    if on(0):
                        dve.wait_ge(S["gn_std"], i + 1)
                        dve.reciprocal(GV[:, 2:3], GV[:, 1:2]).then_inc(S["gn_scale"], 1)
                        dve.wait_ge(S["gn_scale"], i + 1)
                        _above(dve.wait_ge, S["u_done"], i - 1)
                        dve.tensor_scalar(XS[:, r, :], X[:, r, :], GS[:, 0:1], GV[:, 2:3], ALU.subtract,
                                          ALU.mult).then_inc(S["xs_ready"], 1)
                _pipeline(dve, body, BATCH, 7, 2, ahead=1)

            @block.gpsimd
            def _(pool):
                def body(i, r, lap, on):
                    q = (r + 1) % 2
                    if on(3):
                        pool.wait_ge(S["o_scale"], i - 2)
                        _above(pool.wait_ge, S["oht_psum"], i - 3)
                        pool.tensor_tensor(OH[:, :, :].rearrange("p t (h d) -> p (t h) d", d=LIN_DIM),
                                           O[:, :, :].rearrange("p t (h d) -> p (t h) d", d=LIN_DIM),
                                           _bcast(OI[:, :], 2, LIN_DIM), ALU.mult).then_inc(S["ohat_ready"], 1)
                    if on(5):
                        pool.wait_ge(S["a_scale"], i - 4)
                        _above(pool.wait_ge, rows_stored[q], _dmas(lap, r, 7, 2))
                        v = PK[:, q, :, PW:PW + HD].bitcast(FP32).rearrange("p (t j) d -> p t j d", j=HEADS)
                        pool.tensor_tensor(v, AQKV[:, q, :, 2 * C:3 * C].rearrange("p t (j d) -> p t j d", d=HD),
                                           _bcast(_bcast(ASC[:, q, :], 2, HEADS), 3, HD),
                                           ALU.mult).then_inc(S["v_ready"], 1)
                        pool.wait_ge(S["high_ready"], i - 4)
                        _above(pool.wait_ge, S["low_ready"], i - 5)
                        pool.tensor_tensor(AR1[:, :, :, :], AQK[:, :, :, :], part(q, 0),
                                           ALU.subtract).then_inc(S["rest_ready"], 1)
                    if on(1):
                        pool.wait_ge(S["norm_roots"], 2 * i)
                        pool.tensor_tensor(QV[:, q, :, :].rearrange("p t (h d) -> p t h d", d=LIN_DIM),
                                           QKV[:, q, :, 2 * C:3 * C].rearrange("p t (h d) -> p t h d", d=LIN_DIM),
                                           _bcast(NR[:, q, :, 0:8], 3, LIN_DIM), ALU.mult).then_inc(S["qv_ready"], 1)
                    if on(5):
                        pool.tensor_tensor(part(q, 1), AQK[:, :, :, :], part(q, 0),
                                           ALU.subtract).then_inc(S["mid_ready"], 1)
                _pipeline(pool, body, BATCH, 7, 2)

            @block.scalar
            def _(act):
                def body(i, r, lap, on):
                    q = (r + 1) % 2
                    if on(3):
                        act.wait_ge(S["o_ready"], i - 2)
                        act.activation(OSQ[:, :, :], O[:, :, :], ACT.Square).then_inc(S["o_squares"], 1)
                    if on(2):
                        act.wait_ge(S["xnt_psum"], i - 1)
                        act.activation(XNT[:, :], pt[0:C, :], ACT.Copy).then_inc(S["xnt_ready"], 1)
                    if on(5):
                        act.wait_ge(S["a_sums"], i - 4)
                        act.activation(AVR[:, :], AVS[:, :], ACT.Sqrt, bias=w["eps"][:, 0:1],
                                       scale=1.0 / C).then_inc(S["a_roots"], 1)
                    if on(3):
                        act.wait_ge(S["o_sums"], i - 2)
                        act.activation(OR[:, :], OS[:, :], ACT.Sqrt).then_inc(S["o_roots"], 1)
                    if on(1):
                        for t in range(TILES):
                            act.wait_ge(S["qkv_psum"], 8 * (i - 1) + t + 1)
                            act.activation(QKV[:, q, t, :], pq[:, (t % 2) * BANK:(t % 2) * BANK + 4 * C],
                                           ACT.Copy).then_inc(S["qkv_copied"], 1)
                        act.wait_ge(S["qkv_copied"], 8 * i)
                        act.activation(SQ[:, :, 2 * C:3 * C], QKV[:, q, :, 3 * C:4 * C],
                                       ACT.Square).then_inc(S["squares"], 1)
                        act.activation(SQ[:, :, 0:2 * C], QKV[:, q, :, 0:2 * C], ACT.Square).then_inc(S["squares"], 1)
                    if on(3):
                        act.wait_ge(S["oht_psum"], i - 2)
                        act.activation(OHT[:, :], pt[0:C, :], ACT.Copy).then_inc(S["oht_ready"], 1)
                    if on(5):
                        act.wait_ge(S["qk_ready"], i - 4)
                        _above(act.wait_ge, rows_stored[q], _dmas(lap, r, 7, 2))
                        act.activation(part(q, 0), AQK[:, :, :, :], ACT.Copy).then_inc(S["high_ready"], 1)
                    if on(0):
                        act.wait_ge(S["gn_var"], i + 1)
                        act.activation(GV[:, 1:2], GV[:, 0:1], ACT.Sqrt, bias=w["eps"][0:C, 0:1],
                                       scale=-1.0).then_inc(S["gn_std"], 1)
                    if on(1):
                        act.wait_ge(S["norm_sums"], i)
                        act.activation(VR[:, :], VS[:, :], ACT.Sqrt, bias=w["eps"][:, 0:1],
                                       scale=1.0 / C).then_inc(S["norm_roots"], 1)
                        act.activation(NR[:, q, :, :], NS[:, :, :], ACT.Sqrt).then_inc(S["norm_roots"], 1)
                    if on(2):
                        for k in range(CHUNKS):
                            for a in range(2):
                                act.wait_ge(S["fc1_psum"], 6 * (i - 2) + 2 * k + a + 1)
                                act.activation(HT[:, r, k, a * BANK:(a + 1) * BANK], pf[:, a * BANK:(a + 1) * BANK],
                                               ACT.Silu, bias=w["fc1_bias"][:, k:k + 1]).then_inc(S["hid_ready"], 1)
                    if on(4):
                        for t in range(TILES):
                            act.wait_ge(S["a_psum"], TILES * (i - 4) + t + 1)
                            if t == 0:
                                _above(act.wait_ge, S["v_ready"], i - 5)
                                _above(act.wait_ge, S["a_sums"], i - 4)
                            act.activation(AQKV[:, r, t, :], pq[:, (t % 2) * BANK:(t % 2) * BANK + 3 * C], ACT.Copy)
                            act.activation(ASQ[:, t, :], pq[:, (t % 2) * BANK + 3 * C:(t % 2) * BANK + 4 * C],
                                           ACT.Square).then_inc(S["a_copied"], 1)
                _pipeline(act, body, BATCH, 7, 2)

            @block.tensor
            def _(pe):
                def hidden(i, k):
                    for a in range(2):
                        if k:
                            pe.wait_ge(S["hid_ready"], 6 * (i - 2) + 2 * k + a - 1)
                        pe.matmul(pf[:, a * BANK:(a + 1) * BANK], w["fc1"][:, k * P:(k + 1) * P],
                                  XNT[:, a * BANK:(a + 1) * BANK], start=True, stop=True).then_inc(S["fc1_psum"], 1)

                def body(i, r, lap, on):
                    q = (r + 1) % 2
                    if on(2):
                        pe.wait_ge(S["xn_ready"], i - 1)
                        _above(pe.wait_ge, S["oht_ready"], i - 3)
                        for t in range(TILES):
                            mm = pe.transpose(pt[0:C, t * P:(t + 1) * P], XN[:, r, t, :], w["ident"][:, :])
                        mm.then_inc(S["xnt_psum"], 1)
                        pe.wait_ge(S["khat_ready"], i - 1)
                    if on(4):
                        pe.wait_ge(S["x1_ready"], i - 3)
                    if on(2):
                        for t in range(TILES):
                            mm = pe.matmul(KV, KH[:, r, t, :], QKV[:, r, t, 2 * C:3 * C], start=(t == 0),
                                           stop=(t == TILES - 1))
                        mm.then_inc(S["kv_done"], 1)
                        pe.wait_ge(S["a_ready"], i - 1)
                    if on(0):
                        pe.wait_ge(S["mv_ready"], i + 1)
                        pe.matmul(G_, w["group_mean"][:, :], MV[:, 0:3], start=True, stop=True).then_inc(S["g_done"], 1)
                    if on(1):
                        pe.wait_ge(S["xs_ready"], i)
                        for t in range(TILES):
                            if t >= 2:
                                pe.wait_ge(S["qkv_copied"], 8 * (i - 1) + t - 1)
                            elif on(5):
                                pe.wait_ge(S["a_copied"], 8 * (i - 5) + t + 7)
                            elif on(2):
                                pe.wait_ge(S["qkv_copied"], 8 * (i - 1) + t - 1)
                            pe.matmul(pq[:, (t % 2) * BANK:(t % 2) * BANK + 4 * C], XS[:, q, t * P:(t + 1) * P],
                                      w["w_lin"][:, :], start=True, stop=True).then_inc(S["qkv_psum"], 1)
                    if on(0):
                        pe.wait_ge(S["g_copied"], i + 1)
                    if on(2):
                        pe.matmul(M_, w["wq_t"][:, :], AM[:, :], start=True, stop=True).then_inc(S["m_done"], 1)
                    if on(3):
                        pe.wait_ge(S["ohat_ready"], i - 2)
                        if on(2):
                            pe.wait_ge(S["xnt_ready"], i - 1)
                        for t in range(TILES):
                            mm = pe.transpose(pt[0:C, t * P:(t + 1) * P], OH[:, t, :], w["ident"][:, :])
                        mm.then_inc(S["oht_psum"], 1)
                    if on(2):
                        pe.wait_ge(S["xnt_ready"], i - 1)
                        _above(pe.wait_ge, S["o_ready"], i - 2)
                        hidden(i, 0)
                    if on(3):
                        if on(2):
                            pe.wait_ge(S["m_ready"], i - 1)
                        for a in range(2):
                            half = slice(a * BANK, (a + 1) * BANK)
                            for k in range(CHUNKS):
                                pe.matmul(po[0:C, half], w["fc2"][:, k, :], HT[:, q, k, half], start=(k == 0),
                                          stop=False)
                            if a == 0:
                                pe.wait_ge(S["oht_ready"], i - 2)
                            mm = pe.matmul(po[0:C, half], w["proj"][:, :], OHT[:, half], start=False, stop=True)
                        mm.then_inc(S["out_done"], 1)
                    if on(2):
                        hidden(i, 1)
                        hidden(i, 2)
                    if on(4):
                        for t in range(TILES):
                            if t >= 2:
                                pe.wait_ge(S["a_copied"], 8 * (i - 4) + t - 1)
                            elif on(1):
                                pe.wait_ge(S["qkv_copied"], 8 * (i - 1) + t + 7)
                            elif on(5):
                                pe.wait_ge(S["a_copied"], 8 * (i - 5) + t + 7)
                            pe.matmul(pq[:, (t % 2) * BANK:(t % 2) * BANK + 4 * C], X1[:, r, t * P:(t + 1) * P],
                                      w["w_attn"][:, :], start=True, stop=True).then_inc(S["a_psum"], 1)
                    if on(2):
                        pe.wait_ge(S["m_ready"], i - 1)
                        pe.wait_ge(S["hid_ready"], 6 * (i - 1))
                        for t in range(TILES):
                            c0 = (t // 4) * BANK + (t % 4) * C
                            mm = pe.matmul(pf[:, c0:c0 + C], XS[:, r, t * P:(t + 1) * P], MM[:, :], start=True,
                                           stop=True)
                        mm.then_inc(S["u_done"], 1)
                _pipeline(pe, body, BATCH, 7, 2)


def _score_units():
    units = [[(0, 0, BANK, 0)], [(0, BANK, BANK, 0)]]
    for kb in range(1, TILES // 2 + 1):
        q0 = kb * P
        units.append([(kb, q0, BANK, 0)])
        rest = L - q0 - BANK
        if rest:
            other = TILES - kb
            units.append([(kb, q0 + BANK, rest, 0), (other, other * P, kb * P, rest)])
    return units


def causal_attention(nc, w, rows, att):
    scale = C ** -0.5
    UNITS = _score_units()
    NU = len(UNITS)
    QUNITS = [(qb, k0, min(BANK, (qb + 1) * P - k0)) for qb in range(TILES)
              for k0 in range(0, (qb + 1) * P, BANK)]
    NQ = len(QUNITS)
    SLOTS = 4
    RING = 4
    QBANKS, KBANKS = 3, 2
    LAG = 4
    VALUES_LAG = LAG + 2
    MAX_TURN, Q_TURN, K_TURN, OUT_TURN = 3, 4, 6, 8
    VW = 32
    OUT_QUNIT = -(-NQ * (OUT_TURN + 1) // NU) - 1
    QG = P // VW
    with ExitStack() as ctx:
        def sb(name, shape, dt=FP32):
            return ctx.enter_context(nc.sbuf_tensor("at_" + name, shape, dt))

        def pb(name, shape, dt=FP32):
            return ctx.enter_context(nc.psum_tensor("at_ps_" + name, shape, dt))

        def sem(name):
            return ctx.enter_context(nc.semaphore("at_" + name))
        ST = sb("stacks", [P, SLOTS, TILES, PW + PACK + PW], U32)
        V = sb("v", [P, SLOTS, TILES, VW])
        QT = sb("q_t", [P, SLOTS, L], BF16)
        KT = sb("k_t", [P, SLOTS, L], BF16)
        MX = sb("unit_max", [P, 2, TILES, 2])
        NM = sb("neg_max", [P, TILES])
        MP = sb("max_parts", [P, TILES, 32], BF16)
        PR = sb("probs", [P, RING, BANK])
        RC = sb("recip", [P, TILES])
        ONE = sb("one", [P, 1, 1])
        OT = sb("out_t", [P, 2 * P])
        AT = sb("att", [P, SLOTS, TILES, HD])
        pq = pb("queries", [P, QBANKS, BANK])
        pk = pb("keys", [P, KBANKS, BANK])
        pv = pb("values", [P, 2, BANK])
        bank = pb("turn", [P, BANK])
        turned = bank[:, :].bitcast(BF16)
        out_t = [pv[:, i, 0:2 * P] for i in range(2)]
        out_ps = bank[:, 0:2 * P].rearrange("p (t d) -> p t d", d=VW)
        loaded = [sem(f"loaded{i}") for i in range(SLOTS)]
        stored = [sem(f"stored{i}") for i in range(SLOTS)]
        names = ("set_up zeros_set one_set max_set parts_set spread q_turned k_turned q_ready k_ready q_scores "
                 "unit_max head_max max_high max_parts max_turned max_ready k_scores probs values out_copied out_turned recip out_ready").split()
        S = {n: sem(n) for n in names}
        src = rows.rearrange("b l (j n) -> (b l j) n", n=PACK).rearrange("(h t p) n -> h p t n", t=TILES, p=P)
        dst = att.rearrange("b l (j d) -> (b l j) d", d=HD).rearrange("(h t p) d -> h p t d", t=TILES, p=P)

        def k_stack(slot):
            return ST[:, slot, :, 0:2 * PW].bitcast(BF16)

        def q_stack(slot):
            return ST[:, slot, :, 2 * PW + HD:4 * PW + HD].bitcast(BF16)

        with nc.Block() as block:
            @block.sync
            def _(sp):
                def body(i, r, lap, on):
                    if on(0):
                        _above(sp.wait_ge, S["k_turned"], i - SLOTS + 1)
                        _above(sp.wait_ge, S["spread"], i - SLOTS + 1)
                        sp.dma_start(ST[:, r, :, PW:PW + PACK], src[i]).then_inc(loaded[r], 16)
                    if on(5):
                        q = (r - 5) % SLOTS
                        sp.wait_ge(S["out_ready"], i - 4)
                        sp.dma_start(dst[i - 5], AT[:, q, :, :]).then_inc(stored[q], 16)
                _pipeline(sp, body, NHEADS, 6, SLOTS)
                for r in range(SLOTS):
                    sp.wait_ge(stored[r], 16 * (NHEADS // SLOTS))

            @block.gpsimd
            def _(pool):
                pool.memset(V[:, :, :, HD:VW], 0.0).then_inc(S["zeros_set"], 1)
                pool.wait_ge(S["zeros_set"], 1)
                pool.memset(V[:, :, :, HD:HD + 1], 1.0)
                pool.memset(ONE[:, :, :], 1.0).then_inc(S["one_set"], 1)
                pool.wait_ge(S["one_set"], 1)

                def body(i, r, lap, on):
                    if on(0):
                        pool.wait_ge(loaded[r], _dmas(lap, r, 0, SLOTS))
                        _above(pool.wait_ge, S["values"], NU * (i - SLOTS + 1))
                        v = ST[:, r, :, 2 * PW:2 * PW + HD].bitcast(FP32)
                        pool.tensor_tensor(V[:, r, :, 0:HD], v, ONE[:, :, :].broadcast_to([P, TILES, HD]), ALU.mult)
                        ks, qs = k_stack(r), q_stack(r)
                        pool.tensor_copy(ks[:, :, 0:2 * HD], ks[:, :, 3 * HD:5 * HD])
                        pool.tensor_copy(ks[:, :, 2 * HD:3 * HD], ks[:, :, 3 * HD:4 * HD])
                        pool.tensor_copy(qs[:, :, 3 * HD:4 * HD], qs[:, :, HD:2 * HD])
                        high = qs[:, :, 0:HD].rearrange("p t (m d) -> p t m d", m=1)
                        pool.tensor_copy(qs[:, :, 4 * HD:6 * HD].rearrange("p t (m d) -> p t m d", m=2),
                                         high.broadcast_to([P, TILES, 2, HD])).then_inc(S["spread"], 1)
                _pipeline(pool, body, NHEADS, 5, SLOTS)

            @block.tensor
            def _(pe):
                pe.wait_ge(S["set_up"], 2)

                def turn_q(i, r, bank_read):
                    pe.wait_ge(S["spread"], i + 1)
                    bank_read()
                    for t in range(TILES):
                        mm = pe.transpose(turned[0:STACK, t * P:(t + 1) * P], q_stack(r)[:, t, :], w["ident_bf"][:, :])
                    mm.then_inc(S["q_turned"], 1)

                def turn_max(h, bank_read):
                    pe.wait_ge(S["max_parts"], h + 1)
                    bank_read()
                    for t in range(TILES):
                        mm = pe.transpose(turned[96:128, t * P:(t + 1) * P], MP[:, t, :], w["ident_bf"][:, :])
                    mm.then_inc(S["max_turned"], 1)

                def turn_k(i, r, bank_read):
                    bank_read()
                    for t in range(TILES):
                        mm = pe.transpose(turned[0:STACK, t * P:(t + 1) * P], k_stack(r)[:, t, :], w["ident_bf"][:, :])
                    mm.then_inc(S["k_turned"], 1)

                def turn_out(h, bank_read):
                    pe.wait_ge(S["out_copied"], h + 1)
                    bank_read()
                    for a in range(2):
                        mm = pe.transpose(bank[:, a * P:(a + 1) * P], OT[:, a * P:(a + 1) * P], w["ident"][:, :])
                    mm.then_inc(S["out_turned"], 1)

                def query_scores(h, slot, u):
                    qb, k0, n = QUNITS[u]
                    if u == 0:
                        pe.wait_ge(S["q_ready"], h + 1)
                        pe.wait_ge(S["k_ready"], h + 1)
                    _above(pe.wait_ge, S["unit_max"], NQ * h + u - QBANKS + 1)
                    diag = k0 + n == (qb + 1) * P
                    mm = pe.matmul(pq[:, u % QBANKS, 0:n], QT[0:STACK, slot, qb * P:(qb + 1) * P],
                                   KT[0:STACK, slot, k0:k0 + n], start=True, stop=True)
                    if diag:
                        mm = pe.matmul(pq[:, u % QBANKS, n - P:n], w["ident_bf"][:, :], w["mask_queries"][:, :],
                                       start=False, stop=True, skip_group_check=True)
                    mm.then_inc(S["q_scores"], 1)

                def key_scores(h, slot, u):
                    if u == 0:
                        pe.wait_ge(S["max_ready"], h + 1)
                    _above(pe.wait_ge, S["probs"], NU * h + u - KBANKS + 1)
                    for kb, q0, n, c0 in UNITS[u]:
                        diag = q0 == kb * P
                        mm = pe.matmul(pk[:, (slot * NU + u) % KBANKS, c0:c0 + n], KT[:, slot, kb * P:(kb + 1) * P],
                                       QT[:, slot, q0:q0 + n], start=True, stop=True)
                        if diag:
                            mm = pe.matmul(pk[:, (slot * NU + u) % KBANKS, c0:c0 + P], w["ident_bf"][:, :],
                                           w["mask_keys"][:, :],
                                           start=False, stop=True, skip_group_check=True)
                    mm.then_inc(S["k_scores"], 1)

                def values(h, slot, u):
                    pe.wait_ge(S["probs"], NU * h + u + 1)
                    if u == 0:
                        _above(pe.wait_ge, S["out_copied"], h - 1)
                    for kb, q0, n, c0 in UNITS[u]:
                        for b in range(n // P):
                            qb = q0 // P + b
                            row, col = VW * (qb % QG), P * (qb // QG)
                            mm = pe.matmul(out_t[slot % 2][row:row + VW, col:col + P], V[:, slot, kb, :],
                                           PR[:, (slot * NU + u) % RING, c0 + b * P:c0 + (b + 1) * P],
                                           start=(u == 0 and b < QG), stop=True, skip_group_check=True)
                    mm.then_inc(S["values"], 1)

                def body(i, r, lap, on):
                    def out_read():
                        if on(5):
                            pe.wait_ge(S["out_ready"], i - 4)
                        elif on(2):
                            pe.wait_ge(S["k_ready"], i - 1)

                    def max_read():
                        if on(3):
                            pe.wait_ge(S["max_ready"], i - 2)
                        else:
                            out_read()

                    def q_read():
                        pe.wait_ge(S["q_ready"], i)

                    def k_read():
                        if on(1):
                            pe.wait_ge(S["k_ready"], i)
                        else:
                            max_read()

                    nq = 0
                    for u in range(NU):
                        if u == MAX_TURN and on(3):
                            turn_max(i - 3, out_read)
                        if on(2):
                            want = -(-NQ * (u + 1) // NU)
                            while nq < want:
                                query_scores(i - 2, (r - 2) % SLOTS, nq)
                                nq += 1
                        back = 3 if u >= LAG else 4
                        if on(back):
                            key_scores(i - back, (r - back) % SLOTS, (u - LAG) % NU)
                        back = 3 if u >= VALUES_LAG else 4
                        if on(back):
                            values(i - back, (r - back) % SLOTS, (u - VALUES_LAG) % NU)
                        if u == Q_TURN and on(1):
                            turn_q(i - 1, (r - 1) % SLOTS, max_read)
                        if u == K_TURN and on(1):
                            turn_k(i - 1, (r - 1) % SLOTS, q_read)
                        if u == OUT_TURN and on(4):
                            turn_out(i - 4, k_read)
                _pipeline(pe, body, NHEADS, 5, SLOTS)

            @block.scalar
            def _(act):
                def body(i, r, lap, on):
                    q = (r - 1) % SLOTS
                    for u in range(NU):
                        back = 3 if u >= LAG else 4
                        if on(back):
                            v = (u - LAG) % NU
                            act.wait_ge(S["k_scores"], NU * (i - back) + v + 1)
                            _above(act.wait_ge, S["values"], NU * (i - back) + v - RING + 1)
                            slot_unit = (r - back) % SLOTS * NU + v
                            act.activation(PR[:, slot_unit % RING, :], pk[:, slot_unit % KBANKS, :], ACT.Exp,
                                           scale=scale).then_inc(S["probs"], 1)
                        if u == OUT_TURN - 2 and on(4):
                            act.wait_ge(S["values"], NU * (i - 3))
                            act.activation(OT[:, :], out_t[r % 2], ACT.Copy).then_inc(S["out_copied"], 1)
                        if u == Q_TURN and on(1):
                            act.wait_ge(S["q_turned"], i)
                            act.activation(QT[0:STACK, q, :], turned[0:STACK, :], ACT.Copy).then_inc(S["q_ready"], 1)
                        if u == K_TURN and on(1):
                            act.wait_ge(S["k_turned"], i)
                            act.activation(KT[0:STACK, q, :], turned[0:STACK, :], ACT.Copy).then_inc(S["k_ready"], 1)
                _pipeline(act, body, NHEADS, 5, SLOTS)

            @block.vector
            def _(dve):
                dve.memset(MX[:, :, :, :], -3.0e38).then_inc(S["max_set"], 1)
                dve.memset(MP[:, :, :], 0.0).then_inc(S["parts_set"], 1)
                dve.memset(KT[96:128, :, :], 0.0).then_inc(S["set_up"], 1)
                dve.wait_ge(S["set_up"], 1)
                dve.memset(KT[96:98, :, :], 1.0).then_inc(S["set_up"], 1)
                dve.wait_ge(S["max_set"], 1)
                dve.wait_ge(S["parts_set"], 1)

                def body(i, r, lap, on):
                    for u, (qb, k0, n) in enumerate(QUNITS):
                        if on(2):
                            dve.wait_ge(S["q_scores"], NQ * (i - 2) + u + 1)
                            dve.tensor_reduce(MX[:, r % 2, qb, k0 // BANK:k0 // BANK + 1], pq[:, u % QBANKS, 0:n], AX.X,
                                              ALU.max).then_inc(S["unit_max"], 1)
                        if u == 0 and on(3):
                            dve.wait_ge(S["head_max"], i - 2)
                            _above(dve.wait_ge, S["max_turned"], i - 3)
                            dve.tensor_copy(MP[:, :, 0], NM[:, :]).then_inc(S["max_high"], 1)
                        if u == 1 and on(3):
                            dve.wait_ge(S["max_high"], i - 2)
                            dve.tensor_tensor(MP[:, :, 1], NM[:, :], MP[:, :, 0],
                                              ALU.subtract).then_inc(S["max_parts"], 1)
                        if u == 3 and on(3):
                            dve.wait_ge(S["max_turned"], i - 2)
                            dve.tensor_copy(QT[96:128, (r - 3) % SLOTS, :], turned[96:128, :]
                                            ).then_inc(S["max_ready"], 1)
                        if u == OUT_QUNIT and on(4):
                            dve.wait_ge(S["out_turned"], i - 3)
                            dve.reciprocal(RC[:, :], out_ps[:, :, HD]).then_inc(S["recip"], 1)
                            dve.wait_ge(S["recip"], i - 3)
                            _above(dve.wait_ge, stored[r], _dmas(lap, r, 8, SLOTS))
                            dve.tensor_tensor(AT[:, r, :, :], out_ps[:, :, 0:HD], _bcast(RC[:, :], 2, HD),
                                              ALU.mult).then_inc(S["out_ready"], 1)
                    if on(2):
                        dve.wait_ge(S["unit_max"], NQ * (i - 1))
                        _above(dve.wait_ge, S["max_parts"], i - 2)
                        dve.tensor_reduce(NM[:, :], MX[:, r % 2, :, :], AX.X, ALU.max,
                                          negate=True).then_inc(S["head_max"], 1)
                _pipeline(dve, body, NHEADS, 5, SLOTS)


def project_and_ffn(nc, w, att, x1, y_out):
    LIMIT = QB - QEPS
    REST = BATCH - GROUPS * GB
    with ExitStack() as ctx:
        def sb(name, shape, dt=FP32):
            return ctx.enter_context(nc.sbuf_tensor("ff_" + name, shape, dt))

        def sem(name):
            return ctx.enter_context(nc.semaphore("ff_" + name))
        AR = sb("att_rows", [P, 2, TILES, C])
        X1 = sb("x1", [C, 2, L])
        AT = sb("att_t", [C, L])
        X2 = sb("x2", [C, GB, L])
        SQ = sb("squares", [P, TILES, C])
        VS = sb("var_sums", [P, TILES])
        VR = sb("var_roots", [P, TILES])
        SCALE = sb("scale", [P, TILES])
        XN = sb("xn", [P, 2, TILES, C])
        XNT = sb("xn_t", [C + 1, L])
        Y1 = sb("hidden", [P, GB, CHUNKS, L])
        Y2 = sb("ffn", [C, GB, L])
        OUT = sb("out", [C, 2, L])
        G1, G2 = sb("max1", [P, GB * CHUNKS]), sb("max2", [C, GB])
        ROW = sb("row_of_ones", [1, P])
        M1, M2 = sb("group_max1", [P, 4]), sb("group_max2", [C, 4])
        pt, py, pc, pf = (ctx.enter_context(nc.psum_tensor("ff_ps_" + n, [P, 2 * BANK], FP32))
                          for n in ("turn", "out", "centred", "hidden"))
        xc = pc[:, :].rearrange("p (a n) -> p a n", a=2)[:, :, 0:4 * C]
        a_loaded = [sem(f"att_loaded{i}") for i in range(2)]
        x_loaded = [sem(f"x1_loaded{i}") for i in range(2)]
        stored = [sem(f"stored{i}") for i in range(2)]
        names = ("ones_set att_turned att_copied y_done x2_ready xc_done squares var_sums var_roots scale xn_ready "
                 "xn_turned xnt_ready y1_psum y1_copied y1_max max1 all_max1 scale1 gelu h_ready y2_psum y2_ready "
                 "y2_max max2 all_max2 scale2 limited out_ready").split()
        S = {n: sem(n) for n in names}

        def groups(eng, body):
            body(0, lambda j: j, GB)
            with eng.Fori(1, GROUPS) as g:
                body(g, lambda j: g * GB + j, GB)
            body(GROUPS, lambda j: GROUPS * GB + j, REST)

        def first(g):
            return isinstance(g, int) and g == 0

        with nc.Block() as block:
            @block.sync
            def _(sp):
                def load(j, entry):
                    sp.dma_start(AR[:, j % 2, :, :], att[entry].rearrange("(t p) c -> p t c", p=P)
                                 ).then_inc(a_loaded[j % 2], 16)
                    sp.dma_start(X1[:, j % 2, :], x1[entry]).then_inc(x_loaded[j % 2], 16)

                def body(g, n, size):
                    for j in range(GB):
                        if not first(g):
                            sp.wait_ge(S["out_ready"], n(j + 1) - GB)
                            sp.dma_start(y_out[n(j) - GB], OUT[:, j % 2, :]).then_inc(stored[j % 2], 16)
                        if size == GB:
                            sp.wait_ge(S["att_turned"], n(j + 1))
                            sp.wait_ge(S["x2_ready"], n(j + 1))
                            load(j, n(j + 2))
                    if size == REST:
                        for j in range(REST):
                            sp.wait_ge(S["x2_ready"], n(j + 1))
                            sp.dma_start(y_out[n(j)], X2[:, j, :]).then_inc(stored[j % 2], 16)
                load(0, 0)
                load(1, 1)
                groups(sp, body)
                for r in range(2):
                    sp.wait_ge(stored[r], 16 * (BATCH // 2))

            @block.tensor
            def _(pe):
                pe.wait_ge(S["ones_set"], 2)

                def body(g, n, size):
                    full = size == GB

                    def hidden(j, k):
                        for a in range(2):
                            if k or j:
                                pe.wait_ge(S["y1_copied"], 6 * n(j) + 2 * k + a - 1)
                            pe.matmul(pf[:, a * BANK:(a + 1) * BANK], w["w1"][:, k * P:(k + 1) * P],
                                      XNT[:, a * BANK:(a + 1) * BANK], start=True, stop=True
                                      ).then_inc(S["y1_psum"], 1)

                    def row_of_maxima(M, name, all_name, g):
                        parts = M.shape[0]
                        pe.wait_ge(S[name], 2 * g + 1)
                        pe.transpose(pc[0:1, 0:parts], M[:, 0:1], w["ident"][0:parts, 0:parts]
                                     ).then_inc(S[all_name], 1)

                    def spread_max(M, name, all_name, g):
                        parts = M.shape[0]
                        pe.wait_ge(S[name], 2 * g + 2)
                        pe.matmul(pc[0:parts, BANK:BANK + 1], ROW[:, 0:parts], M[0:1, 1:2], start=True, stop=True
                                  ).then_inc(S[all_name], 1)

                    for j in range(size + 2):
                        if full and j >= 2:
                            pe.wait_ge(S["xn_ready"], n(j - 1))
                            for t in range(TILES):
                                mm = pe.transpose(pt[0:C, t * P:(t + 1) * P], XN[:, j % 2, t, :], w["ident"][:, :])
                            mm.then_inc(S["xn_turned"], 1)
                        if full and 1 <= j <= size:
                            pe.wait_ge(S["x2_ready"], n(j))
                            for t in range(TILES):
                                c0 = (t // 4) * BANK + (t % 4) * C
                                mm = pe.matmul(pc[:, c0:c0 + C], X2[:, j - 1, t * P:(t + 1) * P], w["centre"][:, :],
                                               start=True, stop=True)
                            mm.then_inc(S["xc_done"], 1)
                        if j < size:
                            pe.wait_ge(a_loaded[j % 2], (g * (GB // 2) + (j // 2 + 1)) * 16)
                            if full and j >= 2:
                                pe.wait_ge(S["xnt_ready"], n(j - 1))
                            for t in range(TILES):
                                mm = pe.transpose(pt[0:C, t * P:(t + 1) * P], AR[:, j % 2, t, :], w["ident"][:, :])
                            mm.then_inc(S["att_turned"], 1)
                        if j == 0 and not first(g):
                            row_of_maxima(M2, "max2", "all_max2", g - 1)
                        if full and j >= 2:
                            pe.wait_ge(S["xnt_ready"], n(j - 1))
                            hidden(j - 2, 0)
                        if j < size:
                            pe.wait_ge(S["att_copied"], n(j + 1))
                            if j:
                                pe.wait_ge(S["x2_ready"], n(j))
                            elif not first(g):
                                pe.wait_ge(S["y2_ready"], n(0) - 1)
                            for a in range(2):
                                half = slice(a * BANK, (a + 1) * BANK)
                                mm = pe.matmul(py[0:C, half], w["wp"][:, :], AT[:, half], start=True, stop=True)
                            mm.then_inc(S["y_done"], 1)
                        if j == 0 and not first(g):
                            spread_max(M2, "max2", "all_max2", g - 1)
                        if full and j >= 2:
                            hidden(j - 2, 1)
                            hidden(j - 2, 2)
                    if not full:
                        return
                    row_of_maxima(M1, "max1", "all_max1", g)
                    spread_max(M1, "max1", "all_max1", g)
                    for j in range(size):
                        if j >= 2:
                            pe.wait_ge(S["y2_ready"], n(j - 1))
                        banks = (py, pf)[j % 2]
                        for k in range(CHUNKS):
                            pe.wait_ge(S["h_ready"], 3 * n(j) + k + 1)
                            for a in range(2):
                                half = slice(a * BANK, (a + 1) * BANK)
                                mm = pe.matmul(banks[0:C, half], w["w2"][:, k, :], Y1[:, j, k, half], start=(k == 0),
                                               stop=(k == CHUNKS - 1))
                        mm.then_inc(S["y2_psum"], 1)
                groups(pe, body)

            @block.scalar
            def _(act):
                def body(g, n, size):
                    full = size == GB
                    for j in range(size + 2):
                        if full and j >= 2:
                            act.wait_ge(S["xn_turned"], n(j - 1))
                            act.activation(XNT[0:C, :], pt[0:C, :], ACT.Copy).then_inc(S["xnt_ready"], 1)
                        if j < size:
                            act.wait_ge(S["att_turned"], n(j + 1))
                            act.activation(AT[:, :], pt[0:C, :], ACT.Copy).then_inc(S["att_copied"], 1)
                        if full and 1 <= j <= size:
                            act.wait_ge(S["xc_done"], n(j))
                            act.activation(SQ[:, :, :].rearrange("p (a t) c -> p a (t c)", a=2), xc,
                                           ACT.Square).then_inc(S["squares"], 1)
                            act.wait_ge(S["var_sums"], n(j))
                            act.activation(VR[:, :], VS[:, :], ACT.Sqrt, bias=w["eps"][:, 0:1],
                                           scale=1.0 / C).then_inc(S["var_roots"], 1)
                        if full and j >= 2:
                            for k in range(CHUNKS):
                                for a in range(2):
                                    act.wait_ge(S["y1_psum"], 6 * n(j - 2) + 2 * k + a + 1)
                                    act.activation(Y1[:, j - 2, k, a * BANK:(a + 1) * BANK],
                                                   pf[:, a * BANK:(a + 1) * BANK], ACT.Copy
                                                   ).then_inc(S["y1_copied"], 1)
                    if full:
                        act.wait_ge(S["scale1"], 2 * g + 2)
                        for j in range(size + 1):
                            if j < size:
                                for k in range(CHUNKS):
                                    act.activation(Y1[:, j, k, :], Y1[:, j, k, :], ACT.Gelu,
                                                   scale=M1[:, 3:4]).then_inc(S["gelu"], 1)
                            if j:
                                act.wait_ge(S["y2_psum"], n(j))
                                act.activation(Y2[:, j - 1, :], (py, pf)[(j - 1) % 2][0:C, :], ACT.Identity,
                                               bias=w["b2"][:, 0:1]).then_inc(S["y2_ready"], 1)
                groups(act, body)

            @block.vector
            def _(dve):
                dve.memset(ROW[:, :], 1.0).then_inc(S["ones_set"], 1)
                dve.memset(XNT[C:C + 1, :], 1.0).then_inc(S["ones_set"], 1)

                def group_scale(g, entry, peak, maxima, M, name, all_name, scale_name):
                    dve.wait_ge(S[peak], entry)
                    dve.tensor_reduce(M[:, 0:1], maxima[:, :], AX.X, ALU.max).then_inc(S[name], 1)
                    dve.wait_ge(S[all_name], 2 * g + 1)
                    dve.tensor_reduce(M[0:1, 1:2], pc[0:1, 0:M.shape[0]], AX.X, ALU.max).then_inc(S[name], 1)
                    dve.wait_ge(S[all_name], 2 * g + 2)
                    dve.tensor_scalar(M[:, 2:3], pc[0:M.shape[0], BANK:BANK + 1], QEPS, 1.0 / QB, ALU.add, ALU.mult
                                      ).then_inc(S[scale_name], 1)
                    dve.wait_ge(S[scale_name], 2 * g + 1)
                    dve.reciprocal(M[:, 3:4], M[:, 2:3]).then_inc(S[scale_name], 1)

                def body(g, n, size):
                    full = size == GB

                    def peak1(j):
                        for k in range(CHUNKS):
                            dve.wait_ge(S["y1_copied"], 6 * n(j) + 2 * k + 2)
                            dve.tensor_reduce(G1[:, CHUNKS * j + k:CHUNKS * j + k + 1], Y1[:, j, k, :], AX.X,
                                              ALU.max, apply_absolute_value=True).then_inc(S["y1_max"], 1)

                    def output(j):
                        dve.tensor_scalar(Y2[:, j, :], Y2[:, j, :], M2[:, 3:4], LIMIT, ALU.mult, ALU.min
                                          ).then_inc(S["limited"], 1)
                        dve.wait_ge(S["limited"], n(j + 1) - GB)
                        if j >= 2:
                            dve.wait_ge(stored[j % 2], (g * (GB // 2) + (j // 2 - GB // 2)) * 16)
                        dve.scalar_tensor_tensor(out=OUT[:, j % 2, :], in0=Y2[:, j, :], scalar=-LIMIT,
                                                 in1=X2[:, j, :], op0=ALU.max, op1=ALU.add
                                                 ).then_inc(S["out_ready"], 1)

                    if not first(g):
                        group_scale(g - 1, n(0), "y2_max", G2, M2, "max2", "all_max2", "scale2")
                        dve.wait_ge(S["scale2"], 2 * g)
                    for j in range(max(size + 2, GB)):
                        if not first(g) and j < GB:
                            output(j)
                        if full and 1 <= j <= size:
                            q = (j - 1) % 2
                            dve.wait_ge(S["squares"], n(j))
                            dve.tensor_reduce(VS[:, :], SQ[:, :, :], AX.X, ALU.add).then_inc(S["var_sums"], 1)
                            dve.wait_ge(S["var_roots"], n(j))
                            dve.reciprocal(SCALE[:, :], VR[:, :]).then_inc(S["scale"], 1)
                            dve.wait_ge(S["scale"], n(j))
                            for a in range(2):
                                ins = dve.tensor_tensor(XN[:, q, 4 * a:4 * a + 4, :],
                                                        xc[:, a, :].rearrange("p (t c) -> p t c", c=C),
                                                        _bcast(SCALE[:, 4 * a:4 * a + 4], 2, C), ALU.mult)
                            ins.then_inc(S["xn_ready"], 1)
                        if j < size:
                            dve.wait_ge(S["y_done"], n(j + 1))
                            if not first(g):
                                dve.wait_ge(S["out_ready"], n(j + 1) - GB)
                            dve.wait_ge(x_loaded[j % 2], (g * (GB // 2) + (j // 2 + 1)) * 16)
                            dve.scalar_tensor_tensor(out=X2[:, j, :], in0=py[0:C, :], scalar=w["bp"][:, 0:1],
                                                     in1=X1[:, j % 2, :], op0=ALU.add, op1=ALU.add
                                                     ).then_inc(S["x2_ready"], 1)
                        if full and j >= 2:
                            peak1(j - 2)
                    if not full:
                        return
                    if not first(g):
                        for r in range(2):
                            dve.wait_ge(stored[r], g * (16 * GB // 2))
                    group_scale(g, 3 * n(size), "y1_max", G1, M1, "max1", "all_max1", "scale1")
                    for j in range(size + 1):
                        if j < size:
                            for k in range(CHUNKS):
                                dve.wait_ge(S["gelu"], 3 * n(j) + k + 1)
                                dve.tensor_scalar(Y1[:, j, k, :], Y1[:, j, k, :], LIMIT, None, ALU.min
                                                  ).then_inc(S["h_ready"], 1)
                        if j:
                            dve.wait_ge(S["y2_ready"], n(j))
                            dve.tensor_reduce(G2[:, j - 1:j], Y2[:, j - 1, :], AX.X, ALU.max,
                                              apply_absolute_value=True).then_inc(S["y2_max"], 1)
                groups(dve, body)


def build(nc, A, out):
    x1 = nc.dram_tensor("x_after_conv", [BATCH, C, L], FP32, kind="Internal").ap()
    rows = nc.dram_tensor("qkv_rows", [BATCH, L, HEADS * PACK], U32, kind="Internal").ap()
    att = nc.dram_tensor("attention_rows", [BATCH, L, C], FP32, kind="Internal").ap()
    x_in = A["x"].rearrange("b c h w -> b c (h w)")
    y_out = out.rearrange("b c h w -> b c (h w)")
    with ExitStack() as ctx:
        w = _constants(nc, ctx)
        prepare(nc, w, A)
        conv_block(nc, w, x_in, x1, rows)
        causal_attention(nc, w, rows, att)
        project_and_ffn(nc, w, att, x1, y_out)


_INS = ['x', 'L0_conv_qkv_w', 'L0_conv_proj_w', 'L0_conv_proj_b', 'L0_conv_ln_g', 'L0_conv_ln_b',
        'L0_conv_fc1_w', 'L0_conv_fc1_b', 'L0_conv_fc2_w', 'L0_conv_fc2_b', 'L1_attn_Wk', 'L1_attn_Wq',
        'L1_attn_Wv', 'L1_attn_Wp', 'L1_attn_bp', 'L1_ffn_W1', 'L1_ffn_b1', 'L1_ffn_W2', 'L1_ffn_b2']


def kernel(**inputs):
    import numpy as _np
    import concourse.bacc as _bacc
    from concourse import mybir as _mybir
    from concourse.bass_utils import run_bass_kernel_spmd as _run

    nc = _bacc.Bacc("TRN2", target_bir_lowering=False, num_devices=1)
    arrays, args = {}, {}
    for name in _INS:
        a = _np.ascontiguousarray(inputs[name])
        arrays[f"in_{name}_dram"] = a
        args[name] = nc.dram_tensor(f"in_{name}_dram", a.shape, _mybir.dt.from_np(a.dtype), kind="ExternalInput").ap()
    out = nc.dram_tensor("out_0_dram", (BATCH, C, SIDE, SIDE), _mybir.dt.from_np(_np.dtype("float32")),
                         kind="ExternalOutput").ap()
    build(nc, args, out)
    r = _run(nc, [arrays], core_ids=[0])
    return r.results[0]["out_0_dram"]
```
